# Optimizing a Trainium2 kernel written in Bass

```python
import numpy as np
import jax
import jax.numpy as jnp

def _softmax(x, axis=-1):
    return jax.nn.softmax(x, axis=axis)

def _gelu(x):
    return jax.nn.gelu(x, approximate=True)

def _silu(x):
    return jax.nn.silu(x)

def _sigmoid(x):
    return jax.nn.sigmoid(x)

def _layernorm(x, axis=-1, eps=1e-05):
    m = jnp.mean(x, axis=axis, keepdims=True)
    v = jnp.var(x, axis=axis, keepdims=True)
    return (x - m) / jnp.sqrt(v + eps)

def _scatter_add(tgt, idx, src, axis=0):
    return tgt.at[idx].add(src)

def _segment_sum(src, seg, n):
    return jax.ops.segment_sum(src, seg, n)
kernel_name = 'mk_pixart_resid_d2_seqx_r4_68aa6a'

def setup_inputs(seed: int=0):
    np.random.seed(seed)
    _w = jnp.asarray

    def _rec_inputs():
        import jax
        import jax.numpy as jnp
        _rk = jax.random.key(seed)
        x = -1.528e-05 + 0.9999 * jax.random.normal(jax.random.fold_in(_rk, 1), (16, 256, 256), jnp.float32)
        _lenS = 256 - jax.random.randint(jax.random.fold_in(_rk, 7), (16,), 0, max(1, 256 // 4) + 1, jnp.int32)
        _lenS2 = 256 - jax.random.randint(jax.random.fold_in(_rk, 8), (16,), 0, max(1, 256 // 4) + 1, jnp.int32)
        cond_1024 = -0.0142567 + 1.00875 * jax.random.normal(jax.random.fold_in(_rk, 11), (16, 256), jnp.float32)
        _ctx_1024P = jax.random.normal(jax.random.fold_in(_rk, 12), (16, 16, 256), jnp.float32)
        _ctx_1024c = jax.random.dirichlet(jax.random.fold_in(_rk, 512), 0.3 * jnp.ones((16,), jnp.float32), (16, 256))
        _ctx_1024t = jnp.einsum('bsk,bkd->bsd', _ctx_1024c, _ctx_1024P)
        _ctx_1024t = _ctx_1024t * jax.lax.rsqrt(jnp.mean(jnp.square(_ctx_1024t)) + 1e-12) * 0.953939
        ctx_1024 = 0.000121155 + 1.00018 * (_ctx_1024t + 0.3 * jax.random.normal(jax.random.fold_in(_rk, 612), (16, 256, 256), jnp.float32))
        return (x, cond_1024, ctx_1024)
    x, cond_1024, ctx_1024 = _rec_inputs()

    def _L0_xcond_setup():
        import jax, jax.numpy as jnp
        import numpy as np
        B, S, D = (16, 512, 256)
        key = jax.random.key(seed)
        kq, kk, kv, kW, kU = jax.random.split(key, 5)
        scale = 1.0 / np.sqrt(D)
        return {'q': jax.random.normal(kq, (B, D), dtype=jnp.float32), 'k': jax.random.normal(kk, (B, S, D), dtype=jnp.float32), 'v': jax.random.normal(kv, (B, S, D), dtype=jnp.float32), 'W': jax.random.normal(kW, (D, D), dtype=jnp.float32) * scale, 'U': jax.random.normal(kU, (D, D), dtype=jnp.float32) * scale}
    _L0_xcond_all = _L0_xcond_setup()
    _L0_xcond_in = {k: v for k, v in _L0_xcond_all.items() if k in ('W', 'U')}
    del _L0_xcond_all

    def _L0_ffn_setup():
        import jax, jax.numpy as jnp
        import numpy as np
        D_MODEL = 256
        M = 64
        INNER = 16
        key = jax.random.key(seed)
        ks = jax.random.split(key, 9)

        def init(k, shape, fan_in):
            bound = 1.0 / np.sqrt(fan_in)
            return jax.random.uniform(k, shape, jnp.float32, -bound, bound)
        x = jax.random.normal(ks[0], (16, 1024, D_MODEL), dtype=jnp.float32)
        Win = init(ks[1], (D_MODEL, M), D_MODEL)
        bin_ = init(ks[2], (M,), D_MODEL)
        W1 = init(ks[3], (M, INNER), 1)
        b1 = init(ks[4], (M, INNER), 1)
        W2 = init(ks[5], (M, INNER), INNER)
        b2 = init(ks[6], (M,), INNER)
        Wout = init(ks[7], (M, D_MODEL), M)
        bout = init(ks[8], (D_MODEL,), M)
        return {'x': x, 'Win': Win, 'bin_': bin_, 'W1': W1, 'b1': b1, 'W2': W2, 'b2': b2, 'Wout': Wout, 'bout': bout}
    _L0_ffn_all = _L0_ffn_setup()
    _L0_ffn_in = {k: v for k, v in _L0_ffn_all.items() if k in ('Win', 'bin_', 'W1', 'b1', 'W2', 'b2', 'Wout', 'bout')}
    del _L0_ffn_all

    def _L1_xcond_setup():
        import jax, jax.numpy as jnp
        import numpy as np
        import math
        B, S, CTX, D, H, DH = (2, 512, 64, 256, 16, 64)
        INNER = H * DH
        DFF = 4 * D

        def layernorm(x, eps=1e-05):
            m = jnp.mean(x, axis=-1, keepdims=True)
            v = jnp.var(x, axis=-1, keepdims=True)
            return (x - m) * jax.lax.rsqrt(v + eps)

        def adaln(x, t, w, b):
            emb = t @ w + b
            scale, shift = jnp.split(emb, 2, axis=-1)
            return layernorm(x) * (1.0 + scale) + shift

        def mha(xq, ctx, wq, wk, wv, wo, bo):
            b, sq, _ = xq.shape
            sk = ctx.shape[1]
            q = (xq @ wq).reshape(b, sq, H, DH).transpose(0, 2, 1, 3)
            k = (ctx @ wk).reshape(b, sk, H, DH).transpose(0, 2, 1, 3)
            v = (ctx @ wv).reshape(b, sk, H, DH).transpose(0, 2, 1, 3)
            scores = jnp.einsum('bhqd,bhkd->bhqk', q, k) / math.sqrt(DH)
            attn = jax.nn.softmax(scores, axis=-1)
            out = jnp.einsum('bhqk,bhkd->bhqd', attn, v)
            out = out.transpose(0, 2, 1, 3).reshape(b, sq, INNER)
            return out @ wo + bo

        def glu_ff(x, w1, b1, w2, b2):
            u = x @ w1 + b1
            a, gate = jnp.split(u, 2, axis=-1)
            return a * jax.nn.gelu(gate, approximate=False) @ w2 + b2
        key = jax.random.key(seed)
        ks = jax.random.split(key, 24)
        s = 1.0 / math.sqrt(D)

        def n(k, shape, scale=1.0):
            return jax.random.normal(k, shape, dtype=jnp.float32) * scale
        return {'x': n(ks[0], (B, S, D)), 't': n(ks[1], (B, 1, D)), 'context': n(ks[2], (B, CTX, D)), 'attn1_wq': n(ks[3], (D, INNER), s), 'attn1_wk': n(ks[4], (D, INNER), s), 'attn1_wv': n(ks[5], (D, INNER), s), 'attn1_wo': n(ks[6], (INNER, D), s), 'attn1_bo': n(ks[7], (D,), 0.01), 'attn2_wq': n(ks[8], (D, INNER), s), 'attn2_wk': n(ks[9], (D, INNER), s), 'attn2_wv': n(ks[10], (D, INNER), s), 'attn2_wo': n(ks[11], (INNER, D), s), 'attn2_bo': n(ks[12], (D,), 0.01), 'ff_w1': n(ks[13], (D, 2 * DFF), s), 'ff_b1': n(ks[14], (2 * DFF,), 0.01), 'ff_w2': n(ks[15], (DFF, D), 1.0 / math.sqrt(DFF)), 'ff_b2': n(ks[16], (D,), 0.01), 'norm1_w': n(ks[17], (D, 2 * D), s), 'norm1_b': n(ks[18], (2 * D,), 0.01), 'norm2_w': n(ks[19], (D, 2 * D), s), 'norm2_b': n(ks[20], (2 * D,), 0.01), 'norm3_w': n(ks[21], (D, 2 * D), s), 'norm3_b': n(ks[22], (2 * D,), 0.01)}
    _L1_xcond_all = _L1_xcond_setup()
    _L1_xcond_in = {k: v for k, v in _L1_xcond_all.items() if k in ('attn1_wq', 'attn1_wk', 'attn1_wv', 'attn1_wo', 'attn1_bo', 'attn2_wq', 'attn2_wk', 'attn2_wv', 'attn2_wo', 'attn2_bo', 'ff_w1', 'ff_b1', 'ff_w2', 'ff_b2', 'norm1_w', 'norm1_b', 'norm2_w', 'norm2_b', 'norm3_w', 'norm3_b')}
    del _L1_xcond_all

    def _L1_ffn_setup():
        import jax, jax.numpy as jnp
        import numpy as np
        E = 8
        K = 2
        CF = 1.25
        key = jax.random.key(seed)
        kx, kr, kg, ku, kd = jax.random.split(key, 5)
        D, F = (256, 1024)
        x = jax.random.normal(kx, (4, 512, D), dtype=jnp.float32)
        router_w = 0.02 * jax.random.normal(kr, (E, D), dtype=jnp.float32)
        wg = jax.random.normal(kg, (E, D, F), dtype=jnp.float32) / np.sqrt(D)
        wu = jax.random.normal(ku, (E, D, F), dtype=jnp.float32) / np.sqrt(D)
        wd = jax.random.normal(kd, (E, F, D), dtype=jnp.float32) / np.sqrt(F)
        return {'x': x, 'router_w': router_w, 'wg': wg, 'wu': wu, 'wd': wd}
    _L1_ffn_all = _L1_ffn_setup()
    _L1_ffn_in = {k: v for k, v in _L1_ffn_all.items() if k in ('router_w', 'wg', 'wu', 'wd')}
    del _L1_ffn_all
    return {'x': x, 'cond_1024': cond_1024, 'ctx_1024': ctx_1024, 'L0_xcond_W': _L0_xcond_in['W'], 'L0_xcond_U': _L0_xcond_in['U'], 'L0_ffn_Win': _L0_ffn_in['Win'], 'L0_ffn_bin_': _L0_ffn_in['bin_'], 'L0_ffn_W1': _L0_ffn_in['W1'], 'L0_ffn_b1': _L0_ffn_in['b1'], 'L0_ffn_W2': _L0_ffn_in['W2'], 'L0_ffn_b2': _L0_ffn_in['b2'], 'L0_ffn_Wout': _L0_ffn_in['Wout'], 'L0_ffn_bout': _L0_ffn_in['bout'], 'L1_xcond_attn1_wq': _L1_xcond_in['attn1_wq'], 'L1_xcond_attn1_wk': _L1_xcond_in['attn1_wk'], 'L1_xcond_attn1_wv': _L1_xcond_in['attn1_wv'], 'L1_xcond_attn1_wo': _L1_xcond_in['attn1_wo'], 'L1_xcond_attn1_bo': _L1_xcond_in['attn1_bo'], 'L1_xcond_attn2_wq': _L1_xcond_in['attn2_wq'], 'L1_xcond_attn2_wk': _L1_xcond_in['attn2_wk'], 'L1_xcond_attn2_wv': _L1_xcond_in['attn2_wv'], 'L1_xcond_attn2_wo': _L1_xcond_in['attn2_wo'], 'L1_xcond_attn2_bo': _L1_xcond_in['attn2_bo'], 'L1_xcond_ff_w1': _L1_xcond_in['ff_w1'], 'L1_xcond_ff_b1': _L1_xcond_in['ff_b1'], 'L1_xcond_ff_w2': _L1_xcond_in['ff_w2'], 'L1_xcond_ff_b2': _L1_xcond_in['ff_b2'], 'L1_xcond_norm1_w': _L1_xcond_in['norm1_w'], 'L1_xcond_norm1_b': _L1_xcond_in['norm1_b'], 'L1_xcond_norm2_w': _L1_xcond_in['norm2_w'], 'L1_xcond_norm2_b': _L1_xcond_in['norm2_b'], 'L1_xcond_norm3_w': _L1_xcond_in['norm3_w'], 'L1_xcond_norm3_b': _L1_xcond_in['norm3_b'], 'L1_ffn_router_w': _L1_ffn_in['router_w'], 'L1_ffn_wg': _L1_ffn_in['wg'], 'L1_ffn_wu': _L1_ffn_in['wu'], 'L1_ffn_wd': _L1_ffn_in['wd']}

def reference(x, cond_1024, ctx_1024, L0_xcond_W, L0_xcond_U, L0_ffn_Win, L0_ffn_bin_, L0_ffn_W1, L0_ffn_b1, L0_ffn_W2, L0_ffn_b2, L0_ffn_Wout, L0_ffn_bout, L1_xcond_attn1_wq, L1_xcond_attn1_wk, L1_xcond_attn1_wv, L1_xcond_attn1_wo, L1_xcond_attn1_bo, L1_xcond_attn2_wq, L1_xcond_attn2_wk, L1_xcond_attn2_wv, L1_xcond_attn2_wo, L1_xcond_attn2_bo, L1_xcond_ff_w1, L1_xcond_ff_b1, L1_xcond_ff_w2, L1_xcond_ff_b2, L1_xcond_norm1_w, L1_xcond_norm1_b, L1_xcond_norm2_w, L1_xcond_norm2_b, L1_xcond_norm3_w, L1_xcond_norm3_b, L1_ffn_router_w, L1_ffn_wg, L1_ffn_wu, L1_ffn_wd):
    import jax
    import jax.numpy as jnp

    def _L0_xcond_ref(q, k, v, W, U):
        import jax, jax.numpy as jnp
        import numpy as np
        B, S, D = (16, 512, 256)
        fac1 = jnp.einsum('bsd,de->bse', k, W)
        fac2 = jnp.einsum('bd,de->be', q, U)[:, None, :]
        t = jnp.tanh(fac1 + fac2)
        s = jnp.einsum('bsd,bse->bde', v, t)
        attn = jax.nn.softmax(s, axis=0)
        out = jnp.einsum('bsd,bde->bse', v, attn)
        return out

    def _L0_ffn_ref(x, Win, bin_, W1, b1, W2, b2, Wout, bout):
        import jax, jax.numpy as jnp
        import numpy as np
        D_MODEL = 256
        M = 64
        INNER = 16
        s = jnp.einsum('btd,dm->btm', x, Win) + bin_
        h = jax.nn.relu(s[..., None] * W1 + b1)
        g = jnp.einsum('btmh,mh->btm', h, W2) + b2
        out = jnp.einsum('btm,md->btd', g, Wout) + bout
        return out

    def _L1_xcond_ref(x, t, context, attn1_wq, attn1_wk, attn1_wv, attn1_wo, attn1_bo, attn2_wq, attn2_wk, attn2_wv, attn2_wo, attn2_bo, ff_w1, ff_b1, ff_w2, ff_b2, norm1_w, norm1_b, norm2_w, norm2_b, norm3_w, norm3_b):
        import jax, jax.numpy as jnp
        import numpy as np
        import math
        B, S, CTX, D, H, DH = (2, 512, 64, 256, 16, 64)
        INNER = H * DH
        DFF = 4 * D

        def layernorm(x, eps=1e-05):
            m = jnp.mean(x, axis=-1, keepdims=True)
            v = jnp.var(x, axis=-1, keepdims=True)
            return (x - m) * jax.lax.rsqrt(v + eps)

        def adaln(x, t, w, b):
            emb = t @ w + b
            scale, shift = jnp.split(emb, 2, axis=-1)
            return layernorm(x) * (1.0 + scale) + shift

        def mha(xq, ctx, wq, wk, wv, wo, bo):
            b, sq, _ = xq.shape
            sk = ctx.shape[1]
            q = (xq @ wq).reshape(b, sq, H, DH).transpose(0, 2, 1, 3)
            k = (ctx @ wk).reshape(b, sk, H, DH).transpose(0, 2, 1, 3)
            v = (ctx @ wv).reshape(b, sk, H, DH).transpose(0, 2, 1, 3)
            scores = jnp.einsum('bhqd,bhkd->bhqk', q, k) / math.sqrt(DH)
            attn = jax.nn.softmax(scores, axis=-1)
            out = jnp.einsum('bhqk,bhkd->bhqd', attn, v)
            out = out.transpose(0, 2, 1, 3).reshape(b, sq, INNER)
            return out @ wo + bo

        def glu_ff(x, w1, b1, w2, b2):
            u = x @ w1 + b1
            a, gate = jnp.split(u, 2, axis=-1)
            return a * jax.nn.gelu(gate, approximate=False) @ w2 + b2
        h1 = adaln(x, t, norm1_w, norm1_b)
        x = mha(h1, h1, attn1_wq, attn1_wk, attn1_wv, attn1_wo, attn1_bo) + x
        h2 = adaln(x, t, norm2_w, norm2_b)
        x = mha(h2, context, attn2_wq, attn2_wk, attn2_wv, attn2_wo, attn2_bo) + x
        h3 = adaln(x, t, norm3_w, norm3_b)
        x = glu_ff(h3, ff_w1, ff_b1, ff_w2, ff_b2) + x
        return x

    def _L1_ffn_ref(x, router_w, wg, wu, wd):
        import jax, jax.numpy as jnp
        import numpy as np
        E = 8
        K = 2
        CF = 1.25
        B, L, D = x.shape
        xf = x.reshape(-1, D)
        N = xf.shape[0]
        capacity = max(1, int(CF * N / E))
        logits = xf @ router_w.T
        probs = jax.nn.softmax(logits, axis=-1)
        topw, topi = jax.lax.top_k(probs, K)
        topw = topw / (topw.sum(-1, keepdims=True) + 1e-06)
        fe = topi.reshape(-1)
        fw = topw.reshape(-1)
        ft = jnp.repeat(jnp.arange(N), K)
        order = jnp.lexsort((-fw, fe))
        se, sw, st = (fe[order], fw[order], ft[order])
        counts = jax.ops.segment_sum(jnp.ones_like(se), se, num_segments=E)
        starts = jnp.cumsum(counts) - counts
        rank = jnp.arange(N * K) - starts[se]
        keep = rank < capacity
        pos = jnp.where(keep, rank, capacity)
        disp = jnp.zeros((E, capacity + 1, D), x.dtype).at[se, pos].set(xf[st])
        disp = disp[:, :capacity]
        g = jnp.einsum('ecd,edf->ecf', disp, wg)
        u = jnp.einsum('ecd,edf->ecf', disp, wu)
        eo = jnp.einsum('ecf,efd->ecd', jax.nn.silu(g) * u, wd)
        gathered = eo[se, jnp.minimum(pos, capacity - 1)]
        contrib = gathered * (sw * keep.astype(x.dtype))[:, None]
        out = jnp.zeros_like(xf).at[st].add(contrib)
        return out.reshape(B, L, D)
    x = x + _L0_xcond_ref(cond_1024, _layernorm(x, axis=-1), ctx_1024, L0_xcond_W, L0_xcond_U)
    x = x + _L0_ffn_ref(_layernorm(x, axis=-1), L0_ffn_Win, L0_ffn_bin_, L0_ffn_W1, L0_ffn_b1, L0_ffn_W2, L0_ffn_b2, L0_ffn_Wout, L0_ffn_bout)
    x = x + _L1_xcond_ref(_layernorm(x, axis=-1), cond_1024[:, None, :], ctx_1024, L1_xcond_attn1_wq, L1_xcond_attn1_wk, L1_xcond_attn1_wv, L1_xcond_attn1_wo, L1_xcond_attn1_bo, L1_xcond_attn2_wq, L1_xcond_attn2_wk, L1_xcond_attn2_wv, L1_xcond_attn2_wo, L1_xcond_attn2_bo, L1_xcond_ff_w1, L1_xcond_ff_b1, L1_xcond_ff_w2, L1_xcond_ff_b2, L1_xcond_norm1_w, L1_xcond_norm1_b, L1_xcond_norm2_w, L1_xcond_norm2_b, L1_xcond_norm3_w, L1_xcond_norm3_b)
    x = x + _L1_ffn_ref(_layernorm(x, axis=-1), L1_ffn_router_w, L1_ffn_wg, L1_ffn_wu, L1_ffn_wd)
    return x

_drawn_inputs = setup_inputs


def setup_inputs(seed=0):
    import zlib

    import numpy as np

    out = dict(_drawn_inputs(seed))
    spreads = {}
    factors = {'L0_ffn_Win': 8.0,
     'L0_ffn_bin_': 8.0,
     'L0_ffn_W1': 8.0,
     'L0_ffn_b1': 7.146,
     'L0_ffn_W2': 5.375,
     'L0_ffn_b2': 8.0,
     'L0_ffn_Wout': 5.099,
     'L0_ffn_bout': 64.0,
     'L1_xcond_attn1_wq': 59.225,
     'L1_xcond_attn1_wk': 57.411,
     'L1_xcond_attn1_bo': 64.0,
     'L1_xcond_attn2_bo': 200.0,
     'L1_xcond_ff_b1': 64.0,
     'L1_xcond_ff_b2': 200.0,
     'L1_xcond_norm1_b': 64.0,
     'L1_xcond_norm2_b': 64.0,
     'L1_xcond_norm3_b': 64.0,
     'L1_ffn_router_w': 12.206,
     'L1_ffn_wg': 12.113,
     'L1_ffn_wu': 10.006,
     'L1_ffn_wd': 9.95,
     'L1_xcond_attn2_wq': 5.82,
     'L1_xcond_attn2_wk': 5.986,
     'L1_xcond_attn2_wv': 4.611,
     'L1_xcond_attn2_wo': 4.481,
     'L1_xcond_ff_w1': 3.323,
     'L1_xcond_ff_w2': 3.488,
     'L1_xcond_norm2_w': 6.641,
     'L1_xcond_norm3_w': 3.618}
    for name, (base, spread) in spreads.items():
        noise = np.random.default_rng([zlib.crc32(name.encode()), seed]).standard_normal(out[name].shape)
        drawn = base * np.exp(spread * noise) if base else spread * noise
        out[name] = jnp.asarray(drawn.astype(out[name].dtype))
    for name, factor in factors.items():
        out[name] = (out[name] * factor).astype(out[name].dtype)
    return out
```

```python
from contextlib import ExitStack, contextmanager

import concourse.bass as bass
from concourse import mybir

ALU = mybir.AluOpType
ACT = mybir.ActivationFunctionType
AX = mybir.AxisListType
F32 = mybir.dt.float32
U32 = mybir.dt.uint32

P = 128


class Tally:

    def __init__(self, engine_tallies, start=0):
        self.base, self.n = start, 0
        engine_tallies.append(self)

    def next(self, more=1):
        self.n += more
        return self.base + self.n

    def now(self):
        return self.base + self.n


@contextmanager
def repeat(eng, times, tallies, per):
    before = [(t, t.base, t.n) for t in tallies]
    with eng.Fori(0, times) as i:
        for t, base, n in before:
            k = per.get(t, 0)
            t.base, t.n = (base + n + i * k if k else base + n), 0
        yield i
        for t, base, n in before:
            assert t.n == per.get(t, 0), (t.n, per.get(t, 0), tallies.index(t))
    for t, base, n in before:
        t.base, t.n = base, n + times * per.get(t, 0)


def build(nc, x_in, cond_in, ctx_in, L0W, L0U, Win, bin_, W1, b1, W2, b2, Wout, bout,
          wq1, wk1, wv1, wo1, bo1, wq2, wk2, wv2, wo2, bo2, ffw1, ffb1, ffw2, ffb2,
          n1w, n1b, n2w, n2b, n3w, n3b, router_w, wg, wu, wd, out):
    B, S, D = x_in.shape
    DK = D // P
    BT = S // P
    GB = 2
    G = B // GB
    GT = GB * BT
    GS = GB * S
    NT = B * BT
    M = Win.shape[1]
    INNER = W1.shape[1]
    DI = wq1.shape[1]
    DH = 64
    HP = DI // P
    DFF = ffw2.shape[0]
    NF = DFF // P
    E = router_w.shape[0]
    NFE = wg.shape[2] // P
    CAP = int(1.25 * B * S / E)
    ET = CAP // P
    EH = CAP // 2
    SLOTS = E * CAP
    TRASH = SLOTS + CAP
    EPS = 1e-5
    assert GS == 512 and 2 * M == P and CAP % P == 0 and EH <= 512 and E % 2 == 0

    disp = nc.dram_tensor("dispatched", [TRASH + 2 * B * S, D], F32).ap()
    eo = nc.dram_tensor("expert_out", [SLOTS, D], F32).ap()
    fac2_dram = nc.dram_tensor("cond_rows", [B, D], F32).ap()

    with ExitStack() as ctx:
        def sb(name, shape, dt=F32):
            return ctx.enter_context(nc.sbuf_tensor(name, shape, dt))

        def sem(name):
            return ctx.enter_context(nc.semaphore(name))

        bank = [ctx.enter_context(nc.psum_tensor(f"bank{i}", [P, 512], F32)) for i in range(8)]

        x_res = sb("x_res", [P, NT * D])
        attn = sb("attn", [P, NT * D])
        wbig = sb("wbig", [P, 8192])
        wv_sb = [wbig[:, a * 2048:(a + 1) * 2048].rearrange("p (k n) -> p k n", k=DK) for a in range(2)]
        wo_sb = [wbig[:, 4096 + a * 2048:4096 + (a + 1) * 2048].rearrange("p (h n) -> p h n", h=HP) for a in range(2)]
        wff2 = sb("wff2", [P, NF, D])
        ew0 = sb("ew0", [P, 6144])
        z = sb("z", [P, GT, D])
        hat = sb("hat", [P, GT, D])
        ctx_nat = sb("ctx_nat", [P, GT, D])
        ctxT = sb("ctxT", [P, DK, GS])
        hT = sb("hT", [P, DK, GS])
        arena = sb("arena", [P, 7680])
        win_sb = sb("win_sb", [P, DK, M])
        wout_sb = sb("wout_sb", [P, D])
        ident = sb("ident", [P, P])
        ones = sb("ones", [P, P])
        upper = sb("upper", [P, P])
        bias_rows = sb("bias_rows", [1, 4, 512])
        condT = sb("condT", [P, DK, B])
        emb = sb("emb", [P, 3, 2 * DK, B])
        norm_b = sb("norm_b", [P, 3, 2 * DK])
        routerT = sb("routerT", [P, DK, E])
        small_w = sb("small_w", [P, 2, INNER])
        b1_sb = sb("b1_sb", [P, INNER])
        bin2 = sb("bin2", [P, 2])
        ffb1_sb = sb("ffb1_sb", [P, 2 * NF])
        stats = sb("stats", [P, GT, 6])
        both = sb("both", [P, GT, 2])
        mdiff = sb("mdiff", [P, GT])
        mdiff2 = sb("mdiff2", [P, GT])
        mean = sb("mean", [P, GT])
        veps = sb("veps", [P, GT])
        rstd = sb("rstd", [P, GT])
        minus_half = sb("minus_half", [P, GT])
        logits = sb("logits", [P, NT, E])
        nmx = sb("nmx", [P, 2, BT])
        rsum = sb("rsum", [P, 2, BT])
        rrec = sb("rrec", [P, 2, BT])
        slot1 = sb("slot1", [P, NT], U32)
        slot2 = sb("slot2", [P, NT], U32)
        gath1 = sb("gath1", [P, NT], U32)
        gath2 = sb("gath2", [P, NT], U32)
        wk12 = sb("wk12", [P, 2, NT])

        setup_small = sem("setup_small")
        setup_w = sem("setup_w")
        x_loaded = [sem(f"x_loaded{i}") for i in range(4)]
        zeroed = sem("zeroed")
        zero_tile = sem("zero_tile")
        const_set = sem("const_set")
        ident_set = sem("ident_set")
        tc_done = sem("tc_done")
        tc_copied = sem("tc_copied")
        emb_done = sem("emb_done")
        emb_ready = sem("emb_ready")
        f2_copied = sem("f2_copied")
        f2_stored = sem("f2_stored")
        f2_loaded = sem("f2_loaded")

        cond_nat = arena[0:B, 0:D]
        router_nat = arena[0:E, 256:256 + D]
        fac2_nat = arena[0:B, 512:512 + D]
        zero_rows = arena[:, 2560:2560 + 2048]
        normw = [ew0[:, n * 1024:(n + 1) * 1024].rearrange("p (k n) -> p k n", k=DK) for n in range(3)]
        l0u = ew0[:, 3072:3584].rearrange("p (k n) -> p k n", k=DK)
        l0w = ew0[:, 3584:4096].rearrange("p (k n) -> p k n", k=DK)
        fac2_row = wbig[0:1, 0:B * D]
        th = arena[:, 5120:5120 + GT * D].rearrange("p (t n) -> p t n", t=GT)
        x_tiles = x_in.rearrange("b s d -> (b s) d").rearrange("(t p) d -> p t d", p=P)
        ctx_tiles = ctx_in.rearrange("b s d -> (b s) d").rearrange("(t p) d -> p t d", p=P)
        out_tiles = out.rearrange("b s d -> (b s) d").rearrange("(t p) d -> p t d", p=P)
        x_res_t = x_res[:, :].rearrange("p (t d) -> p t d", d=D)
        SMALL = 2 + 2 * 5 + 3 + 8 + 1
        ZERO_ROWS = P * 2048 // D
        ZERO_DMAS = -(-TRASH // ZERO_ROWS)

        def kd(w):
            return w.rearrange("(k p) n -> p k n", p=P)

        ctx_loaded = sem("ctx_loaded")
        var_ready = sem("var_ready")
        rstd_ready = sem("rstd_ready")
        dve_own = sem("dve_own")
        hat_ready = sem("hat_ready")
        tr_done = sem("tr_done")
        hT_dve = sem("hT_dve")
        hT_act = sem("hT_act")
        fac_done = sem("fac_done")
        tanh_ready = sem("tanh_ready")
        s_done = sem("s_done")
        s_saved = sem("s_saved")

        LN_OWN = GT + 2

        def layer_norm(dve, src, dst, own, rs, own_sem, var_sem, rstd_sem, hat_sem):
            for t in range(GT):
                dve.bn_stats(stats[:, t, :], src(t)).then_inc(own_sem, 1)
            dve.wait_ge(own_sem, own.next(GT))
            dve.tensor_tensor(both[:, :, :], stats[:, :, 1:3], stats[:, :, 4:6], ALU.add)
            dve.tensor_tensor(mdiff[:, :], stats[:, :, 1], stats[:, :, 4], ALU.subtract).then_inc(own_sem, 1)
            dve.wait_ge(own_sem, own.next())
            dve.tensor_scalar(mean[:, :], both[:, :, 0], 0.5, None, ALU.mult)
            dve.tensor_scalar(veps[:, :], both[:, :, 1], 1.0 / D, EPS, ALU.mult, ALU.add)
            dve.scalar_tensor_tensor(mdiff2[:, :], mdiff[:, :], 0.25, mdiff[:, :], ALU.mult,
                                     ALU.mult).then_inc(own_sem, 1)
            dve.wait_ge(own_sem, own.next())
            dve.tensor_tensor(veps[:, :], veps[:, :], mdiff2[:, :], ALU.add).then_inc(var_sem, 1)
            dve.wait_ge(rstd_sem, rs.next())
            for t in range(GT):
                dve.tensor_scalar(dst(t), src(t), mean[:, t:t + 1], rstd[:, t:t + 1], ALU.subtract,
                                  ALU.mult).then_inc(hat_sem, 1)
        with nc.Block() as block:
            @block.sync
            def _(sp):
                for i, (dst, src) in enumerate((
                        (cond_nat, cond_in), (router_nat, router_w))):
                    sp.dma_start(dst, src).then_inc(setup_small, 16)
                for n, w in enumerate((n1w, n2w, n3w)):
                    sp.dma_start(normw[n], kd(w)).then_inc(setup_w, 16)
                sp.dma_start(l0u, kd(L0U)).then_inc(setup_w, 16)
                sp.dma_start(l0w, kd(L0W)).then_inc(setup_w, 16)
                for half in range(2):
                    rows = slice(half * M, (half + 1) * M)
                    sp.dma_start(small_w[rows, 0, :], W1).then_inc(setup_small, 16)
                    sp.dma_start(small_w[rows, 1, :], W2).then_inc(setup_small, 16)
                    sp.dma_start(b1_sb[rows, :], b1).then_inc(setup_small, 16)
                    sp.dma_start(bin2[rows, 0:1], bin_.rearrange("(m a) -> m a", a=1)).then_inc(setup_small, 16)
                    sp.dma_start(bin2[rows, 1:2], b2.rearrange("(m a) -> m a", a=1)).then_inc(setup_small, 16)
                with nc.allow_non_contiguous_dma("short bias columns"):
                    for n, v in enumerate((n1b, n2b, n3b)):
                        sp.dma_start(norm_b[:, n, :], v.rearrange("(c p) -> p c", p=P)).then_inc(setup_small, 16)
                    sp.dma_start(ffb1_sb[:, :], ffb1.rearrange("(c p) -> p c", p=P)).then_inc(setup_small, 16)
                for n, v in enumerate((bout, bo1, bo2, ffb2)):
                    for half in range(2):
                        sp.dma_start(bias_rows[0:1, n, half * D:(half + 1) * D],
                                     v.rearrange("(a n) -> a n", a=1)).then_inc(setup_small, 16)
                sp.dma_start(win_sb[:, :, :], kd(Win)).then_inc(setup_w, 16)
                for half in range(2):
                    sp.dma_start(wout_sb[half * M:(half + 1) * M, :], Wout).then_inc(setup_w, 16)
                sp.wait_ge(f2_copied, 1)
                sp.dma_start(fac2_dram, fac2_nat).then_inc(f2_stored, 16)
                sp.wait_ge(f2_stored, 16)
                sp.dma_start(fac2_row, fac2_dram.rearrange("(a b) n -> a (b n)", a=1)).then_inc(f2_loaded, 16)
                mine = []
                free = Tally(mine)
                with repeat(sp, G - 1, mine, {free: GB}) as g:
                    sp.wait_ge(s_done, free.next(GB))
                    sp.dma_start(ctx_nat[:, :, :], ctx_tiles[:, bass.ds(GT * g + GT, GT), :]).then_inc(ctx_loaded, 16)

            @block.gpsimd
            def _(pool):
                pool.memset(zero_rows, 0.0).then_inc(zero_tile, 1)
                pool.memset(ident[:, :], 0.0).then_inc(const_set, 1)
                pool.memset(ones[:, :], 1.0).then_inc(const_set, 1)
                pool.memset(minus_half[:, :], -0.5).then_inc(const_set, 1)
                pool.memset(upper[:, :], 1.0).then_inc(const_set, 1)
                pool.wait_ge(const_set, 4)
                pool.affine_select(out=ident[:, :], in_=ident[:, :], compare_op=ALU.not_equal, fill=1.0, base=0,
                                   pattern=[[-1, P]], channel_multiplier=1).then_inc(ident_set, 1)
                pool.affine_select(out=upper[:, :], in_=upper[:, :], compare_op=ALU.is_gt, fill=0.0, base=0,
                                   pattern=[[1, P]], channel_multiplier=-1).then_inc(ident_set, 1)
                mine = []
                v = Tally(mine)
                with repeat(pool, G, mine, {v: 1}) as g:
                    pool.wait_ge(var_ready, v.next())
                    pool.tensor_tensor(rstd[:, :], veps[:, :], minus_half[:, :], ALU.pow).then_inc(rstd_ready, 1)

            @block.scalar
            def _(act):
                act.dma_start(ctx_nat[:, :, :], ctx_tiles[:, 0:GT, :]).then_inc(ctx_loaded, 16)
                for i in range(4):
                    n = NT // 4
                    act.dma_start(x_res_t[:, i * n:(i + 1) * n, :], x_tiles[:, i * n:(i + 1) * n, :]).then_inc(x_loaded[i], 16)
                act.wait_ge(zero_tile, 1)
                rows = ZERO_ROWS
                for i in range(TRASH // rows):
                    act.dma_start(disp[i * rows:(i + 1) * rows, :].rearrange("(p r) d -> p (r d)", p=P),
                                  zero_rows).then_inc(zeroed, 16)
                rest = TRASH % rows
                if rest:
                    act.dma_start(disp[TRASH - rest:TRASH, :].rearrange("(p r) d -> p (r d)", p=P),
                                  zero_rows[:, 0:rest * D // P]).then_inc(zeroed, 16)
                mine = []
                tr, fac, sd, own = Tally(mine), Tally(mine), Tally(mine), Tally(mine)
                with repeat(act, G, mine, {tr: 2, fac: 2, sd: 2}) as g:
                    act.wait_ge(tr_done, tr.next(2))
                    act.activation(hT[:, 1, :], bank[1][:, :], ACT.Copy).then_inc(hT_act, 1)
                    for j in range(2):
                        act.wait_ge(fac_done, fac.next())
                        act.activation(th[:, 2 * j:2 * j + 2, :], bank[2 + j][:, :], ACT.Tanh).then_inc(tanh_ready, 1)
                    for b in range(GB):
                        act.wait_ge(s_done, sd.next())
                        act.activation(attn[:, bass.ds((GT * g + b * DK) * D, DK * D)], bank[4 + b][:, :],
                                       ACT.Copy).then_inc(s_saved, 1)

            @block.tensor
            def _(pe):
                pe.wait_ge(ident_set, 2)
                pe.wait_ge(setup_small, 16 * SMALL)
                for k in range(DK):
                    pe.transpose(bank[0][:, k * B:(k + 1) * B], cond_nat[:, k * P:(k + 1) * P], ident[0:B, 0:B])
                for k in range(DK):
                    last = pe.transpose(bank[0][:, 64 + k * E:64 + (k + 1) * E], router_nat[:, k * P:(k + 1) * P],
                                        ident[0:E, 0:E])
                last.then_inc(tc_done, 1)
                pe.wait_ge(tc_copied, 2)
                pe.wait_ge(setup_w, 16 * 8)
                for k in range(DK):
                    pe.matmul(bank[7][0:B, 0:D], condT[:, k, :], l0u[:, k, :], start=(k == 0), stop=(k == DK - 1))
                for n in range(3):
                    for c in range(2 * DK):
                        for k in range(DK):
                            o = (n * 2 * DK + c) * B
                            last = pe.matmul(bank[6][:, o:o + B], normw[n][:, k, c * P:(c + 1) * P], condT[:, k, :],
                                             start=(k == 0), stop=(k == DK - 1))
                last.then_inc(emb_done, 1)
                pe.wait_ge(f2_loaded, 16)
                mine = []
                hr, hd, ha, cl, tn, ss = (Tally(mine) for _ in range(6))
                with repeat(pe, G, mine, {hr: GT, hd: 1, ha: 1, cl: 16, tn: 2, ss: 0}) as g:
                    pe.wait_ge(hat_ready, hr.next(GT))
                    for k in range(DK):
                        for t in range(GT):
                            last = pe.transpose(bank[k][:, t * P:(t + 1) * P], hat[:, t, k * P:(k + 1) * P], ident[:, :])
                        last.then_inc(tr_done, 1)
                    pe.wait_ge(hT_dve, hd.next())
                    pe.wait_ge(hT_act, ha.next())
                    for t in range(GT):
                        o = bank[2 + t // 2][:, (t % 2) * D:(t % 2 + 1) * D]
                        for k in range(DK):
                            pe.matmul(o, hT[:, k, t * P:(t + 1) * P], l0w[:, k, :], start=(k == 0), stop=False)
                        last = pe.matmul(o, ones[0:1, :], fac2_row[0:1, bass.ds((GB * g + t // BT) * D, D)],
                                         start=False, stop=True)
                        if t % 2:
                            last.then_inc(fac_done, 1)
                    pe.wait_ge(ctx_loaded, cl.next(16))
                    for b in range(GB):
                        pe.wait_ge(tanh_ready, tn.next())
                        for k in range(DK):
                            for t in range(BT):
                                last = pe.matmul(bank[4 + b][:, k * D:(k + 1) * D],
                                                 ctx_nat[:, b * BT + t, k * P:(k + 1) * P], th[:, b * BT + t, :],
                                                 start=(t == 0), stop=(t == BT - 1))
                        last.then_inc(s_done, 1)


            @block.vector
            def _(dve):
                dve.wait_ge(tc_done, 1)
                dve.tensor_copy(condT[:, :, :], bank[0][:, 0:DK * B].rearrange("p (k b) -> p k b", k=DK)).then_inc(tc_copied, 1)
                dve.tensor_copy(routerT[:, :, :], bank[0][:, 64:64 + DK * E].rearrange("p (k e) -> p k e", k=DK)).then_inc(tc_copied, 1)
                dve.wait_ge(emb_done, 1)
                dve.tensor_copy(fac2_nat, bank[7][0:B, 0:D]).then_inc(f2_copied, 1)
                dve.wait_ge(setup_small, 16 * SMALL)
                for n in range(3):
                    for c in range(2 * DK):
                        o = (n * 2 * DK + c) * B
                        dve.tensor_scalar(emb[:, n, c, :], bank[6][:, o:o + B], norm_b[:, n, c:c + 1],
                                          1.0 if c < DK else 0.0, ALU.add, ALU.add).then_inc(emb_ready, 1)
                mine = []
                own, rs, tr = Tally(mine), Tally(mine), Tally(mine)
                for i in range(4):
                    dve.wait_ge(x_loaded[i], 16)
                with repeat(dve, G, mine, {own: LN_OWN, rs: 1, tr: 2}) as g:
                    layer_norm(dve, lambda t: x_res[:, bass.ds((GT * g + t) * D, D)], lambda t: hat[:, t, :], own, rs,
                               dve_own, var_ready, rstd_ready, hat_ready)
                    dve.wait_ge(tr_done, tr.next(2))
                    dve.tensor_copy(hT[:, 0, :], bank[0][:, :]).then_inc(hT_dve, 1)
        max_ready = sem("max_ready")
        shifted = sem("shifted")
        exps_ready = sem("exps_ready")
        attn_ready = sem("attn_ready")
        colmax = arena[:, 0:DK * D].rearrange("p (k e) -> p k e", k=DK)
        colsum = arena[:, 512:512 + DK * D].rearrange("p (k e) -> p k e", k=DK)
        colrec = arena[:, 1024:1024 + DK * D].rearrange("p (k e) -> p k e", k=DK)
        by_dtile = attn[:, :].rearrange("p (b k e) -> p k b e", b=B, k=DK)

        with nc.Block() as block:
            @block.vector
            def _(dve):
                for k in range(DK):
                    dve.tensor_reduce(colmax[:, k, :], by_dtile[:, k].rearrange("p b e -> p e b"), AX.X,
                                      ALU.max).then_inc(max_ready, 1)
                for k in range(DK):
                    dve.wait_ge(max_ready, k + 1)
                    dve.tensor_tensor(by_dtile[:, k], by_dtile[:, k],
                                      colmax[:, k, :].unsqueeze(1).to_broadcast([P, B, D]),
                                      ALU.subtract).then_inc(shifted, 1)
                for k in range(DK):
                    dve.wait_ge(exps_ready, k + 1)
                    dve.tensor_reduce(colsum[:, k, :], by_dtile[:, k].rearrange("p b e -> p e b"), AX.X,
                                      ALU.add).then_inc(dve_own, 1)
                    dve.wait_ge(dve_own, G * LN_OWN + 2 * k + 1)
                    dve.reciprocal(colrec[:, k, :], colsum[:, k, :]).then_inc(dve_own, 1)
                    dve.wait_ge(dve_own, G * LN_OWN + 2 * k + 2)
                    dve.tensor_tensor(by_dtile[:, k], by_dtile[:, k],
                                      colrec[:, k, :].unsqueeze(1).to_broadcast([P, B, D]),
                                      ALU.mult).then_inc(attn_ready, 1)

            @block.scalar
            def _(act):
                for k in range(DK):
                    act.wait_ge(shifted, k + 1)
                    act.activation(by_dtile[:, k], by_dtile[:, k], ACT.Exp).then_inc(exps_ready, 1)
                act.wait_ge(zeroed, 16 * ZERO_DMAS)

        stream_loaded = [sem("stream_loaded0"), sem("stream_loaded1")]
        stream_used = [sem("stream_used0"), sem("stream_used1")]
        resident = sem("resident")
        expert_loaded = [sem("expert_loaded0"), sem("expert_loaded1")]
        expert_w = [[w[:, 0:2048].rearrange("p (k n) -> p k n", k=DK), w[:, 2048:4096].rearrange("p (k n) -> p k n", k=DK),
                     w[:, 4096:6144].rearrange("p (f n) -> p f n", f=NFE)] for w in (ew0, wbig)]
        ctx_in_b = sem("ctx_in_b")
        hatB_ready = sem("hatB_ready")
        trB_done = sem("trB_done")
        hTB_dve = sem("hTB_dve")
        hTB_act = sem("hTB_act")
        varB_ready = sem("varB_ready")
        rstdB_ready = sem("rstdB_ready")
        ln_own = sem("ln_own")
        x1_done = sem("x1_done")
        low_done = sem("low_done")
        low_ready = sem("low_ready")
        relu_ready = sem("relu_ready")
        relu_used = sem("relu_used")
        mlp_ready = sem("mlp_ready")
        x2_done = sem("x2_done")
        proj_done = sem("proj_done")
        q_ready = sem("q_ready")
        k_ready = sem("k_ready")
        v_ready = sem("v_ready")
        scores_done = sem("scores_done")
        negmax_ready = sem("negmax_ready")
        exp_ready = sem("exp_ready")
        rrec_ready = sem("rrec_ready")
        probs_ready = sem("probs_ready")
        pT_done = sem("pT_done")
        pT_dve = sem("pT_dve")
        pT_act = sem("pT_act")
        o_done = sem("o_done")
        o_dve = sem("o_dve")
        o_act = sem("o_act")
        y_done = sem("y_done")
        glu_done = sem("glu_done")
        gelu_ready = sem("gelu_ready")
        gated_ready = sem("gated_ready")
        nrm_saved = sem("nrm_saved")
        logits_done = sem("logits_done")
        z_own = sem("z_own")

        def carve(sizes):
            at, views = 0, []
            for n in sizes:
                views.append(arena[:, at:at + n])
                at += n
            assert at <= 7680
            return views

        two = range(2)
        views = carve([GS] * 6 + [BT * S] * 4 + [GS] + [2 * DK * P] * 2)
        qT, kT, v_at = views[0:2], views[2:4], [v.rearrange("p (t n) -> p t n", t=GT) for v in views[4:6]]
        probs = [v.rearrange("p (t k) -> p t k", t=BT) for v in views[6:8]]
        pT = [v.rearrange("p (k q) -> p k q", k=BT) for v in views[8:10]]
        oT = views[10]
        stream = [v.rearrange("p (w k n) -> p w k n", w=2, k=DK) for v in views[11:13]]
        lowT = qT[0][:, 0:S]
        acc = [qT[1][:, 0:S], qT[1][:, S:2 * S]]
        mlpT = kT[0][:, 0:S]
        relus = [views[4 + j // 2][:, (j % 2) * S:(j % 2 + 1) * S] for j in range(4)]
        gelu = views[0:2]
        gated = views[2:4]
        wq_t, wk_t = [kd(w) for w in (wq1, wq2)], [kd(w) for w in (wk1, wk2)]
        w1_t = kd(ffw1)
        USES = 2 * HP + NF

        with nc.Block() as block:
            @block.sync
            def _(sp):
                mine = []
                used = [Tally(mine), Tally(mine)]
                for a in two:
                    sp.dma_start(wv_sb[a], kd((wv1, wv2)[a])).then_inc(resident, 16)
                    sp.dma_start(wo_sb[a], kd((wo1, wo2)[a])).then_inc(resident, 16)
                sp.dma_start(wff2[:, :, :], kd(ffw2)).then_inc(resident, 16)

                def two_tiles(i, first, second):
                    for p in two:
                        sp.wait_ge(stream_used[p], used[p].next())
                        for w, src in ((0, first), (1, second)):
                            sp.dma_start(stream[p][:, w], src(2 * i + p)).then_inc(stream_loaded[p], 16)

                for w, src in zip(expert_w[0], (wg, wu, wd)):
                    sp.dma_start(w, kd(src[0])).then_inc(expert_loaded[0], 16)
                per = {used[0]: USES // 2, used[1]: USES // 2}
                with repeat(sp, G, mine, per) as g:
                    sp.dma_start(ctx_nat[:, :, :], ctx_tiles[:, bass.ds(GT * g, GT), :]).then_inc(ctx_in_b, 16)
                    for a in two:
                        with repeat(sp, HP // 2, mine, {used[0]: 1, used[1]: 1}) as i:
                            two_tiles(i, lambda h: wq_t[a][:, :, bass.ds(h * P, P)],
                                      lambda h: wk_t[a][:, :, bass.ds(h * P, P)])
                    with repeat(sp, NF // 2, mine, {used[0]: 1, used[1]: 1}) as i:
                        two_tiles(i, lambda f: w1_t[:, :, bass.ds(f * P, P)],
                                  lambda f: w1_t[:, :, bass.ds(f * P + DFF, P)])

            @block.gpsimd
            def _(pool):
                mine = []
                var, hr = Tally(mine), Tally(mine)
                pool.sem_inc(nrm_saved, 1)
                with repeat(pool, G, mine, {var: 6, hr: 6 * GT}) as g:
                    for stage in range(6):
                        pool.wait_ge(varB_ready, var.next())
                        pool.tensor_tensor(rstd[:, :], veps[:, :], minus_half[:, :], ALU.pow).then_inc(rstdB_ready, 1)
                    pool.wait_ge(hatB_ready, hr.next(6 * GT))
                    pool.tensor_copy(attn[:, bass.ds(GT * D * g, GT * D)],
                                     hat[:, :, :].rearrange("p t d -> p (t d)")).then_inc(nrm_saved, 1)

            @block.scalar
            def _(act):
                mine = []
                tr, low, own, used, pd, nm, pt, od, glu = (Tally(mine) for _ in range(9))
                per = {tr: 12, low: 1, own: 1, used: INNER, pd: 6 * HP, nm: 8 * HP, pt: 8 * HP, od: 4 * HP, glu: NF}

                def transposed(g, norm=None):
                    act.wait_ge(trB_done, tr.next(2))
                    if norm is None:
                        act.activation(hT[:, 1, :], bank[1][:, :], ACT.Copy).then_inc(hTB_act, 1)
                        return
                    for b in range(GB):
                        part = slice(b * S, (b + 1) * S)
                        last = act.activation(hT[:, 1, part], bank[1][:, part], ACT.Identity,
                                              scale=emb[:, norm, 1, bass.ds(GB * g + b, 1)],
                                              bias=emb[:, norm, DK + 1, bass.ds(GB * g + b, 1)])
                    last.then_inc(hTB_act, 1)

                def save_q(p):
                    act.wait_ge(proj_done, pd.next())
                    act.activation(qT[p], bank[4][:, :], ACT.Copy, scale=float(DH) ** -0.5).then_inc(q_ready, 1)

                def save_v(p):
                    act.wait_ge(proj_done, pd.next(2))
                    act.activation(v_at[p], bank[4][:, :].rearrange("p (t n) -> p t n", t=GT), ACT.Copy).then_inc(v_ready, 1)

                def exps(u):
                    act.wait_ge(negmax_ready, nm.next())
                    for t in range(BT):
                        last = act.activation(probs[u][:, t, :], bank[u][:, t * S:(t + 1) * S], ACT.Exp,
                                              bias=nmx[:, u, t:t + 1], accum_out=rsum[:, u, t:t + 1])
                    last.then_inc(exp_ready, 1)

                def save_pT():
                    act.wait_ge(pT_done, pt.next(2))
                    act.activation(pT[1][:, :, :], bank[3][:, :].rearrange("p (k q) -> p k q", k=BT),
                                   ACT.Copy).then_inc(pT_act, 1)

                def heads(p, more):
                    exps(0)
                    exps(1)
                    if more:
                        save_q(1 - p)
                    save_pT()
                    exps(0)
                    exps(1)
                    if more:
                        save_v(1 - p)
                    save_pT()
                    act.wait_ge(o_done, od.next(2))
                    act.activation(oT[:, S:2 * S], bank[4][:, 0:S], ACT.Copy).then_inc(o_act, 1)

                with repeat(act, G, mine, per) as g:
                    act.wait_ge(trB_done, tr.next(2))
                    act.activation(ctxT[:, 1, :], bank[1][:, :], ACT.Copy).then_inc(hTB_act, 1)
                    transposed(g)
                    act.wait_ge(low_done, low.next())
                    act.activation(lowT, bank[4][:, 0:S], ACT.Identity, bias=bin2[:, 0:1]).then_inc(low_ready, 1)
                    act.wait_ge(low_ready, own.next())
                    for j in range(INNER):
                        if j >= 4:
                            act.wait_ge(relu_used, used.next())
                        act.activation(relus[j % 4], lowT, ACT.Relu, scale=small_w[:, 0, j:j + 1],
                                       bias=b1_sb[:, j:j + 1]).then_inc(relu_ready, 1)
                    used.next(4)
                    for a in two:
                        transposed(g, a)
                        save_q(0)
                        save_v(0)
                        per_two = {pd: 6, nm: 8, pt: 8, od: 4}
                        with repeat(act, HP // 2 - 1, mine, per_two) as i:
                            heads(0, True)
                            heads(1, True)
                        heads(0, True)
                        heads(1, False)
                    transposed(g, 2)

                    def gelus(f, p):
                        act.wait_ge(glu_done, glu.next())
                        act.activation(gelu[p], bank[2 * p + 1][:, :], ACT.Gelu,
                                       bias=ffb1_sb[:, bass.ds(f + NF, 1)]).then_inc(gelu_ready, 1)
                    with repeat(act, NF // 2, mine, {glu: 2}) as i:
                        gelus(2 * i, 0)
                        gelus(2 * i + 1, 1)
                    transposed(g)

            @block.tensor
            def _(pe):
                mine = []
                cl, hd, ha, hr, mr, qr, kr, vr, pr, pd, pa, od, oa, gd, sl0, sl1 = (Tally(mine) for _ in range(16))
                sl = (sl0, sl1)
                wo_flat = [w.rearrange("p h n -> p (h n)") for w in wo_sb]
                wff2_flat = wff2[:, :, :].rearrange("p f n -> p (f n)")
                per = {cl: 16, hd: 6, ha: 6, hr: 6 * GT, mr: 1, qr: 2 * HP, kr: 2 * HP, vr: 2 * HP,
                       pr: 8 * HP, pd: 4 * HP, pa: 4 * HP, od: 2 * HP, oa: 2 * HP, gd: NF,
                       sl0: 32 * USES // 2, sl1: 32 * USES // 2}
                pe.sem_inc(stream_used[0], 1)
                pe.sem_inc(stream_used[1], 1)
                pe.wait_ge(resident, 16 * 5)

                def transposes(src):
                    for k in range(DK):
                        for t in range(GT):
                            last = pe.transpose(bank[k][:, t * P:(t + 1) * P], src[:, t, k * P:(k + 1) * P], ident[:, :])
                        last.then_inc(trB_done, 1)

                def transposed():
                    pe.wait_ge(hatB_ready, hr.next(GT))
                    transposes(hat)
                    arrived()

                def arrived():
                    pe.wait_ge(hTB_dve, hd.next())
                    pe.wait_ge(hTB_act, ha.next())

                def bias_first(banks, n):
                    for y in banks:
                        pe.matmul(y[:, :], ones[0:1, :], bias_rows[0:1, n, :], start=True, stop=False,
                                  skip_group_check=True)

                def add_rows(banks, lhsT, rhs, last_of_group, ready=None):
                    for t in range(GT):
                        last = pe.matmul(banks[t // 2][:, (t % 2) * D:(t % 2 + 1) * D], lhsT(t), rhs,
                                         start=False, stop=last_of_group and t % 2 == 1, skip_group_check=True)
                        if last_of_group and t % 2:
                            last.then_inc(ready, 1)

                def proj_qk(p, srcq, srck):
                    pe.wait_ge(stream_loaded[p], sl[p].next(32))
                    for w, src, b in ((0, srcq, 4), (1, srck, 5)):
                        for k in range(DK):
                            last = pe.matmul(bank[b][:, :], stream[p][:, w, k, :], src[:, k, :],
                                             start=(k == 0), stop=(k == DK - 1))
                        if w == 0:
                            last.then_inc(proj_done, 1)
                    last.then_inc(proj_done, 1)

                def proj_v(a, srck, h):
                    pe.wait_ge(q_ready, qr.next())
                    for t in range(GT):
                        for k in range(DK):
                            last = pe.matmul(bank[4][:, t * P:(t + 1) * P], srck[:, k, t * P:(t + 1) * P],
                                             wv_sb[a][:, k, bass.ds(h * P, P)], start=(k == 0), stop=(k == DK - 1))
                    last.then_inc(proj_done, 1)

                def scores(p, u):
                    b, h = u // 2, u % 2
                    rows = slice(h * DH, (h + 1) * DH)
                    for t in range(BT):
                        last = pe.matmul(bank[h][:, t * S:(t + 1) * S], qT[p][rows, b * S + t * P:b * S + (t + 1) * P],
                                         kT[p][rows, b * S:(b + 1) * S], start=True, stop=True)
                    last.then_inc(scores_done, 1)

                def turn(u):
                    pe.wait_ge(probs_ready, pr.next())
                    for k in range(BT):
                        for t in range(BT):
                            last = pe.transpose(bank[2 + u][:, k * S + t * P:k * S + (t + 1) * P],
                                                probs[u][:, t, k * P:(k + 1) * P], ident[:, :])
                    last.then_inc(pT_done, 1)

                def weigh(p, u):
                    b, h = u // 2, u % 2
                    if h:
                        pe.wait_ge(pT_act, pa.next())
                    else:
                        pe.wait_ge(pT_dve, pd.next())
                    for k in range(BT):
                        last = pe.matmul(bank[5 - b][h * DH:(h + 1) * DH, 0:S],
                                         v_at[p][:, b * BT + k, h * DH:(h + 1) * DH], pT[h][:, k, :],
                                         start=(k == 0), stop=(k == BT - 1))
                    if h:
                        last.then_inc(o_done, 1)

                def heads(a, p, h, more, srcq, srck):
                    scores(p, 0)
                    scores(p, 1)
                    if more:
                        proj_qk(1 - p, srcq, srck)
                    turn(0)
                    turn(1)
                    scores(p, 2)
                    scores(p, 3)
                    if more:
                        pe.wait_ge(k_ready, kr.next())
                        pe.sem_inc(stream_used[1 - p], 1)
                    weigh(p, 0)
                    weigh(p, 1)
                    if more:
                        proj_v(a, srck, h + 1)
                    turn(0)
                    turn(1)
                    if more:
                        pe.wait_ge(v_ready, vr.next())
                    weigh(p, 2)
                    weigh(p, 3)
                    pe.wait_ge(o_dve, od.next())
                    pe.wait_ge(o_act, oa.next())
                    add_rows(bank[6:8], lambda t: oT[:, t * P:(t + 1) * P], wo_flat[a][:, bass.ds(h * D, D)],
                             not more, y_done)

                with repeat(pe, G, mine, per) as g:
                    pe.wait_ge(ctx_in_b, cl.next(16))
                    transposes(ctx_nat)
                    arrived()
                    for t in range(GT):
                        for k in range(DK):
                            last = pe.matmul(bank[2 + t // 2][:, (t % 2) * D:(t % 2 + 1) * D],
                                             ctxT[:, k, t * P:(t + 1) * P],
                                             attn[:, bass.ds(((GB * g + t // BT) * DK + k) * D, D)],
                                             start=(k == 0), stop=(k == DK - 1))
                        if t % 2:
                            last.then_inc(x1_done, 1)
                    transposed()
                    for b in range(GB):
                        for k in range(DK):
                            last = pe.matmul(bank[4][b * M:(b + 1) * M, 0:S], win_sb[:, k, :],
                                             hT[:, k, b * S:(b + 1) * S], start=(k == 0), stop=(k == DK - 1))
                    last.then_inc(low_done, 1)
                    bias_first(bank[2:4], 0)
                    pe.wait_ge(mlp_ready, mr.next())
                    for t in range(GT):
                        b = t // BT
                        last = pe.matmul(bank[2 + t // 2][:, (t % 2) * D:(t % 2 + 1) * D],
                                         mlpT[b * M:(b + 1) * M, (t % BT) * P:(t % BT + 1) * P],
                                         wout_sb[b * M:(b + 1) * M, :], start=False, stop=t % 2 == 1,
                                         skip_group_check=True)
                        if t % 2:
                            last.then_inc(x2_done, 1)
                    hr.next(GT)
                    for a in two:
                        transposed()
                        srck = hT if a == 0 else ctxT
                        proj_qk(0, hT, srck)
                        pe.wait_ge(k_ready, kr.next())
                        pe.sem_inc(stream_used[0], 1)
                        proj_v(a, srck, 0)
                        pe.wait_ge(v_ready, vr.next())
                        bias_first(bank[6:8], 1 + a)
                        per_two = {qr: 2, kr: 2, vr: 2, pr: 8, pd: 4, pa: 4, od: 2, oa: 2, sl0: 32, sl1: 32}
                        with repeat(pe, HP // 2 - 1, mine, per_two) as i:
                            heads(a, 0, 2 * i, True, hT, srck)
                            heads(a, 1, 2 * i + 1, True, hT, srck)
                        heads(a, 0, HP - 2, True, hT, srck)
                        heads(a, 1, HP - 1, False, hT, srck)
                    transposed()
                    bias_first(bank[6:8], 3)

                    def up(p):
                        pe.wait_ge(stream_loaded[p], sl[p].next(32))
                        for w in two:
                            for k in range(DK):
                                last = pe.matmul(bank[2 * p + w][:, :], stream[p][:, w, k, :], hT[:, k, :],
                                                 start=(k == 0), stop=(k == DK - 1))
                        last.then_inc(glu_done, 1)

                    def down(p, f, last_of_group):
                        pe.wait_ge(gated_ready, gd.next())
                        pe.sem_inc(stream_used[p], 1)
                        add_rows(bank[6:8], lambda t: gated[p][:, t * P:(t + 1) * P],
                                 wff2_flat[:, bass.ds(f * D, D)], last_of_group, y_done)
                    up(0)
                    with repeat(pe, NF // 2 - 1, mine, {gd: 2, sl0: 32, sl1: 32}) as i:
                        up(1)
                        down(0, 2 * i, False)
                        up(0)
                        down(1, 2 * i + 1, False)
                    up(1)
                    down(0, NF - 2, False)
                    down(1, NF - 1, True)
                    transposed()
                    for t in range(GT):
                        for k in range(DK):
                            last = pe.matmul(bank[4][:, t * E:(t + 1) * E], hT[:, k, t * P:(t + 1) * P], routerT[:, k, :],
                                             start=(k == 0), stop=(k == DK - 1))
                    last.then_inc(logits_done, 1)

            @block.vector
            def _(dve):
                mine = []
                own, rs, tr, x1, x2, rl, zo, pd, sc, er, pt, od, yd, gl, ge, lg, ns, rx, rr, hz = (Tally(mine) for _ in range(20))
                per = {own: 6 * LN_OWN, rs: 6, tr: 12, x1: 2, x2: 2, rl: INNER, zo: 13, pd: 6 * HP, sc: 8 * HP,
                       er: 8 * HP, rr: 8 * HP, hz: 6 * GT, pt: 8 * HP, od: 4 * HP, yd: 6, gl: NF, ge: NF, lg: 1, ns: 1, rx: INNER}

                def ln(src, dst):
                    layer_norm(dve, src, dst, own, rs, ln_own, varB_ready, rstdB_ready, hatB_ready)
                    hz.next(GT)

                def transposed(g, norm=None, into=None):
                    dve.wait_ge(trB_done, tr.next())
                    tr.next()
                    if norm is None:
                        dve.tensor_copy((hT if into is None else into)[:, 0, :], bank[0][:, :]).then_inc(hTB_dve, 1)
                        return
                    for b in range(GB):
                        part = slice(b * S, (b + 1) * S)
                        last = dve.tensor_scalar(hT[:, 0, part], bank[0][:, part],
                                                 emb[:, norm, 0, bass.ds(GB * g + b, 1)],
                                                 emb[:, norm, DK, bass.ds(GB * g + b, 1)], ALU.mult, ALU.add)
                    last.then_inc(hTB_dve, 1)

                def save_k(p):
                    dve.wait_ge(proj_done, pd.next(2))
                    dve.tensor_copy(kT[p], bank[5][:, :]).then_inc(k_ready, 1)
                    pd.next()

                def negmax(u):
                    dve.wait_ge(scores_done, sc.next())
                    dve.tensor_reduce(nmx[:, u, :], bank[u][:, :].rearrange("p (t k) -> p t k", t=BT), AX.X, ALU.max,
                                      negate=True).then_inc(negmax_ready, 1)

                def normalise(u):
                    dve.wait_ge(exp_ready, er.next())
                    dve.reciprocal(rrec[:, u, :], rsum[:, u, :]).then_inc(rrec_ready, 1)
                    dve.wait_ge(rrec_ready, rr.next())
                    for t in range(BT):
                        last = dve.tensor_scalar(probs[u][:, t, :], probs[u][:, t, :], rrec[:, u, t:t + 1], None, ALU.mult)
                    last.then_inc(probs_ready, 1)

                def save_pT():
                    dve.wait_ge(pT_done, pt.next())
                    dve.tensor_copy(pT[0][:, :, :], bank[2][:, :].rearrange("p (k q) -> p k q", k=BT)).then_inc(pT_dve, 1)
                    pt.next()

                def heads(p, more):
                    negmax(0)
                    negmax(1)
                    normalise(0)
                    normalise(1)
                    if more:
                        save_k(1 - p)
                    save_pT()
                    negmax(0)
                    negmax(1)
                    normalise(0)
                    dve.wait_ge(o_done, od.next())
                    dve.tensor_copy(oT[:, 0:S], bank[5][:, 0:S]).then_inc(o_dve, 1)
                    od.next()
                    normalise(1)
                    save_pT()

                def add_into(dst, src, done, tally):
                    for j in range(2):
                        dve.wait_ge(done, tally.next())
                        dve.tensor_tensor(dst(j), dst(j), src[j][:, :], ALU.add).then_inc(z_own, 1)
                    dve.wait_ge(z_own, zo.next(2))
                    dve.memset(mdiff2[:, :], 0.0)

                with repeat(dve, G, mine, per) as g:
                    def xt(t, n=1):
                        return x_res[:, bass.ds((GT * g + t) * D, n * D)]

                    def zt(t, n=1):
                        return z[:, :, :].rearrange("p t d -> p (t d)")[:, t * D:(t + n) * D]

                    transposed(g, into=ctxT)
                    dve.wait_ge(nrm_saved, ns.next())
                    add_into(lambda j: xt(2 * j, 2), bank[2:4], x1_done, x1)
                    ln(xt, lambda t: hat[:, t, :])
                    transposed(g)
                    for j in range(INNER):
                        dve.wait_ge(relu_ready, rl.next())
                        if j == 0:
                            last = dve.tensor_scalar(acc[0], relus[0], small_w[:, 1, 0:1], bin2[:, 1:2], ALU.mult, ALU.add)
                        elif j == 1:
                            last = dve.tensor_scalar(acc[1], relus[1], small_w[:, 1, 1:2], None, ALU.mult)
                        else:
                            dve.wait_ge(relu_used, rx.next())
                            last = dve.scalar_tensor_tensor(acc[j % 2], relus[j % 4], small_w[:, 1, j:j + 1], acc[j % 2],
                                                            ALU.mult, ALU.add)
                        last.then_inc(relu_used, 1)
                    rx.next(2)
                    dve.wait_ge(relu_used, rx.now())
                    dve.tensor_tensor(mlpT, acc[0], acc[1], ALU.add).then_inc(mlp_ready, 1)
                    add_into(lambda j: xt(2 * j, 2), bank[2:4], x2_done, x2)
                    ln(xt, lambda t: z[:, t, :])
                    dve.wait_ge(hatB_ready, hz.now())
                    for a in two:
                        ln(lambda t: z[:, t, :], lambda t: hat[:, t, :])
                        transposed(g, a)
                        save_k(0)
                        per_two = {pd: 6, sc: 8, er: 8, rr: 8, pt: 8, od: 4}
                        with repeat(dve, HP // 2 - 1, mine, per_two) as i:
                            heads(0, True)
                            heads(1, True)
                        heads(0, True)
                        heads(1, False)
                        add_into(lambda j: zt(2 * j, 2), bank[6:8], y_done, yd)
                    ln(lambda t: z[:, t, :], lambda t: hat[:, t, :])
                    transposed(g, 2)
                    with repeat(dve, NF // 2, mine, {gl: 2, ge: 2}) as i:
                        for p in two:
                            dve.wait_ge(glu_done, gl.next())
                            dve.wait_ge(gelu_ready, ge.next())
                            dve.scalar_tensor_tensor(gated[p], bank[2 * p][:, :], ffb1_sb[:, bass.ds(2 * i + p, 1)], gelu[p],
                                                     ALU.add, ALU.mult).then_inc(gated_ready, 1)
                    add_into(lambda j: zt(2 * j, 2), bank[6:8], y_done, yd)
                    for j in range(2):
                        dve.tensor_tensor(xt(2 * j, 2), xt(2 * j, 2), zt(2 * j, 2), ALU.add).then_inc(z_own, 1)
                    dve.wait_ge(z_own, zo.next(2))
                    dve.memset(mdiff2[:, :], 0.0)
                    ln(xt, lambda t: hat[:, t, :])
                    transposed(g)
                    dve.wait_ge(logits_done, lg.next())
                    dve.tensor_copy(logits[:, bass.ds(GT * g, GT), :],
                                    bank[4][:, 0:GT * E].rearrange("p (t e) -> p t e", t=GT)).then_inc(z_own, 1)
                    zo.next()


        r_own = sem("r_own")
        shifted_lg = sem("shifted_lg")
        exp_lg = sem("exp_lg")
        masks_ready = sem("masks_ready")
        counted = sem("counted")
        part_ready = sem("part_ready")
        iota_set = sem("iota_set")
        pre_done = sem("pre_done")
        slots_ready = sem("slots_ready")
        scattered = sem("scattered")

        (prob, eqm, cand, oh1, oh2, wm, memb, ge, keep, tot, run_a, run_b, rank, iota_e, slot_e, tmp, tmp2, iota100,
         ex, above) = [c.rearrange("p (t e) -> p t e", t=NT) for c in carve([NT * E] * 20)]
        expert_i = sb("expert_i", [P, NT, E], mybir.dt.int32)
        token_i = sb("token_i", [P, NT], mybir.dt.int32)
        token_f = sb("token_f", [P, NT])
        top_p = sb("top_p", [P, 2, NT])
        top_w = sb("top_w", [P, 2, NT])
        by_token = sb("by_token", [P, 4, NT])
        thr, step, sel, trial, part, room, flag = (sb(n, [P, E]) for n in
                                                   ("thr", "step", "sel", "trial", "part", "room", "flag"))

        def over_e(v):
            return v.unsqueeze(2).to_broadcast([P, NT, E])

        def over_t(v):
            return v.unsqueeze(1).to_broadcast([P, NT, E])

        HALVINGS = 23
        DOUBLINGS = (64, 32, 16, 8, 4, 2, 1)
        TINY = 2.0 ** -126
        COUNTS = 1 + len(DOUBLINGS) + HALVINGS + 1

        with nc.Block() as block:
            @block.gpsimd
            def _(pool):
                pool.iota(expert_i[:, :, :], [[0, NT], [1, E]], base=0, channel_multiplier=0).then_inc(iota_set, 1)
                pool.iota(token_i[:, :], [[P, NT]], base=0, channel_multiplier=1).then_inc(iota_set, 1)
                pool.wait_ge(slots_ready, 4)
                for t in range(NT):
                    for slot in (slot1, slot2):
                        pool.indirect_dma_start(disp[:, :], bass.IndirectOffsetOnAxis(ap=slot[:, t:t + 1], axis=0),
                                                attn[:, t * D:(t + 1) * D], None).then_inc(scattered, 16)
                pool.wait_ge(scattered, 16 * 2 * NT)

            @block.sync
            def _(sp):
                for w, src in zip(expert_w[1], (wg, wu, wd)):
                    sp.dma_start(w, kd(src[1])).then_inc(expert_loaded[1], 16)

            @block.scalar
            def _(act):
                act.wait_ge(shifted_lg, 1)
                act.activation(ex, tmp, ACT.Exp).then_inc(exp_lg, 1)

            @block.tensor
            def _(pe):
                for n in range(COUNTS):
                    pe.wait_ge(part_ready, n + 1)
                    pe.matmul(bank[n % 2][:, 0:E], ones[:, :], part[:, :], start=True, stop=True).then_inc(counted, 1)
                for n, mask in enumerate((eqm, keep)):
                    pe.wait_ge(masks_ready, n + 1)
                    src = mask.rearrange("p t e -> p (t e)")
                    pe.matmul(bank[2][:, 0:NT * E], upper[:, :], src, start=True, stop=True)
                    pe.matmul(bank[3][:, 0:NT * E], ones[:, :], src, start=True, stop=True).then_inc(pre_done, 1)

            @block.vector
            def _(dve):
                steps = [0]

                def link(ins):
                    ins.then_inc(r_own, 1)
                    steps[0] += 1
                    dve.wait_ge(r_own, steps[0])

                dve.wait_ge(iota_set, 2)
                dve.tensor_copy(iota_e, expert_i[:, :, :])
                link(dve.tensor_copy(token_f[:, :], token_i[:, :]))
                dve.tensor_scalar(iota100, iota_e, 100.0, None, ALU.add)
                lmax, lsum, lrec, first = (by_token[:, i, :] for i in range(4))
                link(dve.tensor_reduce(lmax, logits[:, :, :], AX.X, ALU.max))
                dve.tensor_tensor(tmp, logits[:, :, :], over_e(lmax), ALU.subtract).then_inc(shifted_lg, 1)
                dve.wait_ge(exp_lg, 1)
                link(dve.tensor_reduce(lsum, ex, AX.X, ALU.add))
                link(dve.reciprocal(lrec, lsum))
                link(dve.tensor_tensor(prob, ex, over_e(lrec), ALU.mult))
                for c, (p, onehot) in enumerate(((prob, oh1), (tmp2, oh2))):
                    if c:
                        link(dve.scalar_tensor_tensor(tmp2, oh1, -2.0, prob, ALU.mult, ALU.add))
                    link(dve.tensor_reduce(top_p[:, c, :], p, AX.X, ALU.max))
                    link(dve.tensor_tensor(eqm, p, over_e(top_p[:, c, :]), ALU.is_equal))
                    link(dve.scalar_tensor_tensor(cand, eqm, -100.0, iota100, ALU.mult, ALU.add))
                    link(dve.tensor_reduce(first, cand, AX.X, ALU.min))
                    link(dve.tensor_tensor(onehot, iota_e, over_e(first), ALU.is_equal))
                link(dve.tensor_tensor(lsum, top_p[:, 0, :], top_p[:, 1, :], ALU.add))
                link(dve.tensor_scalar(lsum, lsum, 1e-6, None, ALU.add))
                link(dve.reciprocal(lrec, lsum))
                for c in range(2):
                    link(dve.tensor_tensor(top_w[:, c, :], top_p[:, c, :], lrec, ALU.mult))
                dve.tensor_tensor(memb, oh1, oh2, ALU.add)
                dve.tensor_tensor(tmp, oh1, over_e(top_w[:, 0, :]), ALU.mult)
                link(dve.tensor_tensor(tmp2, oh2, over_e(top_w[:, 1, :]), ALU.mult))
                link(dve.tensor_tensor(tmp, tmp, tmp2, ALU.add))
                link(dve.scalar_tensor_tensor(tmp, tmp, TINY, tmp, ALU.is_ge, ALU.mult))
                link(dve.scalar_tensor_tensor(wm, memb, -1.0, tmp, ALU.add, ALU.add))

                counts = [0]

                def count(mask_of):
                    link(mask_of(ge))
                    dve.tensor_reduce(part[:, :], ge.rearrange("p t e -> p e t"), AX.X, ALU.add).then_inc(part_ready, 1)
                    counts[0] += 1
                    dve.wait_ge(counted, counts[0])
                    return bank[(counts[0] - 1) % 2][:, 0:E]

                def enough(dst):
                    total = count(lambda o: dve.tensor_tensor(o, wm, over_t(trial[:, :]), ALU.is_ge))
                    link(dve.tensor_scalar(dst[:, :], total, float(CAP), None, ALU.is_ge))

                dve.memset(thr[:, :], TINY)
                link(dve.memset(trial[:, :], TINY))
                enough(flag)
                for k in DOUBLINGS:
                    link(dve.tensor_scalar(trial[:, :], thr[:, :], 2.0 ** k, None, ALU.mult))
                    enough(sel)
                    link(dve.tensor_scalar(sel[:, :], sel[:, :], 2.0 ** k - 1.0, 1.0, ALU.mult, ALU.add))
                    link(dve.tensor_tensor(thr[:, :], thr[:, :], sel[:, :], ALU.mult))
                link(dve.tensor_scalar(step[:, :], thr[:, :], 0.5, None, ALU.mult))
                for k in range(HALVINGS):
                    link(dve.tensor_tensor(trial[:, :], thr[:, :], step[:, :], ALU.add))
                    enough(sel)
                    link(dve.tensor_tensor(sel[:, :], sel[:, :], step[:, :], ALU.mult))
                    dve.tensor_scalar(step[:, :], step[:, :], 0.5, None, ALU.mult)
                    link(dve.tensor_tensor(thr[:, :], thr[:, :], sel[:, :], ALU.add))
                link(dve.tensor_tensor(thr[:, :], thr[:, :], flag[:, :], ALU.mult))
                total = count(lambda o: dve.tensor_tensor(o, wm, over_t(thr[:, :]), ALU.is_gt))
                dve.tensor_scalar(room[:, :], total, -1.0, float(CAP), ALU.mult, ALU.add)

                def before(n):
                    flat = lambda b: bank[b][:, 0:NT * E].rearrange("p (t e) -> p t e", t=NT)
                    dve.wait_ge(pre_done, n + 1)
                    dve.tensor_copy(tot, flat(3))
                    link(dve.tensor_copy(run_a, flat(3)))
                    a, b = run_a, run_b
                    shift = 1
                    while shift < NT:
                        dve.tensor_copy(b[:, 0:shift, :], a[:, 0:shift, :])
                        link(dve.tensor_tensor(b[:, shift:NT, :], a[:, shift:NT, :], a[:, 0:NT - shift, :], ALU.add))
                        a, b = b, a
                        shift *= 2
                    link(dve.tensor_tensor(a, a, tot, ALU.subtract))
                    link(dve.tensor_tensor(rank, a, flat(2), ALU.add))

                dve.tensor_tensor(eqm, wm, over_t(thr[:, :]), ALU.is_equal).then_inc(masks_ready, 1)
                before(0)
                link(dve.tensor_tensor(tmp, rank, over_t(room[:, :]), ALU.is_lt))
                link(dve.tensor_tensor(tmp, tmp, eqm, ALU.mult))
                dve.tensor_tensor(keep, ge, tmp, ALU.add).then_inc(masks_ready, 1)
                before(1)
                link(dve.scalar_tensor_tensor(slot_e, iota_e, float(CAP), rank, ALU.mult, ALU.add))
                link(dve.tensor_tensor(slot_e, slot_e, keep, ALU.mult))
                for c, (onehot, slot, gath) in enumerate(((oh1, slot1, gath1), (oh2, slot2, gath2))):
                    place, kept, lost, _ = (by_token[:, i, :] for i in range(4))
                    dve.tensor_tensor(tmp, onehot, slot_e, ALU.mult)
                    link(dve.tensor_tensor(tmp2, onehot, keep, ALU.mult))
                    dve.tensor_reduce(place, tmp, AX.X, ALU.add)
                    link(dve.tensor_reduce(kept, tmp2, AX.X, ALU.add))
                    dve.tensor_tensor(wk12[:, c, :], top_w[:, c, :], kept, ALU.mult)
                    dve.tensor_scalar(lost, kept, -1.0, 1.0, ALU.mult, ALU.add)
                    link(dve.tensor_scalar(tmp[:, :, 0], token_f[:, :], float(TRASH + c * B * S), None, ALU.add))
                    link(dve.tensor_tensor(lost, lost, tmp[:, :, 0], ALU.mult))
                    link(dve.tensor_tensor(lost, lost, place, ALU.add))
                    dve.tensor_copy(slot[:, :], lost).then_inc(slots_ready, 1)
                    dve.tensor_copy(gath[:, :], place).then_inc(slots_ready, 1)
                    dve.wait_ge(slots_ready, 2 * c + 2)


        xg_loaded = sem("xg_loaded")
        turned = sem("turned")
        xT_dve = sem("xT_dve")
        xT_act = sem("xT_act")
        up_done = sem("up_done")
        silu_ready = sem("silu_ready")
        act_ready = sem("act_ready")
        down_done = sem("down_done")
        eo_saved = sem("eo_saved")
        eo_stored = sem("eo_stored")
        tiles_free = sem("tiles_free")

        xg_v, xT, actE = carve([ET * D, DK * CAP, NFE * CAP])
        xg = xg_v.rearrange("p (t d) -> p t d", t=ET)
        silu = [z[:, :, :].rearrange("p t d -> p (t d)")[:, u * EH:(u + 1) * EH] for u in range(2)]
        eo_tile = [hat[:, t, :] if t < GT else ctx_nat[:, t - GT, :] for t in range(ET)]
        DOWN = (7, 0, 1, 2, 3)
        assert ET == len(DOWN)
        UPS = 2 * NFE

        with nc.Block() as block:
            @block.sync
            def _(sp):
                mine = []
                tu, dd = Tally(mine), Tally(mine)
                sources = (wg.rearrange("e (k p) n -> p (e k) n", p=P), wu.rearrange("e (k p) n -> p (e k) n", p=P),
                           wd.rearrange("e (f p) n -> p (e f) n", p=P))

                def load_x(e):
                    sp.dma_start(xg, disp[bass.ds(e * CAP, CAP), :].rearrange("(t p) d -> p t d", p=P)).then_inc(xg_loaded, 16)

                load_x(0)
                with repeat(sp, E // 2 - 1, mine, {tu: 2, dd: 2 * ET}) as i:
                    for p in range(2):
                        sp.wait_ge(turned, tu.next())
                        load_x(2 * i + p + 1)
                        sp.wait_ge(down_done, dd.next(ET))
                        for w, src, n in zip(expert_w[p], sources, (DK, DK, NFE)):
                            sp.dma_start(w, src[:, bass.ds((2 * i + p + 2) * n, n), :]).then_inc(expert_loaded[p], 16)
                for e in (E - 2, E - 1):
                    sp.wait_ge(turned, tu.next())
                    load_x(e + 1)

            @block.gpsimd
            def _(pool):
                mine = []
                sv, st = Tally(mine), Tally(mine)
                pool.sem_inc(eo_saved, ET)
                pool.sem_inc(tiles_free, 1)
                sv.next(ET)
                with repeat(pool, E, mine, {sv: ET, st: 32}) as e:
                    pool.wait_ge(eo_saved, sv.next(ET))
                    pool.dma_start(eo[bass.ds(e * CAP, GT * P), :].rearrange("(t p) d -> p t d", p=P),
                                   hat[:, :, :]).then_inc(eo_stored, 16)
                    pool.dma_start(eo[bass.ds(e * CAP + GT * P, P), :], ctx_nat[:, 0, :]).then_inc(eo_stored, 16)
                    pool.wait_ge(eo_stored, st.next(32))
                    pool.sem_inc(tiles_free, 1)

            @block.scalar
            def _(act):
                mine = []
                tu, up, dn, st = (Tally(mine) for _ in range(4))

                def save_xT():
                    act.wait_ge(turned, tu.next())
                    act.activation(xT[:, 512:1024], bank[5][:, :], ACT.Copy).then_inc(xT_act, 1)
                save_xT()
                with repeat(act, E, mine, {tu: 1, up: UPS, dn: ET, st: 1}) as e:
                    for u in range(UPS):
                        act.wait_ge(up_done, up.next())
                        act.activation(silu[u % 2], bank[u % 2][:, 0:EH], ACT.Silu).then_inc(silu_ready, 1)
                    save_xT()
                    act.wait_ge(tiles_free, st.next())
                    for t in (1, 3):
                        act.wait_ge(down_done, dn.next(2))
                        act.activation(eo_tile[t], bank[DOWN[t]][:, 0:D], ACT.Copy).then_inc(eo_saved, 1)
                    dn.next()

            @block.tensor
            def _(pe):
                mine = []
                xl, xd, xa, ga, sv, w0, w1_ = (Tally(mine) for _ in range(7))
                wl = (w0, w1_)

                def turn():
                    pe.wait_ge(xg_loaded, xl.next(16))
                    for c in range(DK * ET):
                        k, t = c // ET, c % ET
                        last = pe.transpose(bank[4 + c // 4][:, (c % 4) * P:(c % 4 + 1) * P], xg[:, t, k * P:(k + 1) * P],
                                            ident[:, :])
                    last.then_inc(turned, 1)

                turn()
                per = {xl: 32, xd: 4, xa: 2, ga: 2 * UPS, sv: 2 * ET, w0: 48, w1_: 48}
                with repeat(pe, E // 2, mine, per) as i:
                    for p in range(2):
                        gate_w, up_w, down_w = expert_w[p]
                        pe.wait_ge(expert_loaded[p], wl[p].next(48))
                        pe.wait_ge(xT_dve, xd.next(2))
                        pe.wait_ge(xT_act, xa.next())
                        pe.wait_ge(eo_saved, sv.next(ET))
                        for u in range(UPS):
                            f, h = u // 2, u % 2
                            if u >= 2:
                                pe.wait_ge(act_ready, ga.next())
                            for w, b in ((gate_w, u % 2), (up_w, 2 + u % 2)):
                                for k in range(DK):
                                    last = pe.matmul(bank[b][:, 0:EH], w[:, k, f * P:(f + 1) * P],
                                                     xT[:, k * CAP + h * EH:k * CAP + (h + 1) * EH],
                                                     start=(k == 0), stop=(k == DK - 1))
                            last.then_inc(up_done, 1)
                        turn()
                        for t in range(ET):
                            for f in range(NFE):
                                if t == 0 and f == NFE - 1:
                                    pe.wait_ge(act_ready, ga.next(2))
                                last = pe.matmul(bank[DOWN[t]][:, 0:D], actE[:, f * CAP + t * P:f * CAP + (t + 1) * P],
                                                 down_w[:, f, :], start=(f == 0), stop=(f == NFE - 1))
                            last.then_inc(down_done, 1)

            @block.vector
            def _(dve):
                mine = []
                tu, sl, dn, st = (Tally(mine) for _ in range(4))

                def save_xT():
                    dve.wait_ge(turned, tu.next())
                    dve.tensor_copy(xT[:, 0:512], bank[4][:, :]).then_inc(xT_dve, 1)
                    dve.tensor_copy(xT[:, 1024:DK * CAP], bank[6][:, 0:DK * CAP - 1024]).then_inc(xT_dve, 1)
                save_xT()
                with repeat(dve, E, mine, {tu: 1, sl: UPS, dn: ET, st: 1}) as e:
                    for u in range(UPS):
                        f, h = u // 2, u % 2
                        dve.wait_ge(silu_ready, sl.next())
                        dve.tensor_tensor(actE[:, f * CAP + h * EH:f * CAP + (h + 1) * EH], bank[2 + u % 2][:, 0:EH],
                                          silu[u % 2], ALU.mult).then_inc(act_ready, 1)
                    save_xT()
                    dve.wait_ge(tiles_free, st.next())
                    for t in (0, 2, 4):
                        dve.wait_ge(down_done, dn.next(2 if t else 1))
                        dve.tensor_copy(eo_tile[t], bank[DOWN[t]][:, 0:D]).then_inc(eo_saved, 1)


        RING = 8
        gathered = [sem(f"gathered{i}") for i in range(RING)]
        first_added = sem("first_added")
        added = sem("added")
        out_stored = sem("out_stored")
        picked = [[v[:, i * D:(i + 1) * D] for i in range(RING)] for v in carve([RING * D] * 2)]

        with nc.Block() as block:
            @block.gpsimd
            def _(pool):
                for t in range(NT):
                    if t >= RING:
                        pool.wait_ge(added, t - RING + 1)
                    for c, gath in enumerate((gath1, gath2)):
                        pool.indirect_dma_start(picked[c][t % RING], None, eo[:, :],
                                                bass.IndirectOffsetOnAxis(ap=gath[:, t:t + 1], axis=0)
                                                ).then_inc(gathered[t % RING], 16)

            @block.vector
            def _(dve):
                for t in range(NT):
                    tile = x_res[:, t * D:(t + 1) * D]
                    dve.wait_ge(gathered[t % RING], 32 * (t // RING + 1))
                    dve.scalar_tensor_tensor(tile, picked[0][t % RING], wk12[:, 0, t:t + 1], tile, ALU.mult,
                                             ALU.add).then_inc(first_added, 1)
                    dve.wait_ge(first_added, t + 1)
                    dve.scalar_tensor_tensor(tile, picked[1][t % RING], wk12[:, 1, t:t + 1], tile, ALU.mult,
                                             ALU.add).then_inc(added, 1)

            @block.sync
            def _(sp):
                for i in range(NT // GT):
                    sp.wait_ge(added, GT * (i + 1))
                    sp.dma_start(out_tiles[:, i * GT:(i + 1) * GT, :], x_res_t[:, i * GT:(i + 1) * GT, :]).then_inc(out_stored, 16)
                sp.wait_ge(out_stored, 16 * (NT // GT))


_INS = ['x', 'cond_1024', 'ctx_1024', 'L0_xcond_W', 'L0_xcond_U', 'L0_ffn_Win', 'L0_ffn_bin_', 'L0_ffn_W1',
        'L0_ffn_b1', 'L0_ffn_W2', 'L0_ffn_b2', 'L0_ffn_Wout', 'L0_ffn_bout', 'L1_xcond_attn1_wq',
        'L1_xcond_attn1_wk', 'L1_xcond_attn1_wv', 'L1_xcond_attn1_wo', 'L1_xcond_attn1_bo', 'L1_xcond_attn2_wq',
        'L1_xcond_attn2_wk', 'L1_xcond_attn2_wv', 'L1_xcond_attn2_wo', 'L1_xcond_attn2_bo', 'L1_xcond_ff_w1',
        'L1_xcond_ff_b1', 'L1_xcond_ff_w2', 'L1_xcond_ff_b2', 'L1_xcond_norm1_w', 'L1_xcond_norm1_b',
        'L1_xcond_norm2_w', 'L1_xcond_norm2_b', 'L1_xcond_norm3_w', 'L1_xcond_norm3_b', 'L1_ffn_router_w',
        'L1_ffn_wg', 'L1_ffn_wu', 'L1_ffn_wd']


def kernel(**inputs):
    import numpy as _np
    import concourse.bacc as _bacc
    from concourse.bass_utils import run_bass_kernel_spmd as _run

    nc = _bacc.Bacc("TRN2", target_bir_lowering=False, num_devices=1)
    arrays, args = {}, []
    for name in _INS:
        a = _np.ascontiguousarray(inputs[name])
        arrays[f"in_{name}_dram"] = a
        args.append(nc.dram_tensor(f"in_{name}_dram", a.shape, mybir.dt.from_np(a.dtype), kind="ExternalInput").ap())
    args.append(nc.dram_tensor("out_dram", inputs["x"].shape, F32, kind="ExternalOutput").ap())
    build(nc, *args)
    r = _run(nc, [arrays], core_ids=[0])
    return r.results[0]["out_dram"]
```

```python
from contextlib import ExitStack, contextmanager

import concourse.bass as bass
from concourse import mybir

ALU = mybir.AluOpType
ACT = mybir.ActivationFunctionType
AX = mybir.AxisListType
F32 = mybir.dt.float32
F32R = mybir.dt.float32r
U32 = mybir.dt.uint32

P = 128


class Tally:

    def __init__(self, engine_tallies, start=0):
        self.base, self.n = start, 0
        engine_tallies.append(self)

    def next(self, more=1):
        self.n += more
        return self.base + self.n

    def now(self):
        return self.base + self.n


@contextmanager
def repeat(eng, times, tallies, per):
    before = [(t, t.base, t.n) for t in tallies]
    with eng.Fori(0, times) as i:
        for t, base, n in before:
            k = per.get(t, 0)
            t.base, t.n = (base + n + i * k if k else base + n), 0
        yield i
        for t, base, n in before:
            assert t.n == per.get(t, 0), (t.n, per.get(t, 0), tallies.index(t))
    for t, base, n in before:
        t.base, t.n = base, n + times * per.get(t, 0)


def build(nc, x_in, cond_in, ctx_in, L0W, L0U, Win, bin_, W1, b1, W2, b2, Wout, bout,
          wq1, wk1, wv1, wo1, bo1, wq2, wk2, wv2, wo2, bo2, ffw1, ffb1, ffw2, ffb2,
          n1w, n1b, n2w, n2b, n3w, n3b, router_w, wg, wu, wd, out):
    B, S, D = x_in.shape
    DK = D // P
    BT = S // P
    GB = 2
    G = B // GB
    GT = GB * BT
    GS = GB * S
    NT = B * BT
    M = Win.shape[1]
    INNER = W1.shape[1]
    DI = wq1.shape[1]
    DH = 64
    HP = DI // P
    DFF = ffw2.shape[0]
    NF = DFF // P
    E = router_w.shape[0]
    NFE = wg.shape[2] // P
    CAP = int(1.25 * B * S / E)
    ET = CAP // P
    EH = CAP // 2
    SLOTS = E * CAP
    TRASH = SLOTS + CAP
    EPS = 1e-5
    assert GS == 512 and 2 * M == P and CAP % P == 0 and EH <= 512 and E % 2 == 0

    disp = nc.dram_tensor("dispatched", [TRASH + 2 * B * S, D], F32).ap()
    eo = nc.dram_tensor("expert_out", [SLOTS, D], F32).ap()
    fac2_dram = nc.dram_tensor("cond_rows", [B, D], F32).ap()
    x3_dram = nc.dram_tensor("x3_rows", [B * S, D], F32).ap()

    with ExitStack() as ctx:
        def sb(name, shape, dt=F32):
            return ctx.enter_context(nc.sbuf_tensor(name, shape, dt))

        def sem(name):
            return ctx.enter_context(nc.semaphore(name))

        bank = [ctx.enter_context(nc.psum_tensor(f"bank{i}", [P, 512], F32)) for i in range(8)]

        attn = sb("attn", [P, NT * D])
        parts = sb("parts", [P, 29184], F32R)
        F_SIZE = 5120
        arena = sb("arena", [P, F_SIZE])
        xg = sb("xg", [P, GT, D])
        z = sb("z", [P, GT, D])
        hat = sb("hat", [P, GT, D])
        ctx_nat = sb("ctx_nat", [P, GT, D])
        win_sb = sb("win_sb", [P, DK, M])
        wout_sb = sb("wout_sb", [P, D])
        ident = sb("ident", [P, P])
        ones = sb("ones", [P, P])
        upper = sb("upper", [P, P])
        bias_rows = sb("bias_rows", [1, 4, D])
        condT = sb("condT", [P, DK, B])
        emb = sb("emb", [P, 3, 2 * DK, B])
        norm_b = sb("norm_b", [P, 3, 2 * DK])
        routerT = sb("routerT", [P, DK, E])
        small_w = sb("small_w", [P, 2, INNER])
        b1_sb = sb("b1_sb", [P, INNER])
        bin2 = sb("bin2", [P, 2])
        ffb1_sb = sb("ffb1_sb", [P, 2 * NF])
        stats = sb("stats", [P, GT, 6])
        both = sb("both", [P, GT, 2])
        mdiff = sb("mdiff", [P, GT])
        mdiff2 = sb("mdiff2", [P, GT])
        mean = sb("mean", [P, GT])
        veps = sb("veps", [P, GT])
        rstd = sb("rstd", [P, GT])
        minus_half = sb("minus_half", [P, GT])
        logits = sb("logits", [P, NT, E])
        nmx = sb("nmx", [P, 2, BT])
        rsum = sb("rsum", [P, 2, BT])
        rrec = sb("rrec", [P, 2, BT])
        slot1 = sb("slot1", [P, NT], U32)
        slot2 = sb("slot2", [P, NT], U32)
        gath1 = sb("gath1", [P, NT], U32)
        gath2 = sb("gath2", [P, NT], U32)
        wk12 = sb("wk12", [P, 2, NT])

        def carve(tensor, sizes):
            at, views = 0, []
            for n in sizes:
                views.append(tensor[:, at:at + n])
                at += n
            assert at <= tensor.shape[1], at
            return views

        W = DK * DI
        parts_cut = carve(parts, [W] * 10 + [2 * DK * P] * 4 + [DK * GS] * 4 + [GS] * 4 + [S] * 2)
        wv_p = [[parts_cut[4 * a + i].rearrange("p (k n) -> p k n", k=DK) for i in range(2)] for a in range(2)]
        wo_p = [[parts_cut[4 * a + 2 + i] for i in range(2)] for a in range(2)]
        wff2_p = parts_cut[8:10]
        tile_p = [[parts_cut[10 + 2 * p + i].rearrange("p (w k n) -> p w k n", w=2, k=DK) for i in range(2)] for p in range(2)]
        tile_flat = [parts_cut[10 + 2 * p:12 + 2 * p] for p in range(2)]
        h_p = [parts_cut[14 + i].rearrange("p (k n) -> p k n", k=DK) for i in range(2)]
        ctx_p = [parts_cut[16 + i].rearrange("p (k n) -> p k n", k=DK) for i in range(2)]
        qk_p = [[parts_cut[18 + 2 * p + i] for i in range(2)] for p in range(2)]
        o_p = parts_cut[22:24]

        def as_f32(ap):
            return ap.bitcast(F32)

        lead_loaded = sem("lead_loaded")
        l0w_loaded = sem("l0w_loaded")
        setup_small = sem("setup_small")
        setup_w = sem("setup_w")
        normw_loaded = sem("normw_loaded")
        zeroed = sem("zeroed")
        zero_tile = sem("zero_tile")
        const_set = sem("const_set")
        ident_set = sem("ident_set")
        tc_done = sem("tc_done")
        tc_copied = sem("tc_copied")
        f2_done = sem("f2_done")
        f2_copied = sem("f2_copied")
        f2_stored = sem("f2_stored")

        cond_nat = arena[0:B, 0:D]
        router_nat = arena[0:E, 256:256 + D]
        fac2_nat = arena[0:B, 512:512 + D]
        zero_rows = arena[:, 1024:2048]
        th = arena[:, 2048:2048 + GT * D].rearrange("p (t n) -> p t n", t=GT)
        l0w = arena[:, 3072:3584].rearrange("p (k n) -> p k n", k=DK)
        l0u = arena[:, 3584:4096].rearrange("p (k n) -> p k n", k=DK)
        nT = arena[:, 4096:5120].rearrange("p (k n) -> p k n", k=DK)
        fac2_row = sb("fac2_row", [1, GS])
        x_tiles = x_in.rearrange("b s d -> (b s) d").rearrange("(t p) d -> p t d", p=P)
        ctx_tiles = ctx_in.rearrange("b s d -> (b s) d").rearrange("(t p) d -> p t d", p=P)
        x3_tiles = x3_dram.rearrange("(t p) d -> p t d", p=P)
        out_tiles = out.rearrange("b s d -> (b s) d").rearrange("(t p) d -> p t d", p=P)
        ZERO_ROWS = P * 1024 // D
        ZERO_DMAS = -(-TRASH // ZERO_ROWS)

        def kd(w):
            return w.rearrange("(k p) n -> p k n", p=P)

        x_loaded = [sem("x_loaded0"), sem("x_loaded1")]
        ctx_loaded = sem("ctx_loaded")
        row_loaded = sem("row_loaded")
        var_ready = sem("var_ready")
        rstd_ready = sem("rstd_ready")
        dve_own = sem("dve_own")
        hat_ready = sem("hat_ready")
        tr_done = sem("tr_done")
        hT_dve = sem("hT_dve")
        hT_act = sem("hT_act")
        fac_done = sem("fac_done")
        tanh_ready = sem("tanh_ready")
        s_done = sem("s_done")
        s_saved = sem("s_saved")
        xbuf = [xg, z]

        def layer_norm_stats(dve, tiles, src, own, own_sem, var_sem):
            r = slice(tiles[0], tiles[-1] + 1)
            for t in tiles:
                dve.bn_stats(stats[:, t, :], src(t)).then_inc(own_sem, 1)
            dve.wait_ge(own_sem, own.next(len(tiles)))
            dve.tensor_tensor(both[:, r, :], stats[:, r, 1:3], stats[:, r, 4:6], ALU.add)
            dve.tensor_tensor(mdiff[:, r], stats[:, r, 1], stats[:, r, 4], ALU.subtract).then_inc(own_sem, 1)
            dve.wait_ge(own_sem, own.next())
            dve.tensor_scalar(mean[:, r], both[:, r, 0], 0.5, None, ALU.mult)
            dve.tensor_scalar(veps[:, r], both[:, r, 1], 1.0 / D, EPS, ALU.mult, ALU.add)
            dve.scalar_tensor_tensor(mdiff2[:, r], mdiff[:, r], 0.25, mdiff[:, r], ALU.mult,
                                     ALU.mult).then_inc(own_sem, 1)
            dve.wait_ge(own_sem, own.next())
            dve.tensor_tensor(veps[:, r], veps[:, r], mdiff2[:, r], ALU.add).then_inc(var_sem, 1)

        def layer_norm_apply(dve, tiles, src, dst, rs, rstd_sem, hat_sem):
            dve.wait_ge(rstd_sem, rs.next())
            for t in tiles:
                dve.tensor_scalar(dst(t), src(t), mean[:, t:t + 1], rstd[:, t:t + 1], ALU.subtract,
                                  ALU.mult).then_inc(hat_sem, 1)

        ALL = range(GT)

        with nc.Block() as block:
            @block.sync
            def _(sp):
                sp.dma_start(xg[:, :, :], x_tiles[:, 0:GT, :]).then_inc(x_loaded[0], 16)
                sp.dma_start(cond_nat, cond_in).then_inc(lead_loaded, 16)
                sp.dma_start(router_nat, router_w).then_inc(lead_loaded, 16)
                sp.dma_start(l0u, kd(L0U)).then_inc(lead_loaded, 16)
                sp.dma_start(l0w, kd(L0W)).then_inc(l0w_loaded, 16)
                sp.dma_start(ctx_nat[:, :, :], ctx_tiles[:, 0:GT, :]).then_inc(ctx_loaded, 16)
                sp.dma_start(z[:, :, :], x_tiles[:, GT:2 * GT, :]).then_inc(x_loaded[1], 16)
                sp.wait_ge(f2_copied, 1)
                sp.dma_start(fac2_dram, fac2_nat).then_inc(f2_stored, 16)
                sp.wait_ge(f2_stored, 16)
                rows = fac2_dram.rearrange("(a b) n -> a (b n)", a=1)
                sp.dma_start(fac2_row[:, :], rows[:, 0:GS]).then_inc(row_loaded, 16)
                mine = []
                hr, fac, sd = Tally(mine), Tally(mine), Tally(mine)

                def ahead(g, p, x_too):
                    sp.wait_ge(hat_ready, hr.next(GT))
                    if x_too:
                        sp.dma_start(xbuf[p][:, :, :], x_tiles[:, bass.ds(GT * (g + 2), GT), :]).then_inc(x_loaded[p], 16)
                    sp.wait_ge(fac_done, fac.next(2))
                    sp.dma_start(fac2_row[:, :], rows[:, bass.ds(GS * (g + 1), GS)]).then_inc(row_loaded, 16)
                    sp.wait_ge(s_done, sd.next(GB))
                    sp.dma_start(ctx_nat[:, :, :], ctx_tiles[:, bass.ds(GT * (g + 1), GT), :]).then_inc(ctx_loaded, 16)
                with repeat(sp, G // 2 - 1, mine, {hr: 2 * GT, fac: 4, sd: 2 * GB}) as i:
                    ahead(2 * i, 0, True)
                    ahead(2 * i + 1, 1, True)
                ahead(G - 2, 0, False)

            @block.gpsimd
            def _(pool):
                pool.memset(ident[:, :], 0.0).then_inc(const_set, 1)
                pool.memset(ones[:, :], 1.0).then_inc(const_set, 1)
                pool.memset(minus_half[:, :], -0.5).then_inc(const_set, 1)
                pool.memset(upper[:, :], 1.0).then_inc(const_set, 1)
                pool.wait_ge(const_set, 4)
                pool.affine_select(out=ident[:, :], in_=ident[:, :], compare_op=ALU.not_equal, fill=1.0, base=0,
                                   pattern=[[-1, P]], channel_multiplier=1).then_inc(ident_set, 1)
                pool.affine_select(out=upper[:, :], in_=upper[:, :], compare_op=ALU.is_gt, fill=0.0, base=0,
                                   pattern=[[1, P]], channel_multiplier=-1).then_inc(ident_set, 1)
                pool.memset(zero_rows, 0.0).then_inc(zero_tile, 1)
                mine = []
                v = Tally(mine)
                with repeat(pool, G, mine, {v: 1}) as g:
                    pool.wait_ge(var_ready, v.next())
                    pool.tensor_tensor(rstd[:, :], veps[:, :], minus_half[:, :], ALU.pow).then_inc(rstd_ready, 1)

            @block.scalar
            def _(act):
                act.wait_ge(zero_tile, 1)
                for i in range(ZERO_DMAS):
                    n = min(ZERO_ROWS, TRASH - i * ZERO_ROWS)
                    act.dma_start(disp[i * ZERO_ROWS:i * ZERO_ROWS + n, :].rearrange("(p r) d -> p (r d)", p=P),
                                  zero_rows[:, 0:n * D // P]).then_inc(zeroed, 16)
                mine = []
                tr, fac, sd = Tally(mine), Tally(mine), Tally(mine)
                with repeat(act, G, mine, {tr: 2, fac: 2, sd: 2}) as g:
                    act.wait_ge(tr_done, tr.next(2))
                    act.activation(nT[:, 1, :], bank[1][:, :], ACT.Copy).then_inc(hT_act, 1)
                    for j in range(2):
                        act.wait_ge(fac_done, fac.next())
                        act.activation(th[:, 2 * j:2 * j + 2, :], bank[2 + j][:, :], ACT.Tanh).then_inc(tanh_ready, 1)
                    for b in range(GB):
                        act.wait_ge(s_done, sd.next())
                        act.activation(attn[:, bass.ds((GT * g + b * DK) * D, DK * D)], bank[4 + b][:, :],
                                       ACT.Copy).then_inc(s_saved, 1)
                act.wait_ge(zeroed, 16 * ZERO_DMAS)

            @block.tensor
            def _(pe):
                pe.wait_ge(ident_set, 2)
                pe.wait_ge(lead_loaded, 16 * 3)
                for k in range(DK):
                    pe.transpose(bank[0][:, k * B:(k + 1) * B], cond_nat[:, k * P:(k + 1) * P], ident[0:B, 0:B])
                for k in range(DK):
                    last = pe.transpose(bank[0][:, 64 + k * E:64 + (k + 1) * E], router_nat[:, k * P:(k + 1) * P],
                                        ident[0:E, 0:E])
                last.then_inc(tc_done, 1)
                pe.wait_ge(tc_copied, 2)
                for k in range(DK):
                    last = pe.matmul(bank[7][0:B, 0:D], condT[:, k, :], l0u[:, k, :], start=(k == 0), stop=(k == DK - 1))
                last.then_inc(f2_done, 1)
                mine = []
                hr, hd, ha, cl, tn, rl = (Tally(mine) for _ in range(6))
                pe.wait_ge(l0w_loaded, 16)
                pe.wait_ge(ident_set, 2)
                with repeat(pe, G, mine, {hr: GT, hd: 1, ha: 1, cl: 16, tn: 2, rl: 16}) as g:
                    pe.wait_ge(hat_ready, hr.next(GT))
                    for k in range(DK):
                        for t in range(GT):
                            last = pe.transpose(bank[k][:, t * P:(t + 1) * P], hat[:, t, k * P:(k + 1) * P], ident[:, :])
                        last.then_inc(tr_done, 1)
                    pe.wait_ge(hT_dve, hd.next())
                    pe.wait_ge(hT_act, ha.next())
                    pe.wait_ge(row_loaded, rl.next(16))
                    for t in range(GT):
                        o = bank[2 + t // 2][:, (t % 2) * D:(t % 2 + 1) * D]
                        for k in range(DK):
                            pe.matmul(o, nT[:, k, t * P:(t + 1) * P], l0w[:, k, :], start=(k == 0), stop=False)
                        last = pe.matmul(o, ones[0:1, :], fac2_row[0:1, (t // BT) * D:(t // BT + 1) * D],
                                         start=False, stop=True)
                        if t % 2:
                            last.then_inc(fac_done, 1)
                    pe.wait_ge(ctx_loaded, cl.next(16))
                    for b in range(GB):
                        pe.wait_ge(tanh_ready, tn.next())
                        for k in range(DK):
                            for t in range(BT):
                                last = pe.matmul(bank[4 + b][:, k * D:(k + 1) * D],
                                                 ctx_nat[:, b * BT + t, k * P:(k + 1) * P], th[:, b * BT + t, :],
                                                 start=(t == 0), stop=(t == BT - 1))
                        last.then_inc(s_done, 1)

            @block.vector
            def _(dve):
                mine = []
                own, rs, tr, x0, x1 = (Tally(mine) for _ in range(5))
                xl = (x0, x1)

                def group(p):
                    dve.wait_ge(x_loaded[p], xl[p].next(16))
                    layer_norm_stats(dve, ALL, lambda t: xbuf[p][:, t, :], own, dve_own, var_ready)
                    layer_norm_apply(dve, ALL, lambda t: xbuf[p][:, t, :], lambda t: hat[:, t, :], rs, rstd_ready, hat_ready)

                def turned():
                    dve.wait_ge(tr_done, tr.next(2))
                    dve.tensor_copy(nT[:, 0, :], bank[0][:, :]).then_inc(hT_dve, 1)

                def pair():
                    group(0)
                    turned()
                    group(1)
                    turned()
                group(0)
                dve.wait_ge(tc_done, 1)
                dve.tensor_copy(condT[:, :, :], bank[0][:, 0:DK * B].rearrange("p (k b) -> p k b", k=DK)).then_inc(tc_copied, 1)
                dve.tensor_copy(routerT[:, :, :], bank[0][:, 64:64 + DK * E].rearrange("p (k e) -> p k e", k=DK)).then_inc(tc_copied, 1)
                dve.wait_ge(f2_done, 1)
                dve.tensor_copy(fac2_nat, bank[7][0:B, 0:D]).then_inc(f2_copied, 1)
                turned()
                group(1)
                turned()
                with repeat(dve, G // 2 - 1, mine, {own: 2 * (GT + 2), rs: 2, tr: 4, x0: 16, x1: 16}) as i:
                    pair()

        max_ready = sem("max_ready")
        shifted = sem("shifted")
        exps_ready = sem("exps_ready")
        attn_ready = sem("attn_ready")
        emb_done = sem("emb_done")
        raw_in = [sem(f"raw_in{i}") for i in range(4)]
        raw_hi = sem("raw_hi")
        raw_lo = sem("raw_lo")
        colmax = arena[:, 0:DK * D].rearrange("p (k e) -> p k e", k=DK)
        colsum = arena[:, 512:512 + DK * D].rearrange("p (k e) -> p k e", k=DK)
        colrec = arena[:, 1024:1024 + DK * D].rearrange("p (k e) -> p k e", k=DK)
        normw = [arena[:, 1536 + n * 1024:1536 + (n + 1) * 1024].rearrange("p (k n) -> p k n", k=DK) for n in range(3)]
        by_dtile = attn[:, :].rearrange("p (b k e) -> p k b e", b=B, k=DK)
        raw = [t[:, :, :].rearrange("p t d -> p (t d)") for t in (xg, z, hat, ctx_nat)]
        pieces = []
        for a, (wv, wo) in enumerate(((wv1, wo1), (wv2, wo2))):
            pieces += [(wv[k * P:(k + 1) * P, :], wv_p[a][0][:, k, :], wv_p[a][1][:, k, :]) for k in range(DK)]
            pieces += [(wo[j * 512:(j + 1) * 512, :].rearrange("(h p) n -> p h n", p=P),
                        wo_p[a][0][:, j * 1024:(j + 1) * 1024], wo_p[a][1][:, j * 1024:(j + 1) * 1024]) for j in range(2)]
        pieces += [(ffw2[j * 512:(j + 1) * 512, :].rearrange("(h p) n -> p h n", p=P),
                    wff2_p[0][:, j * 1024:(j + 1) * 1024], wff2_p[1][:, j * 1024:(j + 1) * 1024]) for j in range(2)]
        SMALL = 2 * 5 + 3 + 4 + 1

        with nc.Block() as block:
            @block.sync
            def _(sp):
                for n, w in enumerate((n1w, n2w, n3w)):
                    sp.dma_start(normw[n], kd(w)).then_inc(normw_loaded, 16)
                for j, (src, _, _) in enumerate(pieces):
                    if j >= 4:
                        sp.wait_ge(raw_lo, j - 3)
                    dst = raw[j % 4] if len(src.shape) == 2 else raw[j % 4].rearrange("p (h n) -> p h n", h=4)
                    sp.dma_start(dst, src).then_inc(raw_in[j % 4], 16)

            @block.gpsimd
            def _(pool):
                for j, (_, hi, lo) in enumerate(pieces):
                    pool.wait_ge(raw_hi, j + 1)
                    pool.tensor_tensor(lo, raw[j % 4], as_f32(hi), ALU.subtract).then_inc(raw_lo, 1)

            @block.tensor
            def _(pe):
                pe.wait_ge(normw_loaded, 16 * 3)
                for n in range(3):
                    for c in range(2 * DK):
                        for k in range(DK):
                            o = (n * 2 * DK + c) * B
                            last = pe.matmul(bank[6][:, o:o + B], normw[n][:, k, c * P:(c + 1) * P], condT[:, k, :],
                                             start=(k == 0), stop=(k == DK - 1))
                last.then_inc(emb_done, 1)

            @block.vector
            def _(dve):
                for k in range(DK):
                    dve.tensor_reduce(colmax[:, k, :], by_dtile[:, k].rearrange("p b e -> p e b"), AX.X,
                                      ALU.max).then_inc(max_ready, 1)
                for k in range(DK):
                    dve.wait_ge(max_ready, k + 1)
                    dve.tensor_tensor(by_dtile[:, k], by_dtile[:, k],
                                      colmax[:, k, :].unsqueeze(1).to_broadcast([P, B, D]),
                                      ALU.subtract).then_inc(shifted, 1)
                for k in range(DK):
                    dve.wait_ge(exps_ready, k + 1)
                    dve.tensor_reduce(colsum[:, k, :], by_dtile[:, k].rearrange("p b e -> p e b"), AX.X,
                                      ALU.add).then_inc(dve_own, 1)
                    dve.wait_ge(dve_own, G * (GT + 2) + 2 * k + 1)
                    dve.reciprocal(colrec[:, k, :], colsum[:, k, :]).then_inc(dve_own, 1)
                    dve.wait_ge(dve_own, G * (GT + 2) + 2 * k + 2)
                    dve.tensor_tensor(by_dtile[:, k], by_dtile[:, k],
                                      colrec[:, k, :].unsqueeze(1).to_broadcast([P, B, D]),
                                      ALU.mult).then_inc(attn_ready, 1)
                dve.wait_ge(emb_done, 1)
                dve.wait_ge(setup_small, 16 * SMALL)
                for n in range(3):
                    for c in range(2 * DK):
                        o = (n * 2 * DK + c) * B
                        dve.tensor_scalar(emb[:, n, c, :], bank[6][:, o:o + B], norm_b[:, n, c:c + 1],
                                          1.0 if c < DK else 0.0, ALU.add, ALU.add)

            @block.scalar
            def _(act):
                for n, v in enumerate((bout, bo1, bo2, ffb2)):
                    act.dma_start(bias_rows[0:1, n, :], v.rearrange("(a n) -> a n", a=1)).then_inc(setup_small, 16)
                with nc.allow_non_contiguous_dma("short bias columns"):
                    for n, v in enumerate((n1b, n2b, n3b)):
                        act.dma_start(norm_b[:, n, :], v.rearrange("(c p) -> p c", p=P)).then_inc(setup_small, 16)
                    act.dma_start(ffb1_sb[:, :], ffb1.rearrange("(c p) -> p c", p=P)).then_inc(setup_small, 16)
                for half in range(2):
                    rows = slice(half * M, (half + 1) * M)
                    act.dma_start(small_w[rows, 0, :], W1).then_inc(setup_small, 16)
                    act.dma_start(small_w[rows, 1, :], W2).then_inc(setup_small, 16)
                    act.dma_start(b1_sb[rows, :], b1).then_inc(setup_small, 16)
                    act.dma_start(bin2[rows, 0:1], bin_.rearrange("(m a) -> m a", a=1)).then_inc(setup_small, 16)
                    act.dma_start(bin2[rows, 1:2], b2.rearrange("(m a) -> m a", a=1)).then_inc(setup_small, 16)
                    act.dma_start(wout_sb[rows, :], Wout).then_inc(setup_w, 16)
                act.dma_start(win_sb[:, :, :], kd(Win)).then_inc(setup_w, 16)

                def cut(j):
                    act.wait_ge(raw_in[j % 4], 16 * (j // 4 + 1))
                    act.activation(pieces[j][1], raw[j % 4], ACT.Copy).then_inc(raw_hi, 1)
                for j in range(4):
                    cut(j)
                for k in range(DK):
                    act.wait_ge(shifted, k + 1)
                    act.activation(by_dtile[:, k], by_dtile[:, k], ACT.Exp).then_inc(exps_ready, 1)
                for j in range(4, len(pieces)):
                    cut(j)
                act.wait_ge(setup_w, 16 * 3)


        xB_loaded = sem("xB_loaded")
        ctxB_loaded = sem("ctxB_loaded")
        x_taken = sem("x_taken")
        rawt_loaded = [sem("rawt_loaded0"), sem("rawt_loaded1")]
        tile_hi = sem("tile_hi")
        tile_ready = [sem("tile_ready0"), sem("tile_ready1")]
        ctx_hi = sem("ctx_hi")
        ctx_cut = sem("ctx_cut")
        trB_done = sem("trB_done")
        nT_dve = sem("nT_dve")
        nT_act = sem("nT_act")
        x1_done = sem("x1_done")
        x2_done = sem("x2_done")
        varB_ready = sem("varB_ready")
        rstdB_ready = sem("rstdB_ready")
        hatB_ready = sem("hatB_ready")
        ln_own = sem("ln_own")
        z_own = sem("z_own")
        low_done = sem("low_done")
        low_ready = sem("low_ready")
        relu_ready = sem("relu_ready")
        relu_used = sem("relu_used")
        mlp_ready = sem("mlp_ready")
        lane_turned = sem("lane_turned")
        modulated = sem("modulated")
        h_hi_ready = sem("h_hi_ready")
        h_ready = sem("h_ready")
        qk_done = sem("qk_done")
        qk_ready = sem("qk_ready")
        v_done = sem("v_done")
        v_ready = sem("v_ready")
        scores_done = sem("scores_done")
        negmax_ready = sem("negmax_ready")
        exp_ready = sem("exp_ready")
        rrec_ready = sem("rrec_ready")
        probs_ready = sem("probs_ready")
        pT_done = sem("pT_done")
        pT_dve = sem("pT_dve")
        pT_act = sem("pT_act")
        o_done = sem("o_done")
        o_hi_ready = sem("o_hi_ready")
        o_ready = sem("o_ready")
        y_done = sem("y_done")
        glu_done = sem("glu_done")
        gelu_ready = sem("gelu_ready")
        gated_sum = sem("gated_sum")
        gated_hi = sem("gated_hi")
        gated_ready = sem("gated_ready")
        x3_ready = sem("x3_ready")
        x3_stored = sem("x3_stored")
        nrm_saved = sem("nrm_saved")
        logits_done = sem("logits_done")

        two = range(2)
        cut_b = carve(arena, [GS] * 2 + [S] * 2 + [GS] * 4 + [2 * DK * P] * 2)
        qk = cut_b[0:2]
        v_at = [v.rearrange("p (t n) -> p t n", t=BT) for v in cut_b[2:4]]
        probs = [v.rearrange("p (t k) -> p t k", t=BT) for v in cut_b[4:6]]
        pT = [v.rearrange("p (k q) -> p k q", k=BT) for v in cut_b[6:8]]
        rawt = cut_b[8:10]
        lowT, mlpT = arena[:, 0:S], arena[:, 3 * S:4 * S]
        acc = [arena[:, S:2 * S], arena[:, 2 * S:3 * S]]
        nTB = arena[:, 1024:2048].rearrange("p (k n) -> p k n", k=DK)
        ctxT = arena[:, 2560:3584].rearrange("p (k n) -> p k n", k=DK)
        relus = [arena[:, o:o + S] for o in (2048, 2048 + S, 4608, 4608 + S)]
        gelu = cut_b[0:2]
        gated_p = [parts_cut[18 + 2 * p:20 + 2 * p] for p in two]
        wq_t, wk_t = [kd(w) for w in (wq1, wq2)], [kd(w) for w in (wk1, wk2)]
        w1_t = kd(ffw1)
        TILES = 2 * HP + NF
        SLOTS_A = 2 * HP
        PASSES = ((0, 0), (0, 1), (1, 0))

        def flat(t):
            return t[:, :, :].rearrange("p t d -> p (t d)")

        with nc.Block() as block:
            @block.sync
            def _(sp):
                mine = []
                used = [Tally(mine), Tally(mine)]
                xt = Tally(mine)

                def two_tiles(i, first, second):
                    for p in two:
                        sp.wait_ge(tile_ready[p], used[p].next())
                        dst = rawt[p].rearrange("p (w k n) -> p w k n", w=2, k=DK)
                        sp.dma_start(dst[:, 0], first(2 * i + p)).then_inc(rawt_loaded[p], 16)
                        sp.dma_start(dst[:, 1], second(2 * i + p)).then_inc(rawt_loaded[p], 16)
                with repeat(sp, G, mine, {used[0]: TILES // 2, used[1]: TILES // 2, xt: 1}) as g:
                    sp.wait_ge(x_taken, xt.next())
                    sp.dma_start(xg[:, :, :], x_tiles[:, bass.ds(GT * g, GT), :]).then_inc(xB_loaded, 16)
                    sp.dma_start(ctx_nat[:, :, :], ctx_tiles[:, bass.ds(GT * g, GT), :]).then_inc(ctxB_loaded, 16)
                    for a in two:
                        with repeat(sp, HP // 2, mine, {used[0]: 1, used[1]: 1}) as i:
                            two_tiles(i, lambda h: wq_t[a][:, :, bass.ds(h * P, P)],
                                      lambda h: wk_t[a][:, :, bass.ds(h * P, P)])
                    with repeat(sp, NF // 2, mine, {used[0]: 1, used[1]: 1}) as i:
                        two_tiles(i, lambda f: w1_t[:, :, bass.ds(f * P, P)],
                                  lambda f: w1_t[:, :, bass.ds(f * P + DFF, P)])

            @block.gpsimd
            def _(pool):
                mine = []
                var, hr, ld0, ld1, qd, gl, th_, ch = (Tally(mine) for _ in range(8))
                ld = (ld0, ld1)
                pool.sem_inc(nrm_saved, 1)
                pool.sem_inc(x_taken, 1)
                pool.sem_inc(tile_ready[0], 1)
                pool.sem_inc(tile_ready[1], 1)

                def cut_tiles(attention):
                    for p in two:
                        pool.wait_ge(rawt_loaded[p], ld[p].next(32))
                        if attention:
                            pool.wait_ge(qk_done, qd.next(2))
                        else:
                            pool.wait_ge(glu_done, gl.next())
                        hi, lo = tile_flat[p]
                        pool.tensor_tensor(hi, rawt[p], ones[:, 0:1].to_broadcast([P, 2 * DK * P]), ALU.mult).then_inc(tile_hi, 1)
                        pool.wait_ge(tile_hi, th_.next())
                        pool.tensor_tensor(lo, rawt[p], as_f32(hi), ALU.subtract).then_inc(tile_ready[p], 1)

                def power(r):
                    pool.wait_ge(varB_ready, var.next())
                    pool.tensor_tensor(rstd[:, r], veps[:, r], minus_half[:, r], ALU.pow).then_inc(rstdB_ready, 1)
                every = slice(0, GT)
                per = {var: 9, hr: 5 * GT + GT, ld0: 16 * TILES, ld1: 16 * TILES, qd: 4 * HP, gl: NF,
                       th_: TILES, ch: 1}
                with repeat(pool, G, mine, per) as g:
                    for seg in range(3):
                        cut_tiles(seg > 0)
                        if seg == 0:
                            power(every)
                            power(every)
                        for l in two:
                            power(slice(BT * l, BT * (l + 1)))
                        if seg == 0:
                            pool.tensor_copy(flat(ctx_p[0]), flat(ctxT)).then_inc(ctx_hi, 1)
                            pool.wait_ge(ctx_hi, ch.next())
                            pool.tensor_tensor(flat(ctx_p[1]), flat(ctxT), as_f32(flat(ctx_p[0])),
                                               ALU.subtract).then_inc(ctx_cut, 1)
                        if seg == 2:
                            pool.wait_ge(hatB_ready, hr.next(5 * GT))
                            pool.tensor_tensor(flat(z), flat(z), flat(xg), ALU.add).then_inc(x_taken, 1)
                        tiles_per = {ld0: 32, ld1: 32, th_: 2, **({qd: 4} if seg < 2 else {gl: 2})}
                        with repeat(pool, HP // 2 - 1, mine, tiles_per) as i:
                            cut_tiles(seg < 2)
                    power(every)
                    pool.wait_ge(hatB_ready, hr.next(GT))
                    pool.tensor_copy(attn[:, bass.ds(GT * D * g, GT * D)], flat(hat)).then_inc(nrm_saved, 1)

            @block.scalar
            def _(act):
                mine = []
                tr, low, own, used, md, qd, vd, nm, pt, od, glu, gs, x3 = (Tally(mine) for _ in range(13))
                per = {tr: 6, low: 1, own: 1, used: INNER, md: 6, qd: 2 * SLOTS_A, vd: 2 * SLOTS_A, nm: 4 * SLOTS_A,
                       pt: 4 * SLOTS_A, od: 2 * SLOTS_A, glu: NF, gs: NF, x3: 1}
                act.sem_inc(x3_stored, 16)
                glu.next(2)

                def turned(dst):
                    act.wait_ge(trB_done, tr.next(2))
                    act.activation(dst[:, 1, :], bank[1][:, :], ACT.Copy).then_inc(nT_act, 1)

                def lane_hi(l):
                    act.wait_ge(modulated, md.next())
                    act.activation(h_p[0][:, :, l * S:(l + 1) * S], bank[6 + l][:, :].rearrange("p (k n) -> p k n", k=DK),
                                   ACT.Copy).then_inc(h_hi_ready, 1)

                def save_qk(l):
                    act.wait_ge(qk_done, qd.next())
                    act.activation(qk[l][:, 0:S], bank[4][:, 0:S], ACT.Copy, scale=float(DH) ** -0.5)
                    act.activation(qk[l][:, S:2 * S], bank[4][:, S:2 * S], ACT.Copy).then_inc(qk_ready, 1)

                def save_v(l):
                    act.wait_ge(v_done, vd.next())
                    act.activation(v_at[l][:, :, :], bank[5][:, 0:S].rearrange("p (t n) -> p t n", t=BT),
                                   ACT.Copy).then_inc(v_ready, 1)

                def exps(u):
                    act.wait_ge(negmax_ready, nm.next())
                    for t in range(BT):
                        last = act.activation(probs[u][:, t, :], bank[u][:, t * S:(t + 1) * S], ACT.Exp,
                                              bias=nmx[:, u, t:t + 1], accum_out=rsum[:, u, t:t + 1])
                    last.then_inc(exp_ready, 1)

                def slot(l, next1, next2):
                    act.wait_ge(pT_done, pt.next(2))
                    act.activation(pT[1][:, :, :], bank[3][:, :].rearrange("p (k q) -> p k q", k=BT),
                                   ACT.Copy).then_inc(pT_act, 1)
                    if next1:
                        exps(0)
                    act.wait_ge(o_done, od.next())
                    act.activation(o_p[0], bank[5][:, S:2 * S], ACT.Copy).then_inc(o_hi_ready, 1)
                    if next1:
                        exps(1)
                    if next2:
                        save_qk(l)
                    if next1:
                        save_v(1 - l)

                with repeat(act, G, mine, per) as g:
                    turned(ctxT)
                    turned(nTB)
                    act.wait_ge(low_done, low.next())
                    act.activation(lowT, bank[4][:, 0:S], ACT.Identity, bias=bin2[:, 0:1]).then_inc(low_ready, 1)
                    act.wait_ge(low_ready, own.next())
                    for j in range(INNER):
                        if j >= 4:
                            act.wait_ge(relu_used, used.next())
                        act.activation(relus[j % 4], lowT, ACT.Relu, scale=small_w[:, 0, j:j + 1],
                                       bias=b1_sb[:, j:j + 1]).then_inc(relu_ready, 1)
                    used.next(4)
                    for a in two:
                        lane_hi(0)
                        lane_hi(1)
                        save_qk(0)
                        save_v(0)
                        save_qk(1)
                        exps(0)
                        exps(1)
                        with repeat(act, HP // 2 - 1, mine, {qd: 4, vd: 4, nm: 8, pt: 8, od: 4}) as i:
                            for s in range(4):
                                slot(s % 2, True, True)
                        for s in range(4):
                            slot(s % 2, s < 3, s < 2)
                    lane_hi(0)
                    lane_hi(1)

                    def gelus(f, p):
                        act.wait_ge(glu_done, glu.next())
                        act.activation(gelu[p], bank[2 * p + 1][:, :], ACT.Gelu,
                                       bias=ffb1_sb[:, bass.ds(f + NF, 1)]).then_inc(gelu_ready, 1)
                        act.wait_ge(gated_sum, gs.next())
                        act.activation(gated_p[p][0], bank[2 * p][:, :], ACT.Copy).then_inc(gated_hi, 1)
                    with repeat(act, NF // 2, mine, {glu: 2, gs: 2}) as i:
                        gelus(2 * i, 0)
                        gelus(2 * i + 1, 1)
                    act.wait_ge(x3_ready, x3.next())
                    act.dma_start(x3_tiles[:, bass.ds(GT * g, GT), :], z[:, :, :]).then_inc(x3_stored, 16)
                    turned(nTB)
                act.wait_ge(x3_stored, 16 * (G + 1))

            @block.tensor
            def _(pe):
                mine = []
                cl, hd, ha, hr, mr, hc, cc, qr, vr, pr, pd, pa, oy, gd, t0, t1 = (Tally(mine) for _ in range(16))
                tl = (t0, t1)
                t0.next(), t1.next()
                per = {cl: 16, hd: 3, ha: 3, hr: 6 * GT, mr: 1, hc: 6, cc: 1, qr: 2 * SLOTS_A, vr: 2 * SLOTS_A,
                       pr: 4 * SLOTS_A, pd: 2 * SLOTS_A, pa: 2 * SLOTS_A, oy: 2 * SLOTS_A, gd: NF,
                       t0: TILES // 2, t1: TILES // 2}
                pe.sem_inc(glu_done, 2)

                def transposes(src):
                    for k in range(DK):
                        for t in range(GT):
                            last = pe.transpose(bank[k][:, t * P:(t + 1) * P], src[:, t, k * P:(k + 1) * P], ident[:, :])
                        last.then_inc(trB_done, 1)
                    pe.wait_ge(nT_dve, hd.next())
                    pe.wait_ge(nT_act, ha.next())

                def turn_lanes():
                    for l in two:
                        pe.wait_ge(hatB_ready, hr.next(BT))
                        for k in range(DK):
                            for t in range(BT):
                                last = pe.transpose(bank[6 + l][:, (k * BT + t) * P:(k * BT + t + 1) * P],
                                                    hat[:, l * BT + t, k * P:(k + 1) * P], ident[:, :])
                        last.then_inc(lane_turned, 1)

                def bias_first(y, n):
                    pe.matmul(y[:, :], ones[0:1, :], bias_rows[0:1, n, :].unsqueeze(1).to_broadcast([1, BT, D]),
                              start=True, stop=False, skip_group_check=True)

                def proj_qk(p, l, srck):
                    cols = slice(l * S, (l + 1) * S)
                    for w, src in ((0, h_p), (1, srck)):
                        for k in range(DK):
                            for n, (i, j) in enumerate(PASSES):
                                last = pe.matmul(bank[4][:, w * S:(w + 1) * S], tile_p[p][i][:, w, k, :],
                                                 src[j][:, k, cols], start=(k == 0 and n == 0),
                                                 stop=(k == DK - 1 and n == 2))
                    last.then_inc(qk_done, 1)

                def proj_v(a, h, l, srck):
                    for t in range(BT):
                        o = l * S + t * P
                        for k in range(DK):
                            for n, (i, j) in enumerate(PASSES):
                                last = pe.matmul(bank[5][:, t * P:(t + 1) * P], srck[i][:, k, o:o + P],
                                                 wv_p[a][j][:, k, bass.ds(h * P, P)], start=(k == 0 and n == 0),
                                                 stop=(k == DK - 1 and n == 2))
                    last.then_inc(v_done, 1)

                def scores(l, u):
                    rows = slice(u * DH, (u + 1) * DH)
                    for t in range(BT):
                        last = pe.matmul(bank[u][:, t * S:(t + 1) * S], qk[l][rows, t * P:(t + 1) * P],
                                         qk[l][rows, S:2 * S], start=True, stop=True)
                    last.then_inc(scores_done, 1)

                def turn(u):
                    pe.wait_ge(probs_ready, pr.next())
                    for k in range(BT):
                        for t in range(BT):
                            last = pe.transpose(bank[2 + u][:, k * S + t * P:k * S + (t + 1) * P],
                                                probs[u][:, t, k * P:(k + 1) * P], ident[:, :])
                    last.then_inc(pT_done, 1)

                def weigh(l, u):
                    for k in range(BT):
                        last = pe.matmul(bank[5][u * DH:(u + 1) * DH, S:2 * S], v_at[l][:, k, u * DH:(u + 1) * DH],
                                         pT[u][:, k, :], start=(k == 0), stop=(k == BT - 1))
                    if u:
                        last.then_inc(o_done, 1)

                def slot(a, h, p, l, srck, next1, next2, last_pair):
                    turn(0)
                    if next1:
                        pe.wait_ge(qk_ready, qr.next())
                        scores(1 - l, 0)
                    turn(1)
                    if next1:
                        scores(1 - l, 1)
                    pe.wait_ge(v_ready, vr.next())
                    pe.wait_ge(pT_dve, pd.next())
                    weigh(l, 0)
                    pe.wait_ge(pT_act, pa.next())
                    weigh(l, 1)
                    if next2:
                        if l == 0:
                            pe.wait_ge(tile_ready[1 - p], tl[1 - p].next())
                        proj_qk(1 - p, l, srck)
                    pe.wait_ge(o_ready, oy.next())
                    if next1:
                        proj_v(a, h if l == 0 else h + 1, 1 - l, srck)
                    for t in range(BT):
                        for n, (i, j) in enumerate(PASSES):
                            last = pe.matmul(bank[6 + l][:, t * D:(t + 1) * D], o_p[i][:, t * P:(t + 1) * P],
                                             wo_p[a][j][:, bass.ds(h * D, D)], start=False,
                                             stop=last_pair and t == BT - 1 and n == 2, skip_group_check=True)
                    if last_pair:
                        last.then_inc(y_done, 1)

                with repeat(pe, G, mine, per) as g:
                    pe.wait_ge(ctxB_loaded, cl.next(16))
                    transposes(ctx_nat)
                    for t in range(GT):
                        for k in range(DK):
                            last = pe.matmul(bank[2 + t // 2][:, (t % 2) * D:(t % 2 + 1) * D],
                                             ctxT[:, k, t * P:(t + 1) * P],
                                             attn[:, bass.ds(((GB * g + t // BT) * DK + k) * D, D)],
                                             start=(k == 0), stop=(k == DK - 1))
                        if t % 2:
                            last.then_inc(x1_done, 1)
                    pe.wait_ge(hatB_ready, hr.next(GT))
                    transposes(hat)
                    for b in range(GB):
                        for k in range(DK):
                            last = pe.matmul(bank[4][b * M:(b + 1) * M, 0:S], win_sb[:, k, :],
                                             nTB[:, k, b * S:(b + 1) * S], start=(k == 0), stop=(k == DK - 1))
                    last.then_inc(low_done, 1)
                    bias_first(bank[2], 0)
                    bias_first(bank[3], 0)
                    pe.wait_ge(mlp_ready, mr.next())
                    for t in range(GT):
                        b = t // BT
                        last = pe.matmul(bank[2 + t // 2][:, (t % 2) * D:(t % 2 + 1) * D],
                                         mlpT[b * M:(b + 1) * M, (t % BT) * P:(t % BT + 1) * P],
                                         wout_sb[b * M:(b + 1) * M, :], start=False, stop=t % 2 == 1,
                                         skip_group_check=True)
                        if t % 2:
                            last.then_inc(x2_done, 1)
                    hr.next(GT)
                    for a in two:
                        turn_lanes()
                        srck = h_p if a == 0 else ctx_p
                        if a == 0:
                            pe.wait_ge(ctx_cut, cc.next())
                        pe.wait_ge(h_ready, hc.next())
                        pe.wait_ge(tile_ready[0], tl[0].next())
                        proj_qk(0, 0, srck)
                        proj_v(a, 0, 0, srck)
                        pe.wait_ge(qk_ready, qr.next())
                        pe.wait_ge(h_ready, hc.next())
                        proj_qk(0, 1, srck)
                        scores(0, 0)
                        scores(0, 1)
                        bias_first(bank[6], 1 + a)
                        bias_first(bank[7], 1 + a)
                        per_four = {qr: 4, vr: 4, pr: 8, pd: 4, pa: 4, oy: 4, t0: 1, t1: 1}
                        with repeat(pe, HP // 2 - 1, mine, per_four) as i:
                            for s in range(4):
                                slot(a, 2 * i + s // 2, s // 2, s % 2, srck, True, True, False)
                        for s in range(4):
                            slot(a, HP - 2 + s // 2, s // 2, s % 2, srck, s < 3, s < 2, s >= 2)
                    turn_lanes()
                    pe.wait_ge(h_ready, hc.next(2))
                    bias_first(bank[6], 3)
                    bias_first(bank[7], 3)

                    def up(p):
                        pe.wait_ge(tile_ready[p], tl[p].next())
                        for w in (1, 0):
                            for k in range(DK):
                                for n, (i, j) in enumerate(PASSES):
                                    last = pe.matmul(bank[2 * p + w][:, :], tile_p[p][i][:, w, k, :], h_p[j][:, k, :],
                                                     start=(k == 0 and n == 0), stop=(k == DK - 1 and n == 2))
                        last.then_inc(glu_done, 1)

                    def down(p, f, last_of_group):
                        pe.wait_ge(gated_ready, gd.next())
                        for t in range(GT):
                            for n, (i, j) in enumerate(PASSES):
                                last = pe.matmul(bank[6 + t // 2][:, (t % 2) * D:(t % 2 + 1) * D],
                                                 gated_p[p][i][:, t * P:(t + 1) * P], wff2_p[j][:, bass.ds(f * D, D)],
                                                 start=False, stop=last_of_group and t % 2 == 1 and n == 2,
                                                 skip_group_check=True)
                            if last_of_group and t % 2:
                                last.then_inc(y_done, 1)
                    up(0)
                    with repeat(pe, NF // 2 - 1, mine, {gd: 2, t0: 1, t1: 1}) as i:
                        up(1)
                        down(0, 2 * i, False)
                        up(0)
                        down(1, 2 * i + 1, False)
                    up(1)
                    down(0, NF - 2, False)
                    down(1, NF - 1, True)
                    pe.wait_ge(hatB_ready, hr.next(GT))
                    transposes(hat)
                    for t in range(GT):
                        for k in range(DK):
                            last = pe.matmul(bank[4][:, t * E:(t + 1) * E], nTB[:, k, t * P:(t + 1) * P], routerT[:, k, :],
                                             start=(k == 0), stop=(k == DK - 1))
                    last.then_inc(logits_done, 1)

            @block.vector
            def _(dve):
                mine = []
                (own, rs, tr, x1, x2, rl, zo, sc, er, rr, pt, ohi, yd, ge, gh, lg, ns, rx, hz, lt, hh, xb,
                 st, st_x) = (Tally(mine) for _ in range(24))
                LN_EACH = 2
                per = {own: 6 * GT + 9 * LN_EACH, rs: 9, tr: 6, x1: 2, x2: 2, rl: INNER, zo: 11, sc: 4 * SLOTS_A,
                       er: 4 * SLOTS_A, rr: 4 * SLOTS_A, pt: 4 * SLOTS_A, ohi: 2 * SLOTS_A, yd: 6, ge: NF, gh: NF, lg: 1,
                       ns: 1, rx: INNER, hz: 6 * GT, lt: 6, hh: 6, xb: 16, st: 16, st_x: 1}

                st_x.next()

                def stats_of(tiles, src):
                    layer_norm_stats(dve, tiles, src, own, ln_own, varB_ready)

                def apply_to(tiles, src, dst):
                    layer_norm_apply(dve, tiles, src, dst, rs, rstdB_ready, hatB_ready)
                    hz.next(len(tiles))

                def xt(t):
                    return xg[:, t, :]

                def zt(t):
                    return z[:, t, :]

                def hatt(t):
                    return hat[:, t, :]

                def turned(dst):
                    dve.wait_ge(trB_done, tr.next())
                    tr.next()
                    dve.tensor_copy(dst[:, 0, :], bank[0][:, :]).then_inc(nT_dve, 1)

                def add_lane(l, dst, src, done, tally):
                    dve.wait_ge(done, tally.next())
                    part = dst[:, l * BT:(l + 1) * BT, :].rearrange("p t d -> p (t d)")
                    dve.tensor_tensor(part, part, src[:, :], ALU.add).then_inc(z_own, 1)
                    dve.wait_ge(z_own, zo.next())
                    dve.memset(mdiff2[:, BT * l:BT * (l + 1)], 0.0)

                def lane_tiles(l):
                    return range(l * BT, (l + 1) * BT)

                def modulate(g, norm):
                    for l in two:
                        dve.wait_ge(lane_turned, lt.next())
                        for k in range(DK):
                            part = bank[6 + l][:, k * S:(k + 1) * S]
                            last = dve.tensor_scalar(part, part, emb[:, norm, k, bass.ds(GB * g + l, 1)],
                                                     emb[:, norm, DK + k, bass.ds(GB * g + l, 1)], ALU.mult, ALU.add)
                        last.then_inc(modulated, 1)
                    for l in two:
                        dve.wait_ge(h_hi_ready, hh.next())
                        cols = slice(l * S, (l + 1) * S)
                        dve.tensor_tensor(h_p[1][:, :, cols], bank[6 + l][:, :].rearrange("p (k n) -> p k n", k=DK),
                                          as_f32(h_p[0][:, :, cols]), ALU.subtract).then_inc(h_ready, 1)

                def negmax(u):
                    dve.wait_ge(scores_done, sc.next())
                    dve.tensor_reduce(nmx[:, u, :], bank[u][:, :].rearrange("p (t k) -> p t k", t=BT), AX.X, ALU.max,
                                      negate=True).then_inc(negmax_ready, 1)

                def normalise(u):
                    dve.wait_ge(exp_ready, er.next())
                    dve.reciprocal(rrec[:, u, :], rsum[:, u, :]).then_inc(rrec_ready, 1)
                    dve.wait_ge(rrec_ready, rr.next())
                    for t in range(BT):
                        last = dve.tensor_scalar(probs[u][:, t, :], probs[u][:, t, :], rrec[:, u, t:t + 1], None, ALU.mult)
                    last.then_inc(probs_ready, 1)

                def slot(next1):
                    dve.wait_ge(pT_done, pt.next())
                    pt.next()
                    dve.tensor_copy(pT[0][:, :, :], bank[2][:, :].rearrange("p (k q) -> p k q", k=BT)).then_inc(pT_dve, 1)
                    if next1:
                        negmax(0)
                        negmax(1)
                        normalise(0)
                    dve.wait_ge(o_hi_ready, ohi.next())
                    dve.tensor_tensor(o_p[1], bank[5][:, S:2 * S], as_f32(o_p[0]), ALU.subtract).then_inc(o_ready, 1)
                    if next1:
                        normalise(1)

                with repeat(dve, G, mine, per) as g:
                    turned(ctxT)
                    dve.wait_ge(xB_loaded, xb.next(16))
                    for l in two:
                        add_lane(l, xg, bank[2 + l], x1_done, x1)
                    stats_of(ALL, xt)
                    dve.wait_ge(nrm_saved, ns.next())
                    apply_to(ALL, xt, hatt)
                    turned(nTB)
                    for j in range(INNER):
                        dve.wait_ge(relu_ready, rl.next())
                        if j == 0:
                            last = dve.tensor_scalar(acc[0], relus[0], small_w[:, 1, 0:1], bin2[:, 1:2], ALU.mult, ALU.add)
                        elif j == 1:
                            last = dve.tensor_scalar(acc[1], relus[1], small_w[:, 1, 1:2], None, ALU.mult)
                        else:
                            dve.wait_ge(relu_used, rx.next())
                            last = dve.scalar_tensor_tensor(acc[j % 2], relus[j % 4], small_w[:, 1, j:j + 1], acc[j % 2],
                                                            ALU.mult, ALU.add)
                        last.then_inc(relu_used, 1)
                    rx.next(2)
                    dve.wait_ge(relu_used, rx.now())
                    dve.tensor_tensor(mlpT, acc[0], acc[1], ALU.add).then_inc(mlp_ready, 1)
                    for l in two:
                        add_lane(l, xg, bank[2 + l], x2_done, x2)
                    stats_of(ALL, xt)
                    dve.wait_ge(x3_stored, st.next(16))
                    apply_to(ALL, xt, zt)
                    dve.wait_ge(hatB_ready, hz.now())
                    dve.memset(mdiff2[:, :], 0.0)
                    for n in range(3):
                        if n == 0:
                            stats_of(lane_tiles(0), zt)
                            stats_of(lane_tiles(1), zt)
                        apply_to(lane_tiles(0), zt, hatt)
                        apply_to(lane_tiles(1), zt, hatt)
                        modulate(g, n)
                        if n == 2:
                            break
                        negmax(0)
                        negmax(1)
                        normalise(0)
                        normalise(1)
                        with repeat(dve, HP // 2 - 1, mine, {sc: 8, er: 8, rr: 8, pt: 8, ohi: 4}) as i:
                            for s in range(4):
                                slot(True)
                        for s in range(4):
                            slot(s < 3)
                        for l in two:
                            add_lane(l, z, bank[6 + l], y_done, yd)
                            stats_of(lane_tiles(l), zt)
                    with repeat(dve, NF // 2, mine, {ge: 2, gh: 2}) as i:
                        for p in two:
                            dve.wait_ge(gelu_ready, ge.next())
                            dve.scalar_tensor_tensor(bank[2 * p][:, :], bank[2 * p][:, :], ffb1_sb[:, bass.ds(2 * i + p, 1)],
                                                     gelu[p], ALU.add, ALU.mult).then_inc(gated_sum, 1)
                            dve.wait_ge(gated_hi, gh.next())
                            dve.tensor_tensor(gated_p[p][1], bank[2 * p][:, :], as_f32(gated_p[p][0]),
                                              ALU.subtract).then_inc(gated_ready, 1)
                    dve.wait_ge(x_taken, st_x.next())
                    for l in two:
                        add_lane(l, z, bank[6 + l], y_done, yd)
                    dve.sem_inc(x3_ready, 1)
                    stats_of(ALL, zt)
                    apply_to(ALL, zt, hatt)
                    turned(nTB)
                    dve.wait_ge(logits_done, lg.next())
                    dve.tensor_copy(logits[:, bass.ds(GT * g, GT), :],
                                    bank[4][:, 0:GT * E].rearrange("p (t e) -> p t e", t=GT)).then_inc(z_own, 1)
                    zo.next()
                    dve.wait_ge(z_own, zo.now())
                    dve.memset(mdiff2[:, :], 0.0)

        r_own = sem("r_own")
        shifted_lg = sem("shifted_lg")
        exp_lg = sem("exp_lg")
        masks_ready = sem("masks_ready")
        counted = sem("counted")
        part_ready = sem("part_ready")
        iota_set = sem("iota_set")
        pre_done = sem("pre_done")
        slots_ready = sem("slots_ready")
        scattered = sem("scattered")
        first_raw = [sem(f"first_raw{i}") for i in range(4)]
        first_hi = sem("first_hi")
        first_lo = sem("first_lo")

        expert_cut = carve(parts, [2 * DK * NFE * P] * 2 + [NFE * D] * 2 + [DK * CAP] * 2 + [NFE * CAP] * 2)
        gu_p, down_p, xT_p, act_p = (expert_cut[2 * i:2 * i + 2] for i in range(4))
        PIECE = 1024
        first = [(w[0, k * P:(k + 1) * P, :], *(part[:, (n * DK + k) * PIECE:(n * DK + k + 1) * PIECE] for part in gu_p))
                 for n, w in enumerate((wg, wu)) for k in range(DK)]
        first += [(wd[0, j * 512:(j + 1) * 512, :].rearrange("(h p) n -> p h n", p=P),
                   *(part[:, j * PIECE:(j + 1) * PIECE] for part in down_p)) for j in range(2)]

        (prob, eqm, cand, oh1, oh2, wm, memb, ge, keep, tot, run_a, run_b, rank, iota_e, slot_e, tmp, tmp2, iota100,
         ex, above) = [c.rearrange("p (t e) -> p t e", t=NT) for c in carve(arena, [NT * E] * 20)]
        expert_i = sb("expert_i", [P, NT, E], mybir.dt.int32)
        token_i = sb("token_i", [P, NT], mybir.dt.int32)
        token_f = sb("token_f", [P, NT])
        top_p = sb("top_p", [P, 2, NT])
        top_w = sb("top_w", [P, 2, NT])
        by_token = sb("by_token", [P, 4, NT])
        thr, step, sel, trial, part, room, flag = (sb(n, [P, E]) for n in
                                                   ("thr", "step", "sel", "trial", "part", "room", "flag"))

        def over_e(v):
            return v.unsqueeze(2).to_broadcast([P, NT, E])

        def over_t(v):
            return v.unsqueeze(1).to_broadcast([P, NT, E])

        HALVINGS = 23
        DOUBLINGS = (64, 32, 16, 8, 4, 2, 1)
        TINY = 2.0 ** -126
        COUNTS = 1 + len(DOUBLINGS) + HALVINGS + 1

        with nc.Block() as block:
            @block.gpsimd
            def _(pool):
                pool.iota(expert_i[:, :, :], [[0, NT], [1, E]], base=0, channel_multiplier=0).then_inc(iota_set, 1)
                pool.iota(token_i[:, :], [[P, NT]], base=0, channel_multiplier=1).then_inc(iota_set, 1)
                for j, (_, hi, lo) in enumerate(first):
                    pool.wait_ge(first_hi, j + 1)
                    pool.tensor_tensor(lo, raw[j % 4], as_f32(hi), ALU.subtract).then_inc(first_lo, 1)
                pool.wait_ge(slots_ready, 4)
                for t in range(NT):
                    for slot in (slot1, slot2):
                        pool.indirect_dma_start(disp[:, :], bass.IndirectOffsetOnAxis(ap=slot[:, t:t + 1], axis=0),
                                                attn[:, t * D:(t + 1) * D], None).then_inc(scattered, 16)
                pool.wait_ge(scattered, 16 * 2 * NT)

            @block.sync
            def _(sp):
                for j, (src, _, _) in enumerate(first):
                    if j >= 4:
                        sp.wait_ge(first_lo, j - 3)
                    dst = raw[j % 4] if len(src.shape) == 2 else raw[j % 4].rearrange("p (h n) -> p h n", h=4)
                    sp.dma_start(dst, src).then_inc(first_raw[j % 4], 16)

            @block.scalar
            def _(act):
                act.wait_ge(shifted_lg, 1)
                act.activation(ex, tmp, ACT.Exp).then_inc(exp_lg, 1)
                for j, (_, hi, _) in enumerate(first):
                    act.wait_ge(first_raw[j % 4], 16 * (j // 4 + 1))
                    act.activation(hi, raw[j % 4], ACT.Copy).then_inc(first_hi, 1)

            @block.tensor
            def _(pe):
                for n in range(COUNTS):
                    pe.wait_ge(part_ready, n + 1)
                    pe.matmul(bank[n % 2][:, 0:E], ones[:, :], part[:, :], start=True, stop=True).then_inc(counted, 1)
                for n, mask in enumerate((eqm, keep)):
                    pe.wait_ge(masks_ready, n + 1)
                    src = mask.rearrange("p t e -> p (t e)")
                    pe.matmul(bank[2][:, 0:NT * E], upper[:, :], src, start=True, stop=True)
                    pe.matmul(bank[3][:, 0:NT * E], ones[:, :], src, start=True, stop=True).then_inc(pre_done, 1)

            @block.vector
            def _(dve):
                steps = [0]

                def link(ins):
                    ins.then_inc(r_own, 1)
                    steps[0] += 1
                    dve.wait_ge(r_own, steps[0])

                dve.wait_ge(iota_set, 2)
                dve.tensor_copy(iota_e, expert_i[:, :, :])
                link(dve.tensor_copy(token_f[:, :], token_i[:, :]))
                dve.tensor_scalar(iota100, iota_e, 100.0, None, ALU.add)
                lmax, lsum, lrec, first = (by_token[:, i, :] for i in range(4))
                link(dve.tensor_reduce(lmax, logits[:, :, :], AX.X, ALU.max))
                dve.tensor_tensor(tmp, logits[:, :, :], over_e(lmax), ALU.subtract).then_inc(shifted_lg, 1)
                dve.wait_ge(exp_lg, 1)
                link(dve.tensor_reduce(lsum, ex, AX.X, ALU.add))
                link(dve.reciprocal(lrec, lsum))
                link(dve.tensor_tensor(prob, ex, over_e(lrec), ALU.mult))
                for c, (p, onehot) in enumerate(((prob, oh1), (tmp2, oh2))):
                    if c:
                        link(dve.scalar_tensor_tensor(tmp2, oh1, -2.0, prob, ALU.mult, ALU.add))
                    link(dve.tensor_reduce(top_p[:, c, :], p, AX.X, ALU.max))
                    link(dve.tensor_tensor(eqm, p, over_e(top_p[:, c, :]), ALU.is_equal))
                    link(dve.scalar_tensor_tensor(cand, eqm, -100.0, iota100, ALU.mult, ALU.add))
                    link(dve.tensor_reduce(first, cand, AX.X, ALU.min))
                    link(dve.tensor_tensor(onehot, iota_e, over_e(first), ALU.is_equal))
                link(dve.tensor_tensor(lsum, top_p[:, 0, :], top_p[:, 1, :], ALU.add))
                link(dve.tensor_scalar(lsum, lsum, 1e-6, None, ALU.add))
                link(dve.reciprocal(lrec, lsum))
                for c in range(2):
                    link(dve.tensor_tensor(top_w[:, c, :], top_p[:, c, :], lrec, ALU.mult))
                dve.tensor_tensor(memb, oh1, oh2, ALU.add)
                dve.tensor_tensor(tmp, oh1, over_e(top_w[:, 0, :]), ALU.mult)
                link(dve.tensor_tensor(tmp2, oh2, over_e(top_w[:, 1, :]), ALU.mult))
                link(dve.tensor_tensor(tmp, tmp, tmp2, ALU.add))
                link(dve.scalar_tensor_tensor(tmp, tmp, TINY, tmp, ALU.is_ge, ALU.mult))
                link(dve.scalar_tensor_tensor(wm, memb, -1.0, tmp, ALU.add, ALU.add))

                counts = [0]

                def count(mask_of):
                    link(mask_of(ge))
                    dve.tensor_reduce(part[:, :], ge.rearrange("p t e -> p e t"), AX.X, ALU.add).then_inc(part_ready, 1)
                    counts[0] += 1
                    dve.wait_ge(counted, counts[0])
                    return bank[(counts[0] - 1) % 2][:, 0:E]

                def enough(dst):
                    total = count(lambda o: dve.tensor_tensor(o, wm, over_t(trial[:, :]), ALU.is_ge))
                    link(dve.tensor_scalar(dst[:, :], total, float(CAP), None, ALU.is_ge))

                dve.memset(thr[:, :], TINY)
                link(dve.memset(trial[:, :], TINY))
                enough(flag)
                for k in DOUBLINGS:
                    link(dve.tensor_scalar(trial[:, :], thr[:, :], 2.0 ** k, None, ALU.mult))
                    enough(sel)
                    link(dve.tensor_scalar(sel[:, :], sel[:, :], 2.0 ** k - 1.0, 1.0, ALU.mult, ALU.add))
                    link(dve.tensor_tensor(thr[:, :], thr[:, :], sel[:, :], ALU.mult))
                link(dve.tensor_scalar(step[:, :], thr[:, :], 0.5, None, ALU.mult))
                for k in range(HALVINGS):
                    link(dve.tensor_tensor(trial[:, :], thr[:, :], step[:, :], ALU.add))
                    enough(sel)
                    link(dve.tensor_tensor(sel[:, :], sel[:, :], step[:, :], ALU.mult))
                    dve.tensor_scalar(step[:, :], step[:, :], 0.5, None, ALU.mult)
                    link(dve.tensor_tensor(thr[:, :], thr[:, :], sel[:, :], ALU.add))
                link(dve.tensor_tensor(thr[:, :], thr[:, :], flag[:, :], ALU.mult))
                total = count(lambda o: dve.tensor_tensor(o, wm, over_t(thr[:, :]), ALU.is_gt))
                dve.tensor_scalar(room[:, :], total, -1.0, float(CAP), ALU.mult, ALU.add)

                def before(n):
                    flat = lambda b: bank[b][:, 0:NT * E].rearrange("p (t e) -> p t e", t=NT)
                    dve.wait_ge(pre_done, n + 1)
                    dve.tensor_copy(tot, flat(3))
                    link(dve.tensor_copy(run_a, flat(3)))
                    a, b = run_a, run_b
                    shift = 1
                    while shift < NT:
                        dve.tensor_copy(b[:, 0:shift, :], a[:, 0:shift, :])
                        link(dve.tensor_tensor(b[:, shift:NT, :], a[:, shift:NT, :], a[:, 0:NT - shift, :], ALU.add))
                        a, b = b, a
                        shift *= 2
                    link(dve.tensor_tensor(a, a, tot, ALU.subtract))
                    link(dve.tensor_tensor(rank, a, flat(2), ALU.add))

                dve.tensor_tensor(eqm, wm, over_t(thr[:, :]), ALU.is_equal).then_inc(masks_ready, 1)
                before(0)
                link(dve.tensor_tensor(tmp, rank, over_t(room[:, :]), ALU.is_lt))
                link(dve.tensor_tensor(tmp, tmp, eqm, ALU.mult))
                dve.tensor_tensor(keep, ge, tmp, ALU.add).then_inc(masks_ready, 1)
                before(1)
                link(dve.scalar_tensor_tensor(slot_e, iota_e, float(CAP), rank, ALU.mult, ALU.add))
                link(dve.tensor_tensor(slot_e, slot_e, keep, ALU.mult))
                for c, (onehot, slot, gath) in enumerate(((oh1, slot1, gath1), (oh2, slot2, gath2))):
                    place, kept, lost, _ = (by_token[:, i, :] for i in range(4))
                    dve.tensor_tensor(tmp, onehot, slot_e, ALU.mult)
                    link(dve.tensor_tensor(tmp2, onehot, keep, ALU.mult))
                    dve.tensor_reduce(place, tmp, AX.X, ALU.add)
                    link(dve.tensor_reduce(kept, tmp2, AX.X, ALU.add))
                    dve.tensor_tensor(wk12[:, c, :], top_w[:, c, :], kept, ALU.mult)
                    dve.tensor_scalar(lost, kept, -1.0, 1.0, ALU.mult, ALU.add)
                    link(dve.tensor_scalar(tmp[:, :, 0], token_f[:, :], float(TRASH + c * B * S), None, ALU.add))
                    link(dve.tensor_tensor(lost, lost, tmp[:, :, 0], ALU.mult))
                    link(dve.tensor_tensor(lost, lost, place, ALU.add))
                    dve.tensor_copy(slot[:, :], lost).then_inc(slots_ready, 1)
                    dve.tensor_copy(gath[:, :], place).then_inc(slots_ready, 1)
                    dve.wait_ge(slots_ready, 2 * c + 2)


        x_in_e = sem("x_in_e")
        gu_loaded = sem("gu_loaded")
        down_loaded = sem("down_loaded")
        gu_hi = sem("gu_hi")
        gu_cut = sem("gu_cut")
        down_hi = sem("down_hi")
        down_cut = sem("down_cut")
        turned_e = sem("turned_e")
        xT_hi = sem("xT_hi")
        xT_cut = sem("xT_cut")
        up_done = sem("up_done")
        silu_ready = sem("silu_ready")
        act_product = sem("act_product")
        act_hi = sem("act_hi")
        act_cut = sem("act_cut")
        down_done = sem("down_done")
        eo_saved = sem("eo_saved")
        eo_stored = sem("eo_stored")

        raw_gu, raw_down, x_e = carve(attn, [4 * PIECE, 2 * PIECE, ET * D])
        x_e = x_e.rearrange("p (t d) -> p t d", t=ET)
        RING_U = 3
        silu = [flat(z)[:, r * EH:(r + 1) * EH] for r in range(RING_U)]
        eo_tile = [hat[:, t, :] if t < GT else ctx_nat[:, t - GT, :] for t in range(ET)]
        GATE, UP = (0, 1, 4), (2, 3, 5)
        DOWN = (7, 0, 1, 2, 3)
        TURN = ((4, 0, 512), (5, 512, 512), (6, 1024, DK * CAP - 1024))
        assert ET == len(DOWN) and DK * CAP > 1024
        UPS = 2 * NFE

        def piece(t, j):
            return t[:, j * PIECE:(j + 1) * PIECE]

        with nc.Block() as block:
            @block.sync
            def _(sp):
                mine = []
                tu, gc, dc, sv = (Tally(mine) for _ in range(4))
                sources = (wg.rearrange("e (k p) n -> p (e k) n", p=P), wu.rearrange("e (k p) n -> p (e k) n", p=P),
                           wd.rearrange("e (f p) n -> p (e f) n", p=P))

                def load_x(e):
                    sp.dma_start(x_e, disp[bass.ds(e * CAP, CAP), :].rearrange("(t p) d -> p t d", p=P)).then_inc(x_in_e, 16)

                def load_gu(e):
                    for n in range(2):
                        sp.dma_start(raw_gu[:, n * 2 * PIECE:(n + 1) * 2 * PIECE].rearrange("p (k n) -> p k n", k=DK),
                                     sources[n][:, bass.ds(e * DK, DK), :]).then_inc(gu_loaded, 16)

                def load_down(e):
                    sp.dma_start(raw_down.rearrange("p (f n) -> p f n", f=NFE),
                                 sources[2][:, bass.ds(e * NFE, NFE), :]).then_inc(down_loaded, 16)

                def store(e):
                    sp.wait_ge(eo_saved, sv.next(ET))
                    sp.dma_start(eo[bass.ds(e * CAP, GT * P), :].rearrange("(t p) d -> p t d", p=P),
                                 hat[:, :, :]).then_inc(eo_stored, 16)
                    sp.dma_start(eo[bass.ds(e * CAP + GT * P, P), :], ctx_nat[:, 0, :]).then_inc(eo_stored, 16)

                sv.next(ET)
                load_x(0)
                load_gu(1)
                sp.wait_ge(turned_e, tu.next())
                load_x(1)
                load_down(1)
                with repeat(sp, E - 2, mine, {tu: 1, gc: 4, dc: 1, sv: ET}) as i:
                    sp.wait_ge(gu_cut, gc.next(4))
                    load_gu(i + 2)
                    sp.wait_ge(turned_e, tu.next())
                    load_x(i + 2)
                    store(i)
                    sp.wait_ge(down_cut, dc.next())
                    load_down(i + 2)
                store(E - 2)
                store(E - 1)
                sp.wait_ge(eo_stored, 32 * (E + 1))

            @block.gpsimd
            def _(pool):
                mine = []
                gh, dl, dd, dh = (Tally(mine) for _ in range(4))
                pool.sem_inc(eo_saved, ET)
                pool.sem_inc(eo_stored, 32)
                with repeat(pool, E - 1, mine, {gh: 4, dl: 16, dd: ET, dh: 1}) as e:
                    for j in (1, 3):
                        pool.wait_ge(gu_hi, gh.next(2))
                        pool.tensor_tensor(piece(gu_p[1], j), piece(raw_gu, j), as_f32(piece(gu_p[0], j)),
                                           ALU.subtract).then_inc(gu_cut, 1)
                    pool.wait_ge(down_loaded, dl.next(16))
                    pool.wait_ge(down_done, dd.next(ET))
                    pool.tensor_tensor(down_p[0], raw_down, ones[:, 0:1].to_broadcast([P, NFE * D]), ALU.mult).then_inc(down_hi, 1)
                    pool.wait_ge(down_hi, dh.next())
                    pool.tensor_tensor(down_p[1], raw_down, as_f32(down_p[0]), ALU.subtract).then_inc(down_cut, 1)

            @block.scalar
            def _(act):
                mine = []
                tu, up, ap_, gl, dn, st = (Tally(mine) for _ in range(6))

                def hi_xT():
                    act.wait_ge(turned_e, tu.next())
                    for b, o, n in TURN:
                        act.activation(xT_p[0][:, o:o + n], bank[b][:, 0:n], ACT.Copy).then_inc(xT_hi, 1)

                def expert(more):
                    for u in range(UPS):
                        f, h, r = u // 2, u % 2, u % RING_U
                        act.wait_ge(up_done, up.next())
                        act.activation(silu[r], bank[GATE[r]][:, 0:EH], ACT.Silu).then_inc(silu_ready, 1)
                        act.wait_ge(act_product, ap_.next())
                        o = f * CAP + h * EH
                        act.activation(act_p[0][:, o:o + EH], bank[UP[r]][:, 0:EH], ACT.Copy).then_inc(act_hi, 1)
                    if more:
                        act.wait_ge(gu_loaded, gl.next(32))
                        for j in range(4):
                            act.activation(piece(gu_p[0], j), piece(raw_gu, j), ACT.Copy).then_inc(gu_hi, 1)
                        hi_xT()
                    act.wait_ge(eo_stored, st.next(32))
                    for t in (1, 3):
                        act.wait_ge(down_done, dn.next(2))
                        act.activation(eo_tile[t], bank[DOWN[t]][:, 0:D], ACT.Copy).then_inc(eo_saved, 1)
                    dn.next()
                hi_xT()
                with repeat(act, E - 1, mine, {tu: 1, up: UPS, ap_: UPS, gl: 32, dn: ET, st: 32}) as e:
                    expert(True)
                expert(False)

            @block.tensor
            def _(pe):
                mine = []
                xl, xc, gc, dc, ac, sv = (Tally(mine) for _ in range(6))

                def turn():
                    pe.wait_ge(x_in_e, xl.next(16))
                    for c in range(DK * ET):
                        k, t = c // ET, c % ET
                        last = pe.transpose(bank[4 + c // 4][:, (c % 4) * P:(c % 4 + 1) * P], x_e[:, t, k * P:(k + 1) * P],
                                            ident[:, :])
                    last.then_inc(turned_e, 1)

                def expert(cut_here, more):
                    if cut_here:
                        pe.wait_ge(gu_cut, gc.next(4))
                    pe.wait_ge(xT_cut, xc.next(3))
                    pe.wait_ge(eo_saved, sv.next(ET))
                    for u in range(UPS):
                        f, h, r = u // 2, u % 2, u % RING_U
                        if u >= RING_U:
                            pe.wait_ge(act_cut, ac.next())
                        for n, b in ((0, GATE[r]), (1, UP[r])):
                            for k in range(DK):
                                for m, (i, j) in enumerate(PASSES):
                                    o = (n * DK + k) * PIECE + f * P
                                    last = pe.matmul(bank[b][:, 0:EH], gu_p[i][:, o:o + P],
                                                     xT_p[j][:, k * CAP + h * EH:k * CAP + (h + 1) * EH],
                                                     start=(k == 0 and m == 0), stop=(k == DK - 1 and m == 2))
                        last.then_inc(up_done, 1)
                    for t in range(ET):
                        if t == 0:
                            pe.wait_ge(act_cut, ac.next())
                            if cut_here:
                                pe.wait_ge(down_cut, dc.next())
                        for f in range(NFE):
                            if t == 0 and f == NFE - 1:
                                pe.wait_ge(act_cut, ac.next(2))
                            for m, (i, j) in enumerate(PASSES):
                                o = f * CAP + t * P
                                last = pe.matmul(bank[DOWN[t]][:, 0:D], act_p[i][:, o:o + P],
                                                 down_p[j][:, f * D:(f + 1) * D],
                                                 start=(f == 0 and m == 0), stop=(f == NFE - 1 and m == 2))
                        last.then_inc(down_done, 1)
                        if more and t == 0:
                            turn()

                turn()
                expert(False, True)
                with repeat(pe, E - 2, mine, {xl: 16, xc: 3, gc: 4, dc: 1, ac: UPS, sv: ET}) as e:
                    expert(True, True)
                expert(True, False)

            @block.vector
            def _(dve):
                mine = []
                xh, sl, ah, gh, dn, st = (Tally(mine) for _ in range(6))

                def lo_xT():
                    for b, o, n in TURN:
                        dve.wait_ge(xT_hi, xh.next())
                        dve.tensor_tensor(xT_p[1][:, o:o + n], bank[b][:, 0:n], as_f32(xT_p[0][:, o:o + n]),
                                          ALU.subtract).then_inc(xT_cut, 1)

                def expert(more):
                    for u in range(UPS):
                        f, h, r = u // 2, u % 2, u % RING_U
                        dve.wait_ge(silu_ready, sl.next())
                        up = bank[UP[r]][:, 0:EH]
                        dve.tensor_tensor(up, up, silu[r], ALU.mult).then_inc(act_product, 1)
                        dve.wait_ge(act_hi, ah.next())
                        o = f * CAP + h * EH
                        dve.tensor_tensor(act_p[1][:, o:o + EH], up, as_f32(act_p[0][:, o:o + EH]),
                                          ALU.subtract).then_inc(act_cut, 1)
                    if more:
                        for j in (0, 2):
                            dve.wait_ge(gu_hi, gh.next(1 if j == 0 else 2))
                            dve.tensor_tensor(piece(gu_p[1], j), piece(raw_gu, j), as_f32(piece(gu_p[0], j)),
                                              ALU.subtract).then_inc(gu_cut, 1)
                        gh.next()
                        lo_xT()
                    dve.wait_ge(eo_stored, st.next(32))
                    for t in (0, 2, 4):
                        dve.wait_ge(down_done, dn.next(2 if t else 1))
                        dve.tensor_copy(eo_tile[t], bank[DOWN[t]][:, 0:D]).then_inc(eo_saved, 1)
                lo_xT()
                with repeat(dve, E - 1, mine, {xh: 3, sl: UPS, ah: UPS, gh: 4, dn: ET, st: 32}) as e:
                    expert(True)
                expert(False)


        RING = 8
        gathered = [sem(f"gathered{i}") for i in range(RING)]
        x3_back = [sem(f"x3_back{i}") for i in range(G)]
        first_added = sem("first_added")
        added = sem("added")
        out_stored = sem("out_stored")
        picked = [[v[:, i * D:(i + 1) * D] for i in range(RING)] for v in carve(arena, [RING * D] * 2)]
        x3_t = attn[:, :].rearrange("p (t d) -> p t d", t=NT)

        with nc.Block() as block:
            @block.gpsimd
            def _(pool):
                for t in range(NT):
                    if t >= RING:
                        pool.wait_ge(added, t - RING + 1)
                    for c, gath in enumerate((gath1, gath2)):
                        pool.indirect_dma_start(picked[c][t % RING], None, eo[:, :],
                                                bass.IndirectOffsetOnAxis(ap=gath[:, t:t + 1], axis=0)
                                                ).then_inc(gathered[t % RING], 16)

            @block.scalar
            def _(act):
                for i in range(G):
                    act.dma_start(x3_t[:, i * GT:(i + 1) * GT, :], x3_tiles[:, i * GT:(i + 1) * GT, :]).then_inc(x3_back[i], 16)

            @block.vector
            def _(dve):
                for t in range(NT):
                    tile = x3_t[:, t, :]
                    if t % GT == 0:
                        dve.wait_ge(x3_back[t // GT], 16)
                    dve.wait_ge(gathered[t % RING], 32 * (t // RING + 1))
                    dve.scalar_tensor_tensor(tile, picked[0][t % RING], wk12[:, 0, t:t + 1], tile, ALU.mult,
                                             ALU.add).then_inc(first_added, 1)
                    dve.wait_ge(first_added, t + 1)
                    dve.scalar_tensor_tensor(tile, picked[1][t % RING], wk12[:, 1, t:t + 1], tile, ALU.mult,
                                             ALU.add).then_inc(added, 1)

            @block.sync
            def _(sp):
                for i in range(NT // GT):
                    sp.wait_ge(added, GT * (i + 1))
                    sp.dma_start(out_tiles[:, i * GT:(i + 1) * GT, :], x3_t[:, i * GT:(i + 1) * GT, :]).then_inc(out_stored, 16)
                sp.wait_ge(out_stored, 16 * (NT // GT))


_INS = ['x', 'cond_1024', 'ctx_1024', 'L0_xcond_W', 'L0_xcond_U', 'L0_ffn_Win', 'L0_ffn_bin_', 'L0_ffn_W1',
        'L0_ffn_b1', 'L0_ffn_W2', 'L0_ffn_b2', 'L0_ffn_Wout', 'L0_ffn_bout', 'L1_xcond_attn1_wq',
        'L1_xcond_attn1_wk', 'L1_xcond_attn1_wv', 'L1_xcond_attn1_wo', 'L1_xcond_attn1_bo', 'L1_xcond_attn2_wq',
        'L1_xcond_attn2_wk', 'L1_xcond_attn2_wv', 'L1_xcond_attn2_wo', 'L1_xcond_attn2_bo', 'L1_xcond_ff_w1',
        'L1_xcond_ff_b1', 'L1_xcond_ff_w2', 'L1_xcond_ff_b2', 'L1_xcond_norm1_w', 'L1_xcond_norm1_b',
        'L1_xcond_norm2_w', 'L1_xcond_norm2_b', 'L1_xcond_norm3_w', 'L1_xcond_norm3_b', 'L1_ffn_router_w',
        'L1_ffn_wg', 'L1_ffn_wu', 'L1_ffn_wd']


def kernel(**inputs):
    import numpy as _np
    import concourse.bacc as _bacc
    from concourse.bass_utils import run_bass_kernel_spmd as _run

    nc = _bacc.Bacc("TRN2", target_bir_lowering=False, num_devices=1)
    arrays, args = {}, []
    for name in _INS:
        a = _np.ascontiguousarray(inputs[name])
        arrays[f"in_{name}_dram"] = a
        args.append(nc.dram_tensor(f"in_{name}_dram", a.shape, mybir.dt.from_np(a.dtype), kind="ExternalInput").ap())
    args.append(nc.dram_tensor("out_dram", inputs["x"].shape, F32, kind="ExternalOutput").ap())
    build(nc, *args)
    r = _run(nc, [arrays], core_ids=[0])
    return r.results[0]["out_dram"]
```

```python
from contextlib import ExitStack, contextmanager

import concourse.bass as bass
from concourse import mybir

ALU = mybir.AluOpType
ACT = mybir.ActivationFunctionType
AX = mybir.AxisListType
F32 = mybir.dt.float32
F32R = mybir.dt.float32r
U32 = mybir.dt.uint32

P = 128


class Tally:

    def __init__(self, engine_tallies, start=0):
        self.base, self.n = start, 0
        engine_tallies.append(self)

    def next(self, more=1):
        self.n += more
        return self.base + self.n

    def now(self):
        return self.base + self.n


@contextmanager
def repeat(eng, times, tallies, per):
    before = [(t, t.base, t.n) for t in tallies]
    with eng.Fori(0, times) as i:
        for t, base, n in before:
            k = per.get(t, 0)
            t.base, t.n = (base + n + i * k if k else base + n), 0
        yield i
        for t, base, n in before:
            assert t.n == per.get(t, 0), (t.n, per.get(t, 0), tallies.index(t))
    for t, base, n in before:
        t.base, t.n = base, n + times * per.get(t, 0)


def build(nc, x_in, cond_in, ctx_in, L0W, L0U, Win, bin_, W1, b1, W2, b2, Wout, bout,
          wq1, wk1, wv1, wo1, bo1, wq2, wk2, wv2, wo2, bo2, ffw1, ffb1, ffw2, ffb2,
          n1w, n1b, n2w, n2b, n3w, n3b, router_w, wg, wu, wd, out):
    B, S, D = x_in.shape
    DK = D // P
    BT = S // P
    GB = 2
    G = B // GB
    GT = GB * BT
    GS = GB * S
    NT = B * BT
    M = Win.shape[1]
    INNER = W1.shape[1]
    DI = wq1.shape[1]
    DH = 64
    HP = DI // P
    DFF = ffw2.shape[0]
    NF = DFF // P
    E = router_w.shape[0]
    NFE = wg.shape[2] // P
    CAP = int(1.25 * B * S / E)
    ET = CAP // P
    EH = CAP // 2
    SLOTS = E * CAP
    TRASH = SLOTS + CAP
    EPS = 1e-5
    assert GS == 512 and 2 * M == P and CAP % P == 0 and EH <= 512 and E % 2 == 0

    disp = nc.dram_tensor("dispatched", [TRASH + 2 * B * S, D], F32).ap()
    eo = nc.dram_tensor("expert_out", [SLOTS, D], F32).ap()
    fac2_dram = nc.dram_tensor("cond_rows", [B, D], F32).ap()
    x3_dram = nc.dram_tensor("x3_rows", [B * S, D], F32).ap()

    with ExitStack() as ctx:
        def sb(name, shape, dt=F32):
            return ctx.enter_context(nc.sbuf_tensor(name, shape, dt))

        def sem(name):
            return ctx.enter_context(nc.semaphore(name))

        bank = [ctx.enter_context(nc.psum_tensor(f"bank{i}", [P, 512], F32)) for i in range(8)]

        attn = sb("attn", [P, NT * D])
        parts = sb("parts", [P, 29184], F32R)
        F_SIZE = 5120
        arena = sb("arena", [P, F_SIZE])
        xg = sb("xg", [P, GT, D])
        z = sb("z", [P, GT, D])
        hat = sb("hat", [P, GT, D])
        ctx_nat = sb("ctx_nat", [P, GT, D])
        win_sb = sb("win_sb", [P, DK, M])
        wout_sb = sb("wout_sb", [P, D])
        ident = sb("ident", [P, P])
        ones = sb("ones", [P, P])
        upper = sb("upper", [P, P])
        bias_rows = sb("bias_rows", [1, 4, D])
        condT = sb("condT", [P, DK, B])
        emb = sb("emb", [P, 3, 2 * DK, B])
        norm_b = sb("norm_b", [P, 3, 2 * DK])
        routerT = sb("routerT", [P, DK, E])
        small_w = sb("small_w", [P, 2, INNER])
        b1_sb = sb("b1_sb", [P, INNER])
        bin2 = sb("bin2", [P, 2])
        ffb1_sb = sb("ffb1_sb", [P, 2 * NF])
        stats = sb("stats", [P, GT, 6])
        both = sb("both", [P, GT, 2])
        mdiff = sb("mdiff", [P, GT])
        mdiff2 = sb("mdiff2", [P, GT])
        mean = sb("mean", [P, GT])
        veps = sb("veps", [P, GT])
        rstd = sb("rstd", [P, GT])
        minus_half = sb("minus_half", [P, GT])
        logits = sb("logits", [P, NT, E])
        nmx = sb("nmx", [P, 2, BT])
        rsum = sb("rsum", [P, 2, BT])
        rrec = sb("rrec", [P, 2, BT])
        slot1 = sb("slot1", [P, NT], U32)
        slot2 = sb("slot2", [P, NT], U32)
        gath1 = sb("gath1", [P, NT], U32)
        gath2 = sb("gath2", [P, NT], U32)
        wk12 = sb("wk12", [P, 2, NT])

        def carve(tensor, sizes):
            at, views = 0, []
            for n in sizes:
                views.append(tensor[:, at:at + n])
                at += n
            assert at <= tensor.shape[1], at
            return views

        W = DK * DI
        parts_cut = carve(parts, [W] * 10 + [2 * DK * P] * 4 + [DK * GS] * 4 + [GS] * 4 + [S] * 2)
        wv_p = [[parts_cut[4 * a + i].rearrange("p (k n) -> p k n", k=DK) for i in range(2)] for a in range(2)]
        wo_p = [[parts_cut[4 * a + 2 + i] for i in range(2)] for a in range(2)]
        wff2_p = parts_cut[8:10]
        tile_p = [[parts_cut[10 + 2 * p + i].rearrange("p (w k n) -> p w k n", w=2, k=DK) for i in range(2)] for p in range(2)]
        tile_flat = [parts_cut[10 + 2 * p:12 + 2 * p] for p in range(2)]
        h_p = [parts_cut[14 + i].rearrange("p (k n) -> p k n", k=DK) for i in range(2)]
        ctx_p = [parts_cut[16 + i].rearrange("p (k n) -> p k n", k=DK) for i in range(2)]
        qk_p = [[parts_cut[18 + 2 * p + i] for i in range(2)] for p in range(2)]
        o_p = parts_cut[22:24]

        def as_f32(ap):
            return ap.bitcast(F32)

        lead_loaded = sem("lead_loaded")
        l0w_loaded = sem("l0w_loaded")
        setup_small = sem("setup_small")
        setup_w = sem("setup_w")
        normw_loaded = sem("normw_loaded")
        zeroed = sem("zeroed")
        zero_tile = sem("zero_tile")
        const_set = sem("const_set")
        ident_set = sem("ident_set")
        tc_done = sem("tc_done")
        tc_copied = sem("tc_copied")
        f2_done = sem("f2_done")
        f2_copied = sem("f2_copied")
        f2_stored = sem("f2_stored")

        cond_nat = arena[0:B, 0:D]
        router_nat = arena[0:E, 256:256 + D]
        fac2_nat = arena[0:B, 512:512 + D]
        zero_rows = arena[:, 1024:2048]
        th = arena[:, 2048:2048 + GT * D].rearrange("p (t n) -> p t n", t=GT)
        l0w = arena[:, 3072:3584].rearrange("p (k n) -> p k n", k=DK)
        l0u = arena[:, 3584:4096].rearrange("p (k n) -> p k n", k=DK)
        nT = arena[:, 4096:5120].rearrange("p (k n) -> p k n", k=DK)
        fac2_row = sb("fac2_row", [1, GS])
        x_tiles = x_in.rearrange("b s d -> (b s) d").rearrange("(t p) d -> p t d", p=P)
        ctx_tiles = ctx_in.rearrange("b s d -> (b s) d").rearrange("(t p) d -> p t d", p=P)
        x3_tiles = x3_dram.rearrange("(t p) d -> p t d", p=P)
        out_tiles = out.rearrange("b s d -> (b s) d").rearrange("(t p) d -> p t d", p=P)
        ZERO_ROWS = P * 1024 // D
        ZERO_DMAS = -(-TRASH // ZERO_ROWS)

        def kd(w):
            return w.rearrange("(k p) n -> p k n", p=P)

        x_loaded = [sem("x_loaded0"), sem("x_loaded1")]
        ctx_loaded = sem("ctx_loaded")
        row_loaded = sem("row_loaded")
        var_ready = sem("var_ready")
        rstd_ready = sem("rstd_ready")
        dve_own = sem("dve_own")
        hat_ready = sem("hat_ready")
        tr_done = sem("tr_done")
        hT_dve = sem("hT_dve")
        hT_act = sem("hT_act")
        fac_done = sem("fac_done")
        tanh_ready = sem("tanh_ready")
        s_done = sem("s_done")
        xbuf = [xg, z]

        def layer_norm_stats(dve, tiles, src, own, own_sem, var_sem):
            r = slice(tiles[0], tiles[-1] + 1)
            for t in tiles:
                dve.bn_stats(stats[:, t, :], src(t)).then_inc(own_sem, 1)
            dve.wait_ge(own_sem, own.next(len(tiles)))
            dve.tensor_tensor(both[:, r, :], stats[:, r, 1:3], stats[:, r, 4:6], ALU.add)
            dve.tensor_tensor(mdiff[:, r], stats[:, r, 1], stats[:, r, 4], ALU.subtract).then_inc(own_sem, 1)
            dve.wait_ge(own_sem, own.next())
            dve.tensor_scalar(mean[:, r], both[:, r, 0], 0.5, None, ALU.mult)
            dve.tensor_scalar(veps[:, r], both[:, r, 1], 1.0 / D, EPS, ALU.mult, ALU.add)
            dve.scalar_tensor_tensor(mdiff2[:, r], mdiff[:, r], 0.25, mdiff[:, r], ALU.mult,
                                     ALU.mult).then_inc(own_sem, 1)
            dve.wait_ge(own_sem, own.next())
            dve.tensor_tensor(veps[:, r], veps[:, r], mdiff2[:, r], ALU.add).then_inc(var_sem, 1)

        def layer_norm_apply(dve, tiles, src, dst, rs, rstd_sem, hat_sem):
            dve.wait_ge(rstd_sem, rs.next())
            for t in tiles:
                dve.tensor_scalar(dst(t), src(t), mean[:, t:t + 1], rstd[:, t:t + 1], ALU.subtract,
                                  ALU.mult).then_inc(hat_sem, 1)

        ALL = range(GT)

        with nc.Block() as block:
            @block.sync
            def _(sp):
                sp.dma_start(xg[:, :, :], x_tiles[:, 0:GT, :]).then_inc(x_loaded[0], 16)
                sp.dma_start(cond_nat, cond_in).then_inc(lead_loaded, 16)
                sp.dma_start(router_nat, router_w).then_inc(lead_loaded, 16)
                sp.dma_start(l0u, kd(L0U)).then_inc(lead_loaded, 16)
                sp.dma_start(l0w, kd(L0W)).then_inc(l0w_loaded, 16)
                sp.dma_start(ctx_nat[:, :, :], ctx_tiles[:, 0:GT, :]).then_inc(ctx_loaded, 16)
                sp.dma_start(z[:, :, :], x_tiles[:, GT:2 * GT, :]).then_inc(x_loaded[1], 16)
                sp.wait_ge(f2_copied, 1)
                sp.dma_start(fac2_dram, fac2_nat).then_inc(f2_stored, 16)
                sp.wait_ge(f2_stored, 16)
                rows = fac2_dram.rearrange("(a b) n -> a (b n)", a=1)
                sp.dma_start(fac2_row[:, :], rows[:, 0:GS]).then_inc(row_loaded, 16)
                mine = []
                hr, fac, sd = Tally(mine), Tally(mine), Tally(mine)

                def ahead(g, p, x_too):
                    sp.wait_ge(hat_ready, hr.next(GT))
                    if x_too:
                        sp.dma_start(xbuf[p][:, :, :], x_tiles[:, bass.ds(GT * (g + 2), GT), :]).then_inc(x_loaded[p], 16)
                    sp.wait_ge(fac_done, fac.next(2))
                    sp.dma_start(fac2_row[:, :], rows[:, bass.ds(GS * (g + 1), GS)]).then_inc(row_loaded, 16)
                    sp.wait_ge(s_done, sd.next(GB))
                    sp.dma_start(ctx_nat[:, :, :], ctx_tiles[:, bass.ds(GT * (g + 1), GT), :]).then_inc(ctx_loaded, 16)
                with repeat(sp, G // 2 - 1, mine, {hr: 2 * GT, fac: 4, sd: 2 * GB}) as i:
                    ahead(2 * i, 0, True)
                    ahead(2 * i + 1, 1, True)
                ahead(G - 2, 0, False)

            @block.gpsimd
            def _(pool):
                pool.memset(ident[:, :], 0.0).then_inc(const_set, 1)
                pool.memset(ones[:, :], 1.0).then_inc(const_set, 1)
                pool.memset(minus_half[:, :], -0.5).then_inc(const_set, 1)
                pool.memset(upper[:, :], 1.0).then_inc(const_set, 1)
                pool.wait_ge(const_set, 4)
                pool.affine_select(out=ident[:, :], in_=ident[:, :], compare_op=ALU.not_equal, fill=1.0, base=0,
                                   pattern=[[-1, P]], channel_multiplier=1).then_inc(ident_set, 1)
                pool.affine_select(out=upper[:, :], in_=upper[:, :], compare_op=ALU.is_gt, fill=0.0, base=0,
                                   pattern=[[1, P]], channel_multiplier=-1).then_inc(ident_set, 1)
                pool.memset(zero_rows, 0.0).then_inc(zero_tile, 1)
                mine = []
                v = Tally(mine)
                with repeat(pool, G, mine, {v: 1}) as g:
                    pool.wait_ge(var_ready, v.next())
                    pool.tensor_tensor(rstd[:, :], veps[:, :], minus_half[:, :], ALU.pow).then_inc(rstd_ready, 1)

            @block.scalar
            def _(act):
                mine = []
                tr, fac, sd = Tally(mine), Tally(mine), Tally(mine)

                def turned():
                    act.wait_ge(tr_done, tr.next(2))
                    act.activation(nT[:, 1, :], bank[1][:, :], ACT.Copy).then_inc(hT_act, 1)

                def scores(g, more):
                    for j in range(2):
                        act.wait_ge(fac_done, fac.next())
                        act.activation(th[:, 2 * j:2 * j + 2, :], bank[2 + j][:, :], ACT.Tanh).then_inc(tanh_ready, 1)
                    if more:
                        turned()
                    for b in range(GB):
                        act.wait_ge(s_done, sd.next())
                        act.activation(attn[:, bass.ds((GT * g + b * DK) * D, DK * D)], bank[4 + b][:, :], ACT.Copy)
                turned()
                act.wait_ge(zero_tile, 1)
                act.wait_ge(row_loaded, 16)
                for i in range(ZERO_DMAS):
                    n = min(ZERO_ROWS, TRASH - i * ZERO_ROWS)
                    act.dma_start(disp[i * ZERO_ROWS:i * ZERO_ROWS + n, :].rearrange("(p r) d -> p (r d)", p=P),
                                  zero_rows[:, 0:n * D // P]).then_inc(zeroed, 16)
                with repeat(act, G - 1, mine, {tr: 2, fac: 2, sd: 2}) as g:
                    scores(g, True)
                scores(G - 1, False)
                act.wait_ge(zeroed, 16 * ZERO_DMAS)

            @block.tensor
            def _(pe):
                pe.wait_ge(ident_set, 2)
                pe.wait_ge(lead_loaded, 16 * 3)
                for k in range(DK):
                    pe.transpose(bank[0][:, k * B:(k + 1) * B], cond_nat[:, k * P:(k + 1) * P], ident[0:B, 0:B])
                for k in range(DK):
                    last = pe.transpose(bank[0][:, 64 + k * E:64 + (k + 1) * E], router_nat[:, k * P:(k + 1) * P],
                                        ident[0:E, 0:E])
                last.then_inc(tc_done, 1)
                pe.wait_ge(tc_copied, 2)
                for k in range(DK):
                    last = pe.matmul(bank[7][0:B, 0:D], condT[:, k, :], l0u[:, k, :], start=(k == 0), stop=(k == DK - 1))
                last.then_inc(f2_done, 1)
                mine = []
                hr, hd, ha, cl, tn, rl = (Tally(mine) for _ in range(6))
                pe.wait_ge(l0w_loaded, 16)
                pe.wait_ge(ident_set, 2)

                def turn():
                    pe.wait_ge(hat_ready, hr.next(GT))
                    for k in range(DK):
                        for t in range(GT):
                            last = pe.transpose(bank[k][:, t * P:(t + 1) * P], hat[:, t, k * P:(k + 1) * P], ident[:, :])
                        last.then_inc(tr_done, 1)

                def scores(more):
                    pe.wait_ge(hT_dve, hd.next())
                    pe.wait_ge(hT_act, ha.next())
                    pe.wait_ge(row_loaded, rl.next(16))
                    for t in range(GT):
                        o = bank[2 + t // 2][:, (t % 2) * D:(t % 2 + 1) * D]
                        for k in range(DK):
                            pe.matmul(o, nT[:, k, t * P:(t + 1) * P], l0w[:, k, :], start=(k == 0), stop=False)
                        last = pe.matmul(o, ones[0:1, :], fac2_row[0:1, (t // BT) * D:(t // BT + 1) * D],
                                         start=False, stop=True)
                        if t % 2:
                            last.then_inc(fac_done, 1)
                    if more:
                        turn()
                    pe.wait_ge(ctx_loaded, cl.next(16))
                    for b in range(GB):
                        pe.wait_ge(tanh_ready, tn.next())
                        for k in range(DK):
                            for t in range(BT):
                                last = pe.matmul(bank[4 + b][:, k * D:(k + 1) * D],
                                                 ctx_nat[:, b * BT + t, k * P:(k + 1) * P], th[:, b * BT + t, :],
                                                 start=(t == 0), stop=(t == BT - 1))
                        last.then_inc(s_done, 1)
                turn()
                with repeat(pe, G - 1, mine, {hr: GT, hd: 1, ha: 1, cl: 16, tn: 2, rl: 16}) as g:
                    scores(True)
                scores(False)

            @block.vector
            def _(dve):
                mine = []
                own, rs, tr, x0, x1 = (Tally(mine) for _ in range(5))
                xl = (x0, x1)

                def group(p):
                    dve.wait_ge(x_loaded[p], xl[p].next(16))
                    layer_norm_stats(dve, ALL, lambda t: xbuf[p][:, t, :], own, dve_own, var_ready)
                    layer_norm_apply(dve, ALL, lambda t: xbuf[p][:, t, :], lambda t: hat[:, t, :], rs, rstd_ready, hat_ready)

                def turned():
                    dve.wait_ge(tr_done, tr.next(2))
                    dve.tensor_copy(nT[:, 0, :], bank[0][:, :]).then_inc(hT_dve, 1)

                def pair():
                    group(0)
                    turned()
                    group(1)
                    turned()
                group(0)
                dve.wait_ge(tc_done, 1)
                dve.tensor_copy(condT[:, :, :], bank[0][:, 0:DK * B].rearrange("p (k b) -> p k b", k=DK)).then_inc(tc_copied, 1)
                dve.tensor_copy(routerT[:, :, :], bank[0][:, 64:64 + DK * E].rearrange("p (k e) -> p k e", k=DK)).then_inc(tc_copied, 1)
                dve.wait_ge(f2_done, 1)
                dve.tensor_copy(fac2_nat, bank[7][0:B, 0:D]).then_inc(f2_copied, 1)
                turned()
                group(1)
                turned()
                with repeat(dve, G // 2 - 1, mine, {own: 2 * (GT + 2), rs: 2, tr: 4, x0: 16, x1: 16}) as i:
                    pair()

        max_ready = sem("max_ready")
        shifted = sem("shifted")
        exps_ready = sem("exps_ready")
        emb_done = sem("emb_done")
        raw_in = [sem(f"raw_in{i}") for i in range(4)]
        raw_hi = sem("raw_hi")
        raw_lo = sem("raw_lo")
        colmax = arena[:, 0:DK * D].rearrange("p (k e) -> p k e", k=DK)
        colsum = arena[:, 512:512 + DK * D].rearrange("p (k e) -> p k e", k=DK)
        colrec = arena[:, 1024:1024 + DK * D].rearrange("p (k e) -> p k e", k=DK)
        normw = [arena[:, 1536 + n * 1024:1536 + (n + 1) * 1024].rearrange("p (k n) -> p k n", k=DK) for n in range(3)]
        by_dtile = attn[:, :].rearrange("p (b k e) -> p k b e", b=B, k=DK)
        raw = [t[:, :, :].rearrange("p t d -> p (t d)") for t in (xg, z, hat, ctx_nat)]
        pieces = []
        for a, (wv, wo) in enumerate(((wv1, wo1), (wv2, wo2))):
            pieces += [(wv[k * P:(k + 1) * P, :], wv_p[a][0][:, k, :], wv_p[a][1][:, k, :]) for k in range(DK)]
            pieces += [(wo[j * 512:(j + 1) * 512, :].rearrange("(h p) n -> p h n", p=P),
                        wo_p[a][0][:, j * 1024:(j + 1) * 1024], wo_p[a][1][:, j * 1024:(j + 1) * 1024]) for j in range(2)]
        pieces += [(ffw2[j * 512:(j + 1) * 512, :].rearrange("(h p) n -> p h n", p=P),
                    wff2_p[0][:, j * 1024:(j + 1) * 1024], wff2_p[1][:, j * 1024:(j + 1) * 1024]) for j in range(2)]
        SMALL = 2 * 5 + 3 + 4 + 1

        with nc.Block() as block:
            @block.sync
            def _(sp):
                for n, w in enumerate((n1w, n2w, n3w)):
                    sp.dma_start(normw[n], kd(w)).then_inc(normw_loaded, 16)
                for j, (src, _, _) in enumerate(pieces):
                    if j >= 4:
                        sp.wait_ge(raw_lo, j - 3)
                    dst = raw[j % 4] if len(src.shape) == 2 else raw[j % 4].rearrange("p (h n) -> p h n", h=4)
                    sp.dma_start(dst, src).then_inc(raw_in[j % 4], 16)

            @block.gpsimd
            def _(pool):
                for j, (_, hi, lo) in enumerate(pieces):
                    pool.wait_ge(raw_hi, j + 1)
                    pool.tensor_tensor(lo, raw[j % 4], as_f32(hi), ALU.subtract).then_inc(raw_lo, 1)

            @block.tensor
            def _(pe):
                pe.wait_ge(normw_loaded, 16 * 3)
                for n in range(3):
                    for c in range(2 * DK):
                        for k in range(DK):
                            o = (n * 2 * DK + c) * B
                            last = pe.matmul(bank[6][:, o:o + B], normw[n][:, k, c * P:(c + 1) * P], condT[:, k, :],
                                             start=(k == 0), stop=(k == DK - 1))
                last.then_inc(emb_done, 1)

            @block.vector
            def _(dve):
                for k in range(DK):
                    dve.tensor_reduce(colmax[:, k, :], by_dtile[:, k].rearrange("p b e -> p e b"), AX.X,
                                      ALU.max).then_inc(max_ready, 1)
                for k in range(DK):
                    dve.wait_ge(max_ready, k + 1)
                    dve.tensor_tensor(by_dtile[:, k], by_dtile[:, k],
                                      colmax[:, k, :].unsqueeze(1).to_broadcast([P, B, D]),
                                      ALU.subtract).then_inc(shifted, 1)
                for k in range(DK):
                    dve.wait_ge(exps_ready, k + 1)
                    dve.tensor_reduce(colsum[:, k, :], by_dtile[:, k].rearrange("p b e -> p e b"), AX.X,
                                      ALU.add).then_inc(dve_own, 1)
                    dve.wait_ge(dve_own, G * (GT + 2) + 2 * k + 1)
                    dve.reciprocal(colrec[:, k, :], colsum[:, k, :]).then_inc(dve_own, 1)
                    dve.wait_ge(dve_own, G * (GT + 2) + 2 * k + 2)
                    dve.tensor_tensor(by_dtile[:, k], by_dtile[:, k],
                                      colrec[:, k, :].unsqueeze(1).to_broadcast([P, B, D]),
                                      ALU.mult)
                dve.wait_ge(emb_done, 1)
                dve.wait_ge(setup_small, 16 * SMALL)
                for n in range(3):
                    for c in range(2 * DK):
                        o = (n * 2 * DK + c) * B
                        dve.tensor_scalar(emb[:, n, c, :], bank[6][:, o:o + B], norm_b[:, n, c:c + 1],
                                          1.0 if c < DK else 0.0, ALU.add, ALU.add)

            @block.scalar
            def _(act):
                for n, v in enumerate((bout, bo1, bo2, ffb2)):
                    act.dma_start(bias_rows[0:1, n, :], v.rearrange("(a n) -> a n", a=1)).then_inc(setup_small, 16)
                with nc.allow_non_contiguous_dma("short bias columns"):
                    for n, v in enumerate((n1b, n2b, n3b)):
                        act.dma_start(norm_b[:, n, :], v.rearrange("(c p) -> p c", p=P)).then_inc(setup_small, 16)
                    act.dma_start(ffb1_sb[:, :], ffb1.rearrange("(c p) -> p c", p=P)).then_inc(setup_small, 16)
                for half in range(2):
                    rows = slice(half * M, (half + 1) * M)
                    act.dma_start(small_w[rows, 0, :], W1).then_inc(setup_small, 16)
                    act.dma_start(small_w[rows, 1, :], W2).then_inc(setup_small, 16)
                    act.dma_start(b1_sb[rows, :], b1).then_inc(setup_small, 16)
                    act.dma_start(bin2[rows, 0:1], bin_.rearrange("(m a) -> m a", a=1)).then_inc(setup_small, 16)
                    act.dma_start(bin2[rows, 1:2], b2.rearrange("(m a) -> m a", a=1)).then_inc(setup_small, 16)
                    act.dma_start(wout_sb[rows, :], Wout).then_inc(setup_w, 16)
                act.dma_start(win_sb[:, :, :], kd(Win)).then_inc(setup_w, 16)

                def cut(j):
                    act.wait_ge(raw_in[j % 4], 16 * (j // 4 + 1))
                    act.activation(pieces[j][1], raw[j % 4], ACT.Copy).then_inc(raw_hi, 1)
                for j in range(4):
                    cut(j)
                for k in range(DK):
                    act.wait_ge(shifted, k + 1)
                    act.activation(by_dtile[:, k], by_dtile[:, k], ACT.Exp).then_inc(exps_ready, 1)
                for j in range(4, len(pieces)):
                    cut(j)
                act.wait_ge(setup_w, 16 * 3)


        xB_loaded = sem("xB_loaded")
        ctxB_loaded = sem("ctxB_loaded")
        x_taken = sem("x_taken")
        rawt_loaded = [sem("rawt_loaded0"), sem("rawt_loaded1")]
        tile_hi = sem("tile_hi")
        tile_ready = [sem("tile_ready0"), sem("tile_ready1")]
        ctx_hi = sem("ctx_hi")
        ctx_cut = sem("ctx_cut")
        trB_done = sem("trB_done")
        turned_in = sem("turned_in")
        x1_done = sem("x1_done")
        x2_done = sem("x2_done")
        varB_ready = sem("varB_ready")
        rstdB_ready = sem("rstdB_ready")
        hatB_ready = sem("hatB_ready")
        ln_own = sem("ln_own")
        z_own = sem("z_own")
        low_done = sem("low_done")
        low_ready = sem("low_ready")
        relu_ready = sem("relu_ready")
        relu_used = sem("relu_used")
        mlp_ready = sem("mlp_ready")
        lane_turned = sem("lane_turned")
        modulated = sem("modulated")
        h_hi_ready = sem("h_hi_ready")
        h_ready = sem("h_ready")
        qk_done = sem("qk_done")
        qk_hi = sem("qk_hi")
        qk_ready = sem("qk_ready")
        v_done = sem("v_done")
        v_ready = sem("v_ready")
        scores_done = sem("scores_done")
        negmax_ready = sem("negmax_ready")
        exp_ready = sem("exp_ready")
        rrec_ready = sem("rrec_ready")
        probs_ready = sem("probs_ready")
        pT_done = sem("pT_done")
        pT_dve = sem("pT_dve")
        pT_act = sem("pT_act")
        o_done = sem("o_done")
        o_hi_ready = sem("o_hi_ready")
        o_ready = sem("o_ready")
        y_done = sem("y_done")
        glu_done = sem("glu_done")
        gelu_ready = sem("gelu_ready")
        gated_sum = sem("gated_sum")
        gated_hi = sem("gated_hi")
        gated_ready = sem("gated_ready")
        x3_ready = sem("x3_ready")
        x3_stored = sem("x3_stored")
        nrm_saved = sem("nrm_saved")
        z_started = sem("z_started")
        logits_done = sem("logits_done")

        two = range(2)
        cut_b = carve(arena, [GS] * 8 + [2 * DK * P] * 2)
        v_at = [v.rearrange("p (t n) -> p t n", t=BT) for v in cut_b[2:4]]
        probs = [v.rearrange("p (t k) -> p t k", t=BT) for v in cut_b[4:6]]
        pT = [v.rearrange("p (k q) -> p k q", k=BT) for v in cut_b[6:8]]
        rawt = cut_b[8:10]
        nTB = arena[:, 1024:2048].rearrange("p (k n) -> p k n", k=DK)
        lowT, acc, mlpT = arena[:, 1024:1280], [arena[:, 1280:1536], arena[:, 1536:1792]], arena[:, 1792:2048]
        relus = [arena[:, 2048 + j * S:2048 + (j + 1) * S] for j in range(4)]
        ctxT = arena[:, 3072:4096].rearrange("p (k n) -> p k n", k=DK)
        nT3 = ctxT
        RELU_STEPS = {1: range(0, 4), 2: range(4, 8), 3: range(8, 12), 4: range(12, INNER)}
        gelu = cut_b[0:2]
        gated_p = [parts_cut[18 + 2 * p:20 + 2 * p] for p in two]
        wq_t, wk_t = [kd(w) for w in (wq1, wq2)], [kd(w) for w in (wk1, wk2)]
        w1_t = kd(ffw1)
        TILES = 2 * HP + NF
        SLOTS_A = 2 * HP
        V_A = SLOTS_A - 1
        V_PIECES = ((1, 0), (1, 1), (0, 0), (0, 1))
        PASSES = ((0, 0), (0, 1), (1, 0))

        SCALE = float(DH) ** -0.5

        def flat(t):
            return t[:, :, :].rearrange("p t d -> p (t d)")

        with nc.Block() as block:
            @block.sync
            def _(sp):
                mine = []
                used = [Tally(mine), Tally(mine)]
                xt, ns = Tally(mine), Tally(mine)

                def two_tiles(i, first, second):
                    for p in two:
                        sp.wait_ge(tile_ready[p], used[p].next())
                        dst = rawt[p].rearrange("p (w k n) -> p w k n", w=2, k=DK)
                        sp.dma_start(dst[:, 0], first(2 * i + p)).then_inc(rawt_loaded[p], 16)
                        sp.dma_start(dst[:, 1], second(2 * i + p)).then_inc(rawt_loaded[p], 16)

                def load_ctx(g):
                    sp.dma_start(ctx_nat[:, :, :], ctx_tiles[:, bass.ds(GT * g, GT), :]).then_inc(ctxB_loaded, 16)

                def load_x(g):
                    sp.dma_start(xg[:, :, :], x_tiles[:, bass.ds(GT * g, GT), :]).then_inc(xB_loaded, 16)

                def attention_tiles(a):
                    with repeat(sp, HP // 2, mine, {used[0]: 1, used[1]: 1}) as i:
                        two_tiles(i, lambda h: wq_t[a][:, :, bass.ds(h * P, P)],
                                  lambda h: wk_t[a][:, :, bass.ds(h * P, P)])

                def mlp_tiles(i):
                    two_tiles(i, lambda f: w1_t[:, :, bass.ds(f * P, P)], lambda f: w1_t[:, :, bass.ds(f * P + DFF, P)])

                def body(g, more):
                    attention_tiles(0)
                    if more:
                        sp.wait_ge(nrm_saved, ns.next())
                        load_ctx(g + 1)
                    attention_tiles(1)
                    mlp_tiles(0)
                    mlp_tiles(1)
                    if more:
                        sp.wait_ge(x_taken, xt.next())
                        load_x(g + 1)
                    mlp_tiles(2)
                    mlp_tiles(3)
                load_x(0)
                load_ctx(0)
                with repeat(sp, G - 1, mine, {used[0]: TILES // 2, used[1]: TILES // 2, xt: 1, ns: 1}) as g:
                    body(g, True)
                body(G - 1, False)

            @block.gpsimd
            def _(pool):
                mine = []
                var, hr, ld0, ld1, qd, gl, th_, ch, st = (Tally(mine) for _ in range(9))
                ld = (ld0, ld1)
                pool.sem_inc(nrm_saved, 1)
                pool.sem_inc(tile_ready[0], 1)
                pool.sem_inc(tile_ready[1], 1)

                def cut(p, attention):
                    pool.wait_ge(rawt_loaded[p], ld[p].next(32))
                    if attention:
                        pool.wait_ge(qk_done, qd.next(1 if p else 3))
                    else:
                        pool.wait_ge(glu_done, gl.next())
                    hi, lo = tile_flat[p]
                    pool.tensor_tensor(hi, rawt[p], ones[:, 0:1].to_broadcast([P, 2 * DK * P]), ALU.mult).then_inc(tile_hi, 1)
                    pool.wait_ge(tile_hi, th_.next())
                    pool.tensor_tensor(lo, rawt[p], as_f32(hi), ALU.subtract).then_inc(tile_ready[p], 1)

                def power(r):
                    pool.wait_ge(varB_ready, var.next())
                    pool.tensor_tensor(rstd[:, r], veps[:, r], minus_half[:, r], ALU.pow).then_inc(rstdB_ready, 1)

                def lane_powers():
                    for l in two:
                        power(slice(BT * l, BT * (l + 1)))

                def ctx_lo(k):
                    pool.wait_ge(ctx_hi, ch.next())
                    pool.tensor_tensor(ctx_p[1][:, k, :], ctxT[:, k, :], as_f32(ctx_p[0][:, k, :]),
                                       ALU.subtract).then_inc(ctx_cut, 1)
                every = slice(0, GT)

                def save_x3(g):
                    pool.wait_ge(hatB_ready, hr.next(GT))
                    pool.tensor_tensor(attn[:, bass.ds(GT * D * g, GT * D)], flat(ctx_nat),
                                       ones[:, 0:1].to_broadcast([P, GT * D]), ALU.mult).then_inc(nrm_saved, 1)

                def start_z():
                    pool.tensor_tensor(flat(z), flat(hat), ones[:, 0:1].to_broadcast([P, GT * D]),
                                       ALU.mult).then_inc(z_started, 1)

                def pairs_of_tiles(attention):
                    per = {ld0: 32, ld1: 32, th_: 2, **({qd: 4} if attention else {gl: 2})}
                    with repeat(pool, HP // 2 - 1, mine, per) as i:
                        cut(0, attention)
                        cut(1, attention)

                def body(g, more):
                    for a in two:
                        pairs_of_tiles(True)
                        cut(0, True)
                        cut(1, True)
                        lane_powers()
                    pool.wait_ge(hatB_ready, hr.next(2 * GT))
                    pool.tensor_tensor(flat(z), flat(z), flat(xg), ALU.add).then_inc(x_taken, 1)
                    if not more:
                        pairs_of_tiles(False)
                        power(every)
                        save_x3(g)
                        return
                    ctx_lo(0)
                    power(every)
                    ctx_lo(1)
                    for f in range(2, NF):
                        cut(f % 2, False)
                    power(every)
                    cut(0, False)
                    cut(1, False)
                    lane_powers()
                    power(every)
                    hr.next(3 * GT)
                    save_x3(g)
                    pool.wait_ge(x3_stored, st.next(16))
                    start_z()

                cut(0, False)
                cut(1, False)
                power(every)
                power(every)
                lane_powers()
                ctx_lo(0)
                ctx_lo(1)
                pool.wait_ge(hatB_ready, hr.next(3 * GT))
                start_z()
                per = {var: 9, hr: 6 * GT, ld0: 16 * TILES, ld1: 16 * TILES, qd: 4 * HP, gl: NF, th_: TILES, ch: 2, st: 16}
                with repeat(pool, G - 1, mine, per) as g:
                    body(g, True)
                body(G - 1, False)

            @block.scalar
            def _(act):
                mine = []
                tr, cx, low, own, used, md, qd, vd, nm, pt, od, glu, gs, x3 = (Tally(mine) for _ in range(14))
                glu.next(2)

                def turned(dst, banks):
                    act.wait_ge(trB_done, tr.next(2))
                    for k in range(DK):
                        act.activation(dst[:, k, :], bank[banks[k]][:, :], ACT.Copy).then_inc(turned_in, 1)
                    cx.next(DK)

                def turned_ctx(banks):
                    turned(ctxT, banks)
                    for k in range(DK):
                        act.wait_ge(turned_in, cx.now() - (DK - 1 - k))
                        act.activation(ctx_p[0][:, k, :], ctxT[:, k, :], ACT.Copy).then_inc(ctx_hi, 1)

                def save_low():
                    act.wait_ge(low_done, low.next())
                    act.activation(lowT, bank[4][:, 0:S], ACT.Identity, bias=bin2[:, 0:1]).then_inc(low_ready, 1)
                    act.wait_ge(low_ready, own.next())

                def relus_of(js):
                    for j in js:
                        if j >= 4:
                            act.wait_ge(relu_used, used.next())
                        act.activation(relus[j % 4], lowT, ACT.Relu, scale=small_w[:, 0, j:j + 1],
                                       bias=b1_sb[:, j:j + 1]).then_inc(relu_ready, 1)
                    if INNER - 1 in js:
                        used.next(4)

                def lane_hi(l, b):
                    act.wait_ge(modulated, md.next())
                    act.activation(h_p[0][:, :, l * S:(l + 1) * S], bank[b][:, :].rearrange("p (k n) -> p k n", k=DK),
                                   ACT.Copy).then_inc(h_hi_ready, 1)

                def save_qk(s):
                    act.wait_ge(qk_done, qd.next())
                    act.activation(qk_p[s % 2][0][:, 0:S], bank[4][:, 0:S], ACT.Copy, scale=SCALE)
                    act.activation(qk_p[s % 2][0][:, S:2 * S], bank[4][:, S:2 * S], ACT.Copy).then_inc(qk_hi, 1)

                def save_v(l, t):
                    act.wait_ge(v_done, vd.next())
                    act.activation(v_at[l][:, t, :], bank[5][:, 0:2 * P], ACT.Copy).then_inc(v_ready, 1)

                def exps(u):
                    act.wait_ge(negmax_ready, nm.next())
                    for t in range(BT):
                        last = act.activation(probs[u][:, t, :], bank[u][:, t * S:(t + 1) * S], ACT.Exp,
                                              bias=nmx[:, u, t:t + 1], accum_out=rsum[:, u, t:t + 1])
                    last.then_inc(exp_ready, 1)

                def slot(s, next1, next2, next_v):
                    act.wait_ge(pT_done, pt.next(2))
                    act.activation(pT[1][:, :, :], bank[3][:, :].rearrange("p (k q) -> p k q", k=BT),
                                   ACT.Copy).then_inc(pT_act, 1)
                    if next1:
                        exps(0)
                    act.wait_ge(o_done, od.next())
                    act.activation(o_p[0], bank[5][:, S:2 * S], ACT.Copy).then_inc(o_hi_ready, 1)
                    if next1:
                        exps(1)
                    if next2:
                        save_qk(s)
                    if next_v:
                        save_v(*V_PIECES[s])

                def begin(a, x3_too):
                    save_qk(0)
                    act.wait_ge(v_done, vd.next())
                    act.activation(v_at[0][:, :, :], bank[5][:, :].rearrange("p (t n) -> p t n", t=BT),
                                   ACT.Copy).then_inc(v_ready, 1)
                    if a == 0:
                        lane_hi(1, 7)
                    save_qk(1)
                    exps(0)
                    exps(1)
                    if a == 1:
                        lane_hi(1, 3)
                    if x3_too:
                        turned(nT3, (2, 3))

                def slots():
                    with repeat(act, HP // 2 - 1, mine, {qd: 4, vd: 4, nm: 8, pt: 8, od: 4}) as i:
                        for s in range(4):
                            slot(s, True, True, True)
                    for s in range(4):
                        slot(s, s < 3, s < 2, s < 2)

                def body(g, more):
                    slots()
                    lane_hi(0, 6)
                    begin(1, False)
                    slots()
                    lane_hi(0, 6)
                    if more:
                        turned_ctx((0, 1))
                    lane_hi(1, 7)
                    for f in range(NF):
                        p = f % 2
                        act.wait_ge(glu_done, glu.next())
                        act.activation(gelu[p], bank[2 * p + 1][:, :], ACT.Gelu,
                                       bias=ffb1_sb[:, f + NF:f + NF + 1]).then_inc(gelu_ready, 1)
                        act.wait_ge(gated_sum, gs.next())
                        act.activation(gated_p[p][0], bank[2 * p][:, :], ACT.Copy).then_inc(gated_hi, 1)
                        if more:
                            if f == 0:
                                turned(nTB, (4, 5))
                            if f == 1:
                                save_low()
                            if f in RELU_STEPS:
                                relus_of(RELU_STEPS[f])
                    if more:
                        lane_hi(0, 4)
                    act.wait_ge(x3_ready, x3.next())
                    act.dma_start(x3_tiles[:, bass.ds(GT * g, GT), :], z[:, :, :]).then_inc(x3_stored, 16)
                    if more:
                        begin(0, True)
                    else:
                        turned(nT3, (2, 3))

                turned_ctx((0, 1))
                turned(nTB, (4, 5))
                save_low()
                relus_of(range(INNER))
                lane_hi(0, 4)
                begin(0, False)
                per = {tr: 6, cx: 6, low: 1, own: 1, used: INNER, md: 6, qd: 2 * SLOTS_A, vd: 2 * V_A, nm: 4 * SLOTS_A,
                       pt: 4 * SLOTS_A, od: 2 * SLOTS_A, glu: NF, gs: NF, x3: 1}
                with repeat(act, G - 1, mine, per) as g:
                    body(g, True)
                body(G - 1, False)
                act.wait_ge(x3_stored, 16 * G)

            @block.tensor
            def _(pe):
                mine = []
                cl, ti, hr, mr, hc, cc, qr, vr, pr, pd, pa, oy, gd, t0, t1, xr = (Tally(mine) for _ in range(16))
                tl = (t0, t1)
                t0.next(), t1.next()
                pe.sem_inc(glu_done, 2)

                def turn(src, banks):
                    for k in range(DK):
                        for t in range(GT):
                            last = pe.transpose(bank[banks[k]][:, t * P:(t + 1) * P], src[:, t, k * P:(k + 1) * P], ident[:, :])
                        last.then_inc(trB_done, 1)

                def turn_ctx():
                    pe.wait_ge(ctxB_loaded, cl.next(16))
                    turn(ctx_nat, (0, 1))

                def l0_out(g):
                    pe.wait_ge(turned_in, ti.next(DK))
                    for t in range(GT):
                        for k in range(DK):
                            last = pe.matmul(bank[4 + t // 2][:, (t % 2) * D:(t % 2 + 1) * D],
                                             ctxT[:, k, t * P:(t + 1) * P],
                                             attn[:, bass.ds(((GB * g + t // BT) * DK + k) * D, D)],
                                             start=(k == 0), stop=(k == DK - 1))
                        if t % 2:
                            last.then_inc(x1_done, 1)

                def turn_x1():
                    pe.wait_ge(hatB_ready, hr.next(GT))
                    turn(ctx_nat, (4, 5))

                def narrow_low():
                    pe.wait_ge(turned_in, ti.next(DK))
                    for b in range(GB):
                        for k in range(DK):
                            last = pe.matmul(bank[4][b * M:(b + 1) * M, 0:S], win_sb[:, k, :],
                                             nTB[:, k, b * S:(b + 1) * S], start=(k == 0), stop=(k == DK - 1))
                    last.then_inc(low_done, 1)

                def narrow_out():
                    bias_first(bank[5], 0)
                    pe.wait_ge(mlp_ready, mr.next())
                    bias_first(bank[4], 0)
                    for t in range(GT):
                        b = t // BT
                        last = pe.matmul(bank[4 + t // 2][:, (t % 2) * D:(t % 2 + 1) * D],
                                         mlpT[b * M:(b + 1) * M, (t % BT) * P:(t % BT + 1) * P],
                                         wout_sb[b * M:(b + 1) * M, :], start=False, stop=t % 2 == 1,
                                         skip_group_check=True)
                        if t % 2:
                            last.then_inc(x2_done, 1)
                    hr.next(GT)

                def turn_lane(l, src, into):
                    pe.wait_ge(hatB_ready, hr.next(BT))
                    for k in range(DK):
                        for t in range(BT):
                            last = pe.transpose(bank[into][:, (k * BT + t) * P:(k * BT + t + 1) * P],
                                                src[:, l * BT + t, k * P:(k + 1) * P], ident[:, :])
                    last.then_inc(lane_turned, 1)

                def turn_x3():
                    pe.wait_ge(hatB_ready, hr.next(GT))
                    turn(ctx_nat, (2, 3))

                def route():
                    pe.wait_ge(turned_in, ti.next(DK))
                    for t in range(GT):
                        for k in range(DK):
                            last = pe.matmul(bank[3][:, t * E:(t + 1) * E], nT3[:, k, t * P:(t + 1) * P], routerT[:, k, :],
                                             start=(k == 0), stop=(k == DK - 1))
                    last.then_inc(logits_done, 1)

                def bias_first(y, n):
                    pe.matmul(y[:, :], ones[0:1, :], bias_rows[0:1, n, :].unsqueeze(1).to_broadcast([1, BT, D]),
                              start=True, stop=False, skip_group_check=True)

                def proj_qk(p, l, srck):
                    cols = slice(l * S, (l + 1) * S)
                    for w, src in ((0, h_p), (1, srck)):
                        for k in range(DK):
                            for n, (i, j) in enumerate(PASSES):
                                last = pe.matmul(bank[4][:, w * S:(w + 1) * S], tile_p[p][i][:, w, k, :],
                                                 src[j][:, k, cols], start=(k == 0 and n == 0),
                                                 stop=(k == DK - 1 and n == 2))
                    last.then_inc(qk_done, 1)

                def proj_v(a, pairs, l, t, o=0):
                    at = l * S + t * P
                    for k in range(DK):
                        for n, (i, j) in enumerate(PASSES):
                            last = pe.matmul(bank[5][:, o:o + 2 * P], keys[a][i][:, k, at:at + P],
                                             wv_p[a][j][:, k, bass.ds(pairs * 2 * P, 2 * P)],
                                             start=(k == 0 and n == 0), stop=(k == DK - 1 and n == 2))
                    return last

                def scores(s, u):
                    rows = slice(u * DH, (u + 1) * DH)
                    for t in range(BT):
                        for n, (i, j) in enumerate(PASSES):
                            last = pe.matmul(bank[u][:, t * S:(t + 1) * S], qk_p[s % 2][i][rows, t * P:(t + 1) * P],
                                             qk_p[s % 2][j][rows, S:2 * S], start=(n == 0), stop=(n == 2))
                    last.then_inc(scores_done, 1)

                def turn_probs(u):
                    pe.wait_ge(probs_ready, pr.next())
                    for k in range(BT):
                        for t in range(BT):
                            last = pe.transpose(bank[2 + u][:, k * S + t * P:k * S + (t + 1) * P],
                                                probs[u][:, t, k * P:(k + 1) * P], ident[:, :])
                    last.then_inc(pT_done, 1)

                def weigh(s, u):
                    l, o = s // 2, s % 2 * P + u * DH
                    for k in range(BT):
                        last = pe.matmul(bank[5][u * DH:(u + 1) * DH, S:2 * S], v_at[l][:, k, o:o + DH],
                                         pT[u][:, k, :], start=(k == 0), stop=(k == BT - 1))
                    if u:
                        last.then_inc(o_done, 1)

                def slot(a, i, s, last_round=False, ctx_too=False):
                    next1 = not (last_round and s == 3)
                    next2 = next_v = not (last_round and s >= 2)
                    turn_probs(0)
                    if next1:
                        pe.wait_ge(qk_ready, qr.next())
                        scores(s + 1, 0)
                    turn_probs(1)
                    if next1:
                        scores(s + 1, 1)
                    else:
                        turn_lane(0, hat, 6)
                        if ctx_too:
                            turn_ctx()
                    if next_v or s == 2:
                        pe.wait_ge(v_ready, vr.next())
                    pe.wait_ge(pT_dve, pd.next())
                    weigh(s, 0)
                    pe.wait_ge(pT_act, pa.next())
                    weigh(s, 1)
                    if next2:
                        if s >= 2:
                            pe.wait_ge(tile_ready[s % 2], tl[s % 2].next())
                        proj_qk(s % 2, 1 - s // 2, keys[a])
                    pe.wait_ge(o_ready, oy.next())
                    if next_v:
                        proj_v(a, i if s < 2 else i + 1, *V_PIECES[s]).then_inc(v_done, 1)
                    l, h = s // 2, 2 * i + s % 2
                    of_last_pair = not next1 or (last_round and s == 1)
                    for t in range(BT):
                        for n, (part, w) in enumerate(PASSES):
                            last = pe.matmul(bank[6 + l][:, t * D:(t + 1) * D], o_p[part][:, t * P:(t + 1) * P],
                                             wo_p[a][w][:, bass.ds(h * D, D)], start=False,
                                             stop=of_last_pair and t == BT - 1 and n == 2, skip_group_check=True)
                    if of_last_pair:
                        last.then_inc(y_done, 1)

                keys = (h_p, ctx_p)

                def begin(a, src, x3_too):
                    pe.wait_ge(h_ready, hc.next())
                    pe.wait_ge(tile_ready[0], tl[0].next())
                    proj_qk(0, 0, keys[a])
                    proj_v(a, 0, 0, 0)
                    proj_v(a, 0, 0, 1, 2 * P).then_inc(v_done, 1)
                    if x3_too:
                        pe.wait_ge(x3_ready, xr.next())
                    bias_first(bank[6], 1 + a)
                    if a == 0:
                        turn_lane(1, src, 7)
                    pe.wait_ge(qk_ready, qr.next())
                    pe.wait_ge(tile_ready[1], tl[1].next())
                    proj_qk(1, 0, keys[a])
                    scores(0, 0)
                    scores(0, 1)
                    if a == 1:
                        turn_lane(1, src, 3)
                    if a == 0:
                        pe.wait_ge(h_ready, hc.next())
                    else:
                        hc.next()
                    bias_first(bank[7], 1 + a)
                    if a == 0:
                        pe.wait_ge(ctx_cut, cc.next(DK))
                    if x3_too:
                        turn_x3()
                        route()

                def slots(a, ctx_too=False):
                    per_round = {qr: 4, vr: 4, pr: 8, pd: 4, pa: 4, oy: 4, t0: 1, t1: 1}
                    with repeat(pe, HP // 2 - 1, mine, per_round) as i:
                        for s in range(4):
                            slot(a, i, s)
                    for s in range(4):
                        slot(a, HP // 2 - 1, s, True, ctx_too)

                def up(p, first, tokens=S):
                    cols = slice(first, first + tokens)
                    for w in (1, 0):
                        for k in range(DK):
                            for n, (i, j) in enumerate(PASSES):
                                last = pe.matmul(bank[2 * p + w][:, cols], tile_p[p][i][:, w, k, :], h_p[j][:, k, cols],
                                                 start=(k == 0 and n == 0), stop=(k == DK - 1 and n == 2))
                    return last

                def down(f):
                    pe.wait_ge(gated_ready, gd.next())
                    for t in range(GT):
                        for n, (i, j) in enumerate(PASSES):
                            last = pe.matmul(bank[6 + t // 2][:, (t % 2) * D:(t % 2 + 1) * D],
                                             gated_p[f % 2][i][:, t * P:(t + 1) * P], wff2_p[j][:, f * D:(f + 1) * D],
                                             start=False, stop=f == NF - 1 and t % 2 == 1 and n == 2,
                                             skip_group_check=True)
                        if f == NF - 1 and t % 2:
                            last.then_inc(y_done, 1)

                def body(g, more):
                    slots(0)
                    begin(1, hat, False)
                    slots(1, more)
                    if more:
                        l0_out(g + 1)
                    pe.wait_ge(h_ready, hc.next())
                    bias_first(bank[6], 3)
                    pe.wait_ge(tile_ready[0], tl[0].next())
                    up(0, 0)
                    turn_lane(1, hat, 7)
                    pe.wait_ge(tile_ready[1], tl[1].next())
                    up(1, 0)
                    pe.wait_ge(h_ready, hc.next())
                    bias_first(bank[7], 3)
                    up(0, S).then_inc(glu_done, 1)
                    up(1, S).then_inc(glu_done, 1)
                    for f in range(NF):
                        if 0 < f < NF - 1:
                            pe.wait_ge(tile_ready[(f + 1) % 2], tl[(f + 1) % 2].next())
                            up((f + 1) % 2, 0, GS).then_inc(glu_done, 1)
                        if more:
                            if f == 1:
                                narrow_low()
                        down(f)
                        if more and f == 0:
                            turn_x1()
                        if more and f == 4:
                            narrow_out()
                    if more:
                        turn_lane(0, ctx_nat, 4)
                        begin(0, ctx_nat, True)
                    else:
                        turn_x3()
                        route()

                turn_ctx()
                l0_out(0)
                turn_x1()
                narrow_low()
                narrow_out()
                turn_lane(0, ctx_nat, 4)
                begin(0, ctx_nat, False)
                per = {cl: 16, ti: 6, hr: 6 * GT, mr: 1, hc: 6, cc: 2, qr: 2 * SLOTS_A, vr: 2 * V_A,
                       pr: 4 * SLOTS_A, pd: 2 * SLOTS_A, pa: 2 * SLOTS_A, oy: 2 * SLOTS_A, gd: NF,
                       t0: TILES // 2, t1: TILES // 2, xr: 1}
                with repeat(pe, G - 1, mine, per) as g:
                    body(g, True)
                body(G - 1, False)

            @block.vector
            def _(dve):
                mine = []
                (own, rs, x1, x2, rl, zo, sc, er, rr, pt, ohi, yd, ge, gh, lg, rx, hz, lt, hh, xb, zs,
                 xt_, qh) = (Tally(mine) for _ in range(23))

                def stats_of(tiles, src):
                    layer_norm_stats(dve, tiles, src, own, ln_own, varB_ready)

                def apply_to(tiles, src, dst):
                    layer_norm_apply(dve, tiles, src, dst, rs, rstdB_ready, hatB_ready)
                    hz.next(len(tiles))

                def of(buffer):
                    return lambda t: buffer[:, t, :]

                def add_lane(l, dst, src, done, tally):
                    dve.wait_ge(done, tally.next())
                    part = dst[:, l * BT:(l + 1) * BT, :].rearrange("p t d -> p (t d)")
                    dve.tensor_tensor(part, part, src[:, :], ALU.add).then_inc(z_own, 1)

                def added():
                    dve.wait_ge(z_own, zo.next())
                    dve.memset(mdiff2[:, :], 0.0)

                def lane_tiles(l):
                    return range(l * BT, (l + 1) * BT)

                def modulate(g, norm, l, b, between=None):
                    dve.wait_ge(lane_turned, lt.next())
                    for k in range(DK):
                        part = bank[b][:, k * S:(k + 1) * S]
                        last = dve.tensor_scalar(part, part, emb[:, norm, k, bass.ds(GB * g + l, 1)],
                                                 emb[:, norm, DK + k, bass.ds(GB * g + l, 1)], ALU.mult, ALU.add)
                    last.then_inc(modulated, 1)
                    if between is not None:
                        between()
                    dve.wait_ge(h_hi_ready, hh.next())
                    cols = slice(l * S, (l + 1) * S)
                    dve.tensor_tensor(h_p[1][:, :, cols], bank[b][:, :].rearrange("p (k n) -> p k n", k=DK),
                                      as_f32(h_p[0][:, :, cols]), ALU.subtract).then_inc(h_ready, 1)

                def negmax(u):
                    dve.wait_ge(scores_done, sc.next())
                    dve.tensor_reduce(nmx[:, u, :], bank[u][:, :].rearrange("p (t k) -> p t k", t=BT), AX.X, ALU.max,
                                      negate=True).then_inc(negmax_ready, 1)

                def normalise(u):
                    dve.wait_ge(exp_ready, er.next())
                    dve.reciprocal(rrec[:, u, :], rsum[:, u, :]).then_inc(rrec_ready, 1)
                    dve.wait_ge(rrec_ready, rr.next())
                    for t in range(BT):
                        last = dve.tensor_scalar(probs[u][:, t, :], probs[u][:, t, :], rrec[:, u, t:t + 1], None, ALU.mult)
                    last.then_inc(probs_ready, 1)

                def save_pT():
                    dve.wait_ge(pT_done, pt.next())
                    pt.next()
                    dve.tensor_copy(pT[0][:, :, :], bank[2][:, :].rearrange("p (k q) -> p k q", k=BT)).then_inc(pT_dve, 1)

                def o_lo():
                    dve.wait_ge(o_hi_ready, ohi.next())
                    dve.tensor_tensor(o_p[1], bank[5][:, S:2 * S], as_f32(o_p[0]), ALU.subtract).then_inc(o_ready, 1)

                def qk_lo(s):
                    dve.wait_ge(qk_hi, qh.next())
                    hi, lo = qk_p[s % 2]
                    dve.scalar_tensor_tensor(lo[:, 0:S], bank[4][:, 0:S], SCALE, as_f32(hi[:, 0:S]), ALU.mult, ALU.subtract)
                    dve.tensor_tensor(lo[:, S:2 * S], bank[4][:, S:2 * S], as_f32(hi[:, S:2 * S]),
                                      ALU.subtract).then_inc(qk_ready, 1)

                def slot(s):
                    save_pT()
                    negmax(0)
                    negmax(1)
                    normalise(0)
                    o_lo()
                    normalise(1)
                    qk_lo(s)

                def slots(g, a):
                    with repeat(dve, HP // 2 - 1, mine, {sc: 8, er: 8, rr: 8, pt: 8, ohi: 4, qh: 4}) as i:
                        for s in range(4):
                            slot(s)
                    slot(0)
                    slot(1)
                    save_pT()
                    negmax(0)
                    if a == 0:
                        dve.wait_ge(z_started, zs.next())
                    add_lane(0, z, bank[6], y_done, yd)
                    negmax(1)
                    normalise(0)
                    o_lo()
                    added()
                    stats_of(lane_tiles(0), of(z))
                    normalise(1)
                    attention_normed(0)
                    save_pT()
                    modulate(g, a + 1, 0, 6, o_lo)

                def attention_added(l):
                    add_lane(l, z, bank[6 + l], y_done, yd)
                    added()
                    stats_of(lane_tiles(l), of(z))

                def attention_normed(l):
                    apply_to(lane_tiles(l), of(z), of(hat))

                def save_logits(g):
                    dve.wait_ge(logits_done, lg.next())
                    dve.tensor_copy(logits[:, bass.ds(GT * g, GT), :],
                                    bank[3][:, 0:GT * E].rearrange("p (t e) -> p t e", t=GT))

                def begin(middle=None, late=None):
                    negmax(0)
                    negmax(1)
                    normalise(0)
                    qk_lo(1)
                    if middle is not None:
                        middle()
                    if late is not None:
                        late()
                    normalise(1)

                def add_x1():
                    dve.wait_ge(xB_loaded, xb.next(16))
                    for l in two:
                        add_lane(l, xg, bank[4 + l], x1_done, x1)
                    zo.next()
                    added()
                    stats_of(ALL, of(xg))

                def add_x2():
                    for l in two:
                        add_lane(l, xg, bank[4 + l], x2_done, x2)
                    zo.next()
                    added()
                    stats_of(ALL, of(xg))

                def narrow(js):
                    for j in js:
                        dve.wait_ge(relu_ready, rl.next())
                        if j == 0:
                            last = dve.tensor_scalar(acc[0], relus[0], small_w[:, 1, 0:1], bin2[:, 1:2], ALU.mult, ALU.add)
                        elif j == 1:
                            last = dve.tensor_scalar(acc[1], relus[1], small_w[:, 1, 1:2], None, ALU.mult)
                        else:
                            dve.wait_ge(relu_used, rx.next())
                            last = dve.scalar_tensor_tensor(acc[j % 2], relus[j % 4], small_w[:, 1, j:j + 1], acc[j % 2],
                                                            ALU.mult, ALU.add)
                        last.then_inc(relu_used, 1)
                    if INNER - 1 in js:
                        rx.next(2)
                        dve.wait_ge(relu_used, rx.now())
                        dve.tensor_tensor(mlpT, acc[0], acc[1], ALU.add).then_inc(mlp_ready, 1)

                def first_stats():
                    dve.wait_ge(hatB_ready, hz.now())
                    dve.memset(mdiff2[:, :], 0.0)
                    for l in two:
                        stats_of(lane_tiles(l), of(hat))

                def first_norms():
                    for l in two:
                        apply_to(lane_tiles(l), of(hat), of(ctx_nat))

                def gated(f):
                    p = f % 2
                    dve.wait_ge(gelu_ready, ge.next())
                    dve.scalar_tensor_tensor(bank[2 * p][:, :], bank[2 * p][:, :], ffb1_sb[:, f:f + 1],
                                             gelu[p], ALU.add, ALU.mult).then_inc(gated_sum, 1)
                    dve.wait_ge(gated_hi, gh.next())
                    dve.tensor_tensor(gated_p[p][1], bank[2 * p][:, :], as_f32(gated_p[p][0]),
                                      ALU.subtract).then_inc(gated_ready, 1)

                def body(g, more):
                    slots(g, 0)
                    attention_added(1)
                    qk_lo(0)
                    attention_normed(1)
                    begin(middle=lambda: modulate(g, 1, 1, 3))
                    slots(g, 1)
                    attention_added(1)
                    attention_normed(1)
                    modulate(g, 2, 1, 7)
                    if more:
                        add_x1()
                    for f in range(NF):
                        gated(f)
                        if more:
                            if f == 0:
                                apply_to(ALL, of(xg), of(ctx_nat))
                            if f in RELU_STEPS:
                                narrow(RELU_STEPS[f])
                            if f == 5:
                                add_x2()
                                apply_to(ALL, of(xg), of(hat))
                    if more:
                        first_stats()
                        first_norms()
                    dve.wait_ge(x_taken, xt_.next())
                    add_lane(0, z, bank[6], y_done, yd)

                    def second_batch():
                        add_lane(1, z, bank[7], y_done, yd)
                        zo.next()
                        dve.wait_ge(z_own, zo.next())
                        dve.memset(mdiff2[:, :], 0.0).then_inc(x3_ready, 1)
                    if more:
                        modulate(g + 1, 0, 0, 4, second_batch)
                        stats_of(ALL, of(z))
                        qk_lo(0)
                        modulate(g + 1, 0, 1, 7)
                        apply_to(ALL, of(z), of(ctx_nat))
                        begin(late=lambda: save_logits(g))
                    else:
                        second_batch()
                        stats_of(ALL, of(z))
                        apply_to(ALL, of(z), of(ctx_nat))
                        save_logits(g)

                add_x1()
                apply_to(ALL, of(xg), of(ctx_nat))
                narrow(range(INNER))
                add_x2()
                apply_to(ALL, of(xg), of(hat))
                first_stats()
                first_norms()
                modulate(0, 0, 0, 4)
                qk_lo(0)
                modulate(0, 0, 1, 7)
                begin()
                per = {own: 6 * GT + 9 * 2, rs: 9, x1: 2, x2: 2, rl: INNER, zo: 10, sc: 4 * SLOTS_A,
                       er: 4 * SLOTS_A, rr: 4 * SLOTS_A, pt: 4 * SLOTS_A, ohi: 2 * SLOTS_A, yd: 6, ge: NF, gh: NF, lg: 1,
                       rx: INNER, hz: 6 * GT, lt: 6, hh: 6, xb: 16, zs: 1, xt_: 1,
                       qh: 2 * SLOTS_A}
                with repeat(dve, G - 1, mine, per) as g:
                    body(g, True)
                body(G - 1, False)

        r_own = sem("r_own")
        shifted_lg = sem("shifted_lg")
        exp_lg = sem("exp_lg")
        masks_ready = sem("masks_ready")
        counted = sem("counted")
        part_ready = sem("part_ready")
        iota_set = sem("iota_set")
        pre_done = sem("pre_done")
        slots_ready = sem("slots_ready")
        scattered = sem("scattered")
        first_raw = [sem(f"first_raw{i}") for i in range(4)]
        first_hi = sem("first_hi")
        first_lo = sem("first_lo")

        expert_cut = carve(parts, [2 * DK * NFE * P] * 2 + [NFE * D] * 2 + [DK * CAP] * 2 + [NFE * CAP] * 2)
        gu_p, down_p, xT_p, act_p = (expert_cut[2 * i:2 * i + 2] for i in range(4))
        PIECE = 1024
        first = [(w[0, k * P:(k + 1) * P, :], *(part[:, (n * DK + k) * PIECE:(n * DK + k + 1) * PIECE] for part in gu_p))
                 for n, w in enumerate((wg, wu)) for k in range(DK)]
        first += [(wd[0, j * 512:(j + 1) * 512, :].rearrange("(h p) n -> p h n", p=P),
                   *(part[:, j * PIECE:(j + 1) * PIECE] for part in down_p)) for j in range(2)]

        (prob, eqm, cand, oh1, oh2, wm, memb, ge, keep, tot, run_a, run_b, rank, iota_e, slot_e, tmp, tmp2, iota100,
         ex, above) = [c.rearrange("p (t e) -> p t e", t=NT) for c in carve(arena, [NT * E] * 20)]
        expert_i = sb("expert_i", [P, NT, E], mybir.dt.int32)
        token_i = sb("token_i", [P, NT], mybir.dt.int32)
        token_f = sb("token_f", [P, NT])
        top_p = sb("top_p", [P, 2, NT])
        top_w = sb("top_w", [P, 2, NT])
        by_token = sb("by_token", [P, 4, NT])
        thr, part, room = (sb(n, [P, E]) for n in ("thr", "part", "room"))
        thr_q, sel_q, trial_q, below_q, part_q, flag_q = (sb(n, [P, 1]) for n in
                                                          ("thr_q", "sel_q", "trial_q", "below_q", "part_q", "flag_q"))
        step_q = [sb(f"step_q{i}", [P, 1]) for i in range(2)]
        TURNED = NT * E // P
        assert P % E == 0 and NT * E % P == 0
        wm_turned, ge_turned, scratch = (c.rearrange("p t e -> p (t e)") for c in (cand, run_a, rank))
        same_expert, pick = scratch[:, 0:P], scratch[:, P:P + E]
        wm_ready = sem("wm_ready")
        wm_turned_ready = sem("wm_turned_ready")
        part_q_ready = sem("part_q_ready")
        counted_q = sem("counted_q")
        thr_found = sem("thr_found")
        thr_turned = sem("thr_turned")

        def over_e(v):
            return v.unsqueeze(2).to_broadcast([P, NT, E])

        def over_t(v):
            return v.unsqueeze(1).to_broadcast([P, NT, E])

        HALVINGS = 23
        DOUBLINGS = (64, 32, 16, 8, 4, 2, 1)
        TINY = 2.0 ** -126
        COUNTS = 1 + len(DOUBLINGS) + HALVINGS

        with nc.Block() as block:
            @block.gpsimd
            def _(pool):
                pool.iota(expert_i[:, :, :], [[0, NT], [1, E]], base=0, channel_multiplier=0).then_inc(iota_set, 1)
                pool.iota(token_i[:, :], [[P, NT]], base=0, channel_multiplier=1).then_inc(iota_set, 1)
                for j, (_, hi, lo) in enumerate(first):
                    pool.wait_ge(first_hi, j + 1)
                    pool.tensor_tensor(lo, raw[j % 4], as_f32(hi), ALU.subtract).then_inc(first_lo, 1)
                pool.wait_ge(slots_ready, 4)
                for t in range(NT):
                    for slot in (slot1, slot2):
                        pool.indirect_dma_start(disp[:, :], bass.IndirectOffsetOnAxis(ap=slot[:, t:t + 1], axis=0),
                                                attn[:, t * D:(t + 1) * D], None).then_inc(scattered, 16)
                pool.wait_ge(scattered, 16 * 2 * NT)

            @block.sync
            def _(sp):
                for j, (src, _, _) in enumerate(first):
                    if j >= 4:
                        sp.wait_ge(first_lo, j - 3)
                    dst = raw[j % 4] if len(src.shape) == 2 else raw[j % 4].rearrange("p (h n) -> p h n", h=4)
                    sp.dma_start(dst, src).then_inc(first_raw[j % 4], 16)

            @block.scalar
            def _(act):
                act.wait_ge(shifted_lg, 1)
                act.activation(ex, tmp, ACT.Exp).then_inc(exp_lg, 1)
                for j, (_, hi, _) in enumerate(first):
                    act.wait_ge(first_raw[j % 4], 16 * (j // 4 + 1))
                    act.activation(hi, raw[j % 4], ACT.Copy).then_inc(first_hi, 1)

            @block.tensor
            def _(pe):
                pe.wait_ge(wm_ready, 1)
                for j in range(TURNED):
                    last = pe.transpose(bank[4][:, j * P:(j + 1) * P],
                                        wm.rearrange("p t e -> p (t e)")[:, j * P:(j + 1) * P], ident[:, :])
                last.then_inc(wm_turned_ready, 1)
                for n in range(COUNTS):
                    pe.wait_ge(part_q_ready, n + 1)
                    pe.matmul(bank[n % 2][:, 0:1], same_expert, part_q[:, :], start=True, stop=True).then_inc(counted_q, 1)
                pe.wait_ge(thr_found, 1)
                pe.transpose(bank[5][:, 0:P], thr_q[:, 0:1].to_broadcast([P, P]), ident[:, :]).then_inc(thr_turned, 1)
                pe.wait_ge(part_ready, 1)
                pe.matmul(bank[6][:, 0:E], ones[:, :], part[:, :], start=True, stop=True).then_inc(counted, 1)
                for n, mask in enumerate((eqm, keep)):
                    pe.wait_ge(masks_ready, n + 1)
                    src = mask.rearrange("p t e -> p (t e)")
                    pe.matmul(bank[2][:, 0:NT * E], upper[:, :], src, start=True, stop=True)
                    pe.matmul(bank[3][:, 0:NT * E], ones[:, :], src, start=True, stop=True).then_inc(pre_done, 1)

            @block.vector
            def _(dve):
                steps = [0]

                def link(ins):
                    ins.then_inc(r_own, 1)
                    steps[0] += 1
                    dve.wait_ge(r_own, steps[0])

                dve.wait_ge(iota_set, 2)
                dve.tensor_copy(iota_e, expert_i[:, :, :])
                link(dve.tensor_copy(token_f[:, :], token_i[:, :]))
                dve.tensor_scalar(iota100, iota_e, 100.0, None, ALU.add)
                lmax, lsum, lrec, first = (by_token[:, i, :] for i in range(4))
                link(dve.tensor_reduce(lmax, logits[:, :, :], AX.X, ALU.max))
                dve.tensor_tensor(tmp, logits[:, :, :], over_e(lmax), ALU.subtract).then_inc(shifted_lg, 1)
                dve.wait_ge(exp_lg, 1)
                link(dve.tensor_reduce(lsum, ex, AX.X, ALU.add))
                link(dve.reciprocal(lrec, lsum))
                link(dve.tensor_tensor(prob, ex, over_e(lrec), ALU.mult))
                for c, (p, onehot) in enumerate(((prob, oh1), (tmp2, oh2))):
                    if c:
                        link(dve.scalar_tensor_tensor(tmp2, oh1, -2.0, prob, ALU.mult, ALU.add))
                    link(dve.tensor_reduce(top_p[:, c, :], p, AX.X, ALU.max))
                    link(dve.tensor_tensor(eqm, p, over_e(top_p[:, c, :]), ALU.is_equal))
                    link(dve.scalar_tensor_tensor(cand, eqm, -100.0, iota100, ALU.mult, ALU.add))
                    link(dve.tensor_reduce(first, cand, AX.X, ALU.min))
                    link(dve.tensor_tensor(onehot, iota_e, over_e(first), ALU.is_equal))
                link(dve.tensor_tensor(lsum, top_p[:, 0, :], top_p[:, 1, :], ALU.add))
                link(dve.tensor_scalar(lsum, lsum, 1e-6, None, ALU.add))
                link(dve.reciprocal(lrec, lsum))
                for c in range(2):
                    link(dve.tensor_tensor(top_w[:, c, :], top_p[:, c, :], lrec, ALU.mult))
                dve.tensor_tensor(memb, oh1, oh2, ALU.add)
                dve.tensor_tensor(tmp, oh1, over_e(top_w[:, 0, :]), ALU.mult)
                link(dve.tensor_tensor(tmp2, oh2, over_e(top_w[:, 1, :]), ALU.mult))
                link(dve.tensor_tensor(tmp, tmp, tmp2, ALU.add))
                link(dve.scalar_tensor_tensor(tmp, tmp, TINY, tmp, ALU.is_ge, ALU.mult))
                dve.scalar_tensor_tensor(wm, memb, -1.0, tmp, ALU.add, ALU.add).then_inc(wm_ready, 1)
                link(dve.tensor_reduce(pick, ident[:, :].rearrange("p (a b) -> p b a", b=E), AX.X, ALU.add))
                dve.tensor_copy(same_expert.rearrange("p (a b) -> p a b", b=E), pick.unsqueeze(1).to_broadcast([P, P // E, E]))
                dve.wait_ge(wm_turned_ready, 1)
                link(dve.tensor_copy(wm_turned, bank[4][:, 0:NT * E]))

                counts = [0]

                def enough(dst, by=1.0, meanwhile=None):
                    dve.tensor_scalar(ge_turned, wm_turned, trial_q[:, 0:1], 0.0, ALU.is_ge, ALU.add,
                                      accum_out=part_q[:, :]).then_inc(part_q_ready, 1)
                    counts[0] += 1
                    if meanwhile is not None:
                        meanwhile()
                    dve.wait_ge(counted_q, counts[0])
                    link(dve.tensor_scalar(dst[:, :], bank[(counts[0] - 1) % 2][:, 0:1], float(CAP), by, ALU.is_ge, ALU.mult))

                dve.memset(thr_q[:, :], TINY)
                link(dve.memset(trial_q[:, :], TINY))
                enough(flag_q)
                for k in DOUBLINGS:
                    link(dve.tensor_scalar(trial_q[:, :], thr_q[:, :], 2.0 ** k, None, ALU.mult))
                    enough(sel_q, 2.0 ** k - 1.0)
                    link(dve.tensor_scalar(sel_q[:, :], sel_q[:, :], 1.0, None, ALU.add))
                    link(dve.tensor_tensor(thr_q[:, :], thr_q[:, :], sel_q[:, :], ALU.mult))
                link(dve.tensor_scalar(step_q[0][:, :], thr_q[:, :], 0.5, None, ALU.mult))
                link(dve.tensor_tensor(trial_q[:, :], thr_q[:, :], step_q[0][:, :], ALU.add))
                for k in range(HALVINGS):
                    now, then = step_q[k % 2], step_q[1 - k % 2]

                    def next_step():
                        link(dve.tensor_scalar(then[:, :], now[:, :], 0.5, None, ALU.mult))
                        dve.tensor_tensor(below_q[:, :], thr_q[:, :], then[:, :], ALU.add)
                    enough(sel_q, now[:, 0:1], next_step)
                    dve.tensor_tensor(trial_q[:, :], below_q[:, :], sel_q[:, :], ALU.add)
                    link(dve.tensor_tensor(thr_q[:, :], thr_q[:, :], sel_q[:, :], ALU.add))
                dve.tensor_tensor(thr_q[:, :], thr_q[:, :], flag_q[:, :], ALU.mult).then_inc(thr_found, 1)
                dve.wait_ge(thr_turned, 1)
                link(dve.tensor_copy(thr[:, :], bank[5][:, 0:E]))
                link(dve.tensor_tensor(ge, wm, over_t(thr[:, :]), ALU.is_gt))
                dve.tensor_reduce(part[:, :], ge.rearrange("p t e -> p e t"), AX.X, ALU.add).then_inc(part_ready, 1)
                dve.wait_ge(counted, 1)
                dve.tensor_scalar(room[:, :], bank[6][:, 0:E], -1.0, float(CAP), ALU.mult, ALU.add)

                def before(n):
                    flat = lambda b: bank[b][:, 0:NT * E].rearrange("p (t e) -> p t e", t=NT)
                    dve.wait_ge(pre_done, n + 1)
                    dve.tensor_copy(tot, flat(3))
                    link(dve.tensor_copy(run_a, flat(3)))
                    a, b = run_a, run_b
                    shift = 1
                    while shift < NT:
                        dve.tensor_copy(b[:, 0:shift, :], a[:, 0:shift, :])
                        link(dve.tensor_tensor(b[:, shift:NT, :], a[:, shift:NT, :], a[:, 0:NT - shift, :], ALU.add))
                        a, b = b, a
                        shift *= 2
                    link(dve.tensor_tensor(a, a, tot, ALU.subtract))
                    link(dve.tensor_tensor(rank, a, flat(2), ALU.add))

                dve.tensor_tensor(eqm, wm, over_t(thr[:, :]), ALU.is_equal).then_inc(masks_ready, 1)
                before(0)
                link(dve.tensor_tensor(tmp, rank, over_t(room[:, :]), ALU.is_lt))
                link(dve.tensor_tensor(tmp, tmp, eqm, ALU.mult))
                dve.tensor_tensor(keep, ge, tmp, ALU.add).then_inc(masks_ready, 1)
                before(1)
                link(dve.scalar_tensor_tensor(slot_e, iota_e, float(CAP), rank, ALU.mult, ALU.add))
                link(dve.tensor_tensor(slot_e, slot_e, keep, ALU.mult))
                for c, (onehot, slot, gath) in enumerate(((oh1, slot1, gath1), (oh2, slot2, gath2))):
                    place, kept, lost, _ = (by_token[:, i, :] for i in range(4))
                    dve.tensor_tensor(tmp, onehot, slot_e, ALU.mult)
                    link(dve.tensor_tensor(tmp2, onehot, keep, ALU.mult))
                    dve.tensor_reduce(place, tmp, AX.X, ALU.add)
                    link(dve.tensor_reduce(kept, tmp2, AX.X, ALU.add))
                    dve.tensor_tensor(wk12[:, c, :], top_w[:, c, :], kept, ALU.mult)
                    dve.tensor_scalar(lost, kept, -1.0, 1.0, ALU.mult, ALU.add)
                    link(dve.tensor_scalar(tmp[:, :, 0], token_f[:, :], float(TRASH + c * B * S), None, ALU.add))
                    link(dve.tensor_tensor(lost, lost, tmp[:, :, 0], ALU.mult))
                    link(dve.tensor_tensor(lost, lost, place, ALU.add))
                    dve.tensor_copy(slot[:, :], lost).then_inc(slots_ready, 1)
                    dve.tensor_copy(gath[:, :], place).then_inc(slots_ready, 1)
                    dve.wait_ge(slots_ready, 2 * c + 2)


        x_in_e = sem("x_in_e")
        gu_loaded = sem("gu_loaded")
        down_loaded = sem("down_loaded")
        gu_hi = sem("gu_hi")
        gu_cut = sem("gu_cut")
        down_hi = sem("down_hi")
        down_cut = sem("down_cut")
        turned_e = sem("turned_e")
        xT_hi = sem("xT_hi")
        xT_cut = sem("xT_cut")
        up_done = sem("up_done")
        silu_ready = sem("silu_ready")
        act_product = sem("act_product")
        act_hi = sem("act_hi")
        act_cut = sem("act_cut")
        down_done = sem("down_done")
        eo_saved = sem("eo_saved")
        eo_stored = sem("eo_stored")

        raw_gu, raw_down, x_e = carve(attn, [4 * PIECE, 2 * PIECE, ET * D])
        x_e = x_e.rearrange("p (t d) -> p t d", t=ET)
        RING_U = 3
        silu = [flat(z)[:, r * EH:(r + 1) * EH] for r in range(RING_U)]
        eo_tile = [hat[:, t, :] if t < GT else ctx_nat[:, t - GT, :] for t in range(ET)]
        GATE, UP = (0, 1, 4), (2, 3, 5)
        DOWN = (7, 0, 1, 2, 3)
        TURN = ((4, 0, 512), (5, 512, 512), (6, 1024, DK * CAP - 1024))
        assert ET == len(DOWN) and DK * CAP > 1024
        UPS = 2 * NFE

        def piece(t, j):
            return t[:, j * PIECE:(j + 1) * PIECE]

        with nc.Block() as block:
            @block.sync
            def _(sp):
                mine = []
                tu, gc, dc, sv = (Tally(mine) for _ in range(4))
                sources = (wg.rearrange("e (k p) n -> p (e k) n", p=P), wu.rearrange("e (k p) n -> p (e k) n", p=P),
                           wd.rearrange("e (f p) n -> p (e f) n", p=P))

                def load_x(e):
                    sp.dma_start(x_e, disp[bass.ds(e * CAP, CAP), :].rearrange("(t p) d -> p t d", p=P)).then_inc(x_in_e, 16)

                def load_gu(e):
                    for n in range(2):
                        sp.dma_start(raw_gu[:, n * 2 * PIECE:(n + 1) * 2 * PIECE].rearrange("p (k n) -> p k n", k=DK),
                                     sources[n][:, bass.ds(e * DK, DK), :]).then_inc(gu_loaded, 16)

                def load_down(e):
                    sp.dma_start(raw_down.rearrange("p (f n) -> p f n", f=NFE),
                                 sources[2][:, bass.ds(e * NFE, NFE), :]).then_inc(down_loaded, 16)

                def store(e):
                    sp.wait_ge(eo_saved, sv.next(ET))
                    sp.dma_start(eo[bass.ds(e * CAP, GT * P), :].rearrange("(t p) d -> p t d", p=P),
                                 hat[:, :, :]).then_inc(eo_stored, 16)
                    sp.dma_start(eo[bass.ds(e * CAP + GT * P, P), :], ctx_nat[:, 0, :]).then_inc(eo_stored, 16)

                sv.next(ET)
                load_x(0)
                load_gu(1)
                sp.wait_ge(turned_e, tu.next())
                load_x(1)
                load_down(1)
                with repeat(sp, E - 2, mine, {tu: 1, gc: 4, dc: 1, sv: ET}) as i:
                    sp.wait_ge(gu_cut, gc.next(4))
                    load_gu(i + 2)
                    sp.wait_ge(turned_e, tu.next())
                    load_x(i + 2)
                    store(i)
                    sp.wait_ge(down_cut, dc.next())
                    load_down(i + 2)
                store(E - 2)
                store(E - 1)
                sp.wait_ge(eo_stored, 32 * (E + 1))

            @block.gpsimd
            def _(pool):
                mine = []
                gh, dl, dd, dh = (Tally(mine) for _ in range(4))
                pool.sem_inc(eo_saved, ET)
                pool.sem_inc(eo_stored, 32)
                with repeat(pool, E - 1, mine, {gh: 4, dl: 16, dd: ET, dh: 1}) as e:
                    for j in (1, 3):
                        pool.wait_ge(gu_hi, gh.next(2))
                        pool.tensor_tensor(piece(gu_p[1], j), piece(raw_gu, j), as_f32(piece(gu_p[0], j)),
                                           ALU.subtract).then_inc(gu_cut, 1)
                    pool.wait_ge(down_loaded, dl.next(16))
                    pool.wait_ge(down_done, dd.next(ET))
                    pool.tensor_tensor(down_p[0], raw_down, ones[:, 0:1].to_broadcast([P, NFE * D]), ALU.mult).then_inc(down_hi, 1)
                    pool.wait_ge(down_hi, dh.next())
                    pool.tensor_tensor(down_p[1], raw_down, as_f32(down_p[0]), ALU.subtract).then_inc(down_cut, 1)

            @block.scalar
            def _(act):
                mine = []
                tu, up, ap_, gl, dn, st = (Tally(mine) for _ in range(6))

                def hi_xT():
                    act.wait_ge(turned_e, tu.next())
                    for b, o, n in TURN:
                        act.activation(xT_p[0][:, o:o + n], bank[b][:, 0:n], ACT.Copy).then_inc(xT_hi, 1)

                def expert(more):
                    for u in range(UPS):
                        f, h, r = u // 2, u % 2, u % RING_U
                        act.wait_ge(up_done, up.next())
                        act.activation(silu[r], bank[GATE[r]][:, 0:EH], ACT.Silu).then_inc(silu_ready, 1)
                        act.wait_ge(act_product, ap_.next())
                        o = f * CAP + h * EH
                        act.activation(act_p[0][:, o:o + EH], bank[UP[r]][:, 0:EH], ACT.Copy).then_inc(act_hi, 1)
                    if more:
                        act.wait_ge(gu_loaded, gl.next(32))
                        for j in range(4):
                            act.activation(piece(gu_p[0], j), piece(raw_gu, j), ACT.Copy).then_inc(gu_hi, 1)
                        hi_xT()
                    act.wait_ge(eo_stored, st.next(32))
                    for t in (1, 3):
                        act.wait_ge(down_done, dn.next(2))
                        act.activation(eo_tile[t], bank[DOWN[t]][:, 0:D], ACT.Copy).then_inc(eo_saved, 1)
                    dn.next()
                hi_xT()
                with repeat(act, E - 1, mine, {tu: 1, up: UPS, ap_: UPS, gl: 32, dn: ET, st: 32}) as e:
                    expert(True)
                expert(False)

            @block.tensor
            def _(pe):
                mine = []
                xl, xc, gc, dc, ac, sv = (Tally(mine) for _ in range(6))

                def turn():
                    pe.wait_ge(x_in_e, xl.next(16))
                    for c in range(DK * ET):
                        k, t = c // ET, c % ET
                        last = pe.transpose(bank[4 + c // 4][:, (c % 4) * P:(c % 4 + 1) * P], x_e[:, t, k * P:(k + 1) * P],
                                            ident[:, :])
                    last.then_inc(turned_e, 1)

                def expert(cut_here, more):
                    if cut_here:
                        pe.wait_ge(gu_cut, gc.next(4))
                    pe.wait_ge(xT_cut, xc.next(3))
                    pe.wait_ge(eo_saved, sv.next(ET))
                    for u in range(UPS):
                        f, h, r = u // 2, u % 2, u % RING_U
                        if u >= RING_U:
                            pe.wait_ge(act_cut, ac.next())
                        for n, b in ((0, GATE[r]), (1, UP[r])):
                            for k in range(DK):
                                for m, (i, j) in enumerate(PASSES):
                                    o = (n * DK + k) * PIECE + f * P
                                    last = pe.matmul(bank[b][:, 0:EH], gu_p[i][:, o:o + P],
                                                     xT_p[j][:, k * CAP + h * EH:k * CAP + (h + 1) * EH],
                                                     start=(k == 0 and m == 0), stop=(k == DK - 1 and m == 2))
                        last.then_inc(up_done, 1)
                    for t in range(ET):
                        if t == 0:
                            pe.wait_ge(act_cut, ac.next())
                            if cut_here:
                                pe.wait_ge(down_cut, dc.next())
                        for f in range(NFE):
                            if t == 0 and f == NFE - 1:
                                pe.wait_ge(act_cut, ac.next(2))
                            for m, (i, j) in enumerate(PASSES):
                                o = f * CAP + t * P
                                last = pe.matmul(bank[DOWN[t]][:, 0:D], act_p[i][:, o:o + P],
                                                 down_p[j][:, f * D:(f + 1) * D],
                                                 start=(f == 0 and m == 0), stop=(f == NFE - 1 and m == 2))
                        last.then_inc(down_done, 1)
                        if more and t == 0:
                            turn()

                turn()
                expert(False, True)
                with repeat(pe, E - 2, mine, {xl: 16, xc: 3, gc: 4, dc: 1, ac: UPS, sv: ET}) as e:
                    expert(True, True)
                expert(True, False)

            @block.vector
            def _(dve):
                mine = []
                xh, sl, ah, gh, dn, st = (Tally(mine) for _ in range(6))

                def lo_xT():
                    for b, o, n in TURN:
                        dve.wait_ge(xT_hi, xh.next())
                        dve.tensor_tensor(xT_p[1][:, o:o + n], bank[b][:, 0:n], as_f32(xT_p[0][:, o:o + n]),
                                          ALU.subtract).then_inc(xT_cut, 1)

                def expert(more):
                    for u in range(UPS):
                        f, h, r = u // 2, u % 2, u % RING_U
                        dve.wait_ge(silu_ready, sl.next())
                        up = bank[UP[r]][:, 0:EH]
                        dve.tensor_tensor(up, up, silu[r], ALU.mult).then_inc(act_product, 1)
                        dve.wait_ge(act_hi, ah.next())
                        o = f * CAP + h * EH
                        dve.tensor_tensor(act_p[1][:, o:o + EH], up, as_f32(act_p[0][:, o:o + EH]),
                                          ALU.subtract).then_inc(act_cut, 1)
                    if more:
                        for j in (0, 2):
                            dve.wait_ge(gu_hi, gh.next(1 if j == 0 else 2))
                            dve.tensor_tensor(piece(gu_p[1], j), piece(raw_gu, j), as_f32(piece(gu_p[0], j)),
                                              ALU.subtract).then_inc(gu_cut, 1)
                        gh.next()
                        lo_xT()
                    dve.wait_ge(eo_stored, st.next(32))
                    for t in (0, 2, 4):
                        dve.wait_ge(down_done, dn.next(2 if t else 1))
                        dve.tensor_copy(eo_tile[t], bank[DOWN[t]][:, 0:D]).then_inc(eo_saved, 1)
                lo_xT()
                with repeat(dve, E - 1, mine, {xh: 3, sl: UPS, ah: UPS, gh: 4, dn: ET, st: 32}) as e:
                    expert(True)
                expert(False)


        RING = 8
        gathered = [sem(f"gathered{i}") for i in range(RING)]
        x3_back = [sem(f"x3_back{i}") for i in range(G)]
        first_added = sem("first_added")
        added = sem("added")
        out_stored = sem("out_stored")
        picked = [[v[:, i * D:(i + 1) * D] for i in range(RING)] for v in carve(arena, [RING * D] * 2)]
        x3_t = attn[:, :].rearrange("p (t d) -> p t d", t=NT)

        with nc.Block() as block:
            @block.gpsimd
            def _(pool):
                for t in range(NT):
                    if t >= RING:
                        pool.wait_ge(added, t - RING + 1)
                    for c, gath in enumerate((gath1, gath2)):
                        pool.indirect_dma_start(picked[c][t % RING], None, eo[:, :],
                                                bass.IndirectOffsetOnAxis(ap=gath[:, t:t + 1], axis=0)
                                                ).then_inc(gathered[t % RING], 16)

            @block.scalar
            def _(act):
                for i in range(G):
                    act.dma_start(x3_t[:, i * GT:(i + 1) * GT, :], x3_tiles[:, i * GT:(i + 1) * GT, :]).then_inc(x3_back[i], 16)

            @block.vector
            def _(dve):
                for t in range(NT):
                    tile = x3_t[:, t, :]
                    if t % GT == 0:
                        dve.wait_ge(x3_back[t // GT], 16)
                    dve.wait_ge(gathered[t % RING], 32 * (t // RING + 1))
                    dve.scalar_tensor_tensor(tile, picked[0][t % RING], wk12[:, 0, t:t + 1], tile, ALU.mult,
                                             ALU.add).then_inc(first_added, 1)
                    dve.wait_ge(first_added, t + 1)
                    dve.scalar_tensor_tensor(tile, picked[1][t % RING], wk12[:, 1, t:t + 1], tile, ALU.mult,
                                             ALU.add).then_inc(added, 1)

            @block.sync
            def _(sp):
                for i in range(NT // GT):
                    sp.wait_ge(added, GT * (i + 1))
                    sp.dma_start(out_tiles[:, i * GT:(i + 1) * GT, :], x3_t[:, i * GT:(i + 1) * GT, :]).then_inc(out_stored, 16)
                sp.wait_ge(out_stored, 16 * (NT // GT))


_INS = ['x', 'cond_1024', 'ctx_1024', 'L0_xcond_W', 'L0_xcond_U', 'L0_ffn_Win', 'L0_ffn_bin_', 'L0_ffn_W1',
        'L0_ffn_b1', 'L0_ffn_W2', 'L0_ffn_b2', 'L0_ffn_Wout', 'L0_ffn_bout', 'L1_xcond_attn1_wq',
        'L1_xcond_attn1_wk', 'L1_xcond_attn1_wv', 'L1_xcond_attn1_wo', 'L1_xcond_attn1_bo', 'L1_xcond_attn2_wq',
        'L1_xcond_attn2_wk', 'L1_xcond_attn2_wv', 'L1_xcond_attn2_wo', 'L1_xcond_attn2_bo', 'L1_xcond_ff_w1',
        'L1_xcond_ff_b1', 'L1_xcond_ff_w2', 'L1_xcond_ff_b2', 'L1_xcond_norm1_w', 'L1_xcond_norm1_b',
        'L1_xcond_norm2_w', 'L1_xcond_norm2_b', 'L1_xcond_norm3_w', 'L1_xcond_norm3_b', 'L1_ffn_router_w',
        'L1_ffn_wg', 'L1_ffn_wu', 'L1_ffn_wd']


def kernel(**inputs):
    import numpy as _np
    import concourse.bacc as _bacc
    from concourse.bass_utils import run_bass_kernel_spmd as _run

    nc = _bacc.Bacc("TRN2", target_bir_lowering=False, num_devices=1)
    arrays, args = {}, []
    for name in _INS:
        a = _np.ascontiguousarray(inputs[name])
        arrays[f"in_{name}_dram"] = a
        args.append(nc.dram_tensor(f"in_{name}_dram", a.shape, mybir.dt.from_np(a.dtype), kind="ExternalInput").ap())
    args.append(nc.dram_tensor("out_dram", inputs["x"].shape, F32, kind="ExternalOutput").ap())
    build(nc, *args)
    r = _run(nc, [arrays], core_ids=[0])
    return r.results[0]["out_dram"]
```
